# Optimizing a Trainium2 kernel written in Bass

```python
import numpy as np
import jax
import jax.numpy as jnp

def _softmax(x, axis=-1):
    return jax.nn.softmax(x, axis=axis)

def _gelu(x):
    return jax.nn.gelu(x, approximate=True)

def _silu(x):
    return jax.nn.silu(x)

def _sigmoid(x):
    return jax.nn.sigmoid(x)

def _layernorm(x, axis=-1, eps=1e-05):
    m = jnp.mean(x, axis=axis, keepdims=True)
    v = jnp.var(x, axis=axis, keepdims=True)
    return (x - m) / jnp.sqrt(v + eps)

def _scatter_add(tgt, idx, src, axis=0):
    return tgt.at[idx].add(src)

def _segment_sum(src, seg, n):
    return jax.ops.segment_sum(src, seg, n)
kernel_name = 'mk_prb_d2_jaxref_r8_3f05f6'

def setup_inputs(seed: int=0):
    np.random.seed(seed)
    _w = jnp.asarray

    def _L0_attn_setup():
        import jax, jax.numpy as jnp
        import numpy as np
        DIM = 256
        NUM_HEADS = 128
        TOP_K = 32
        D_HEAD_V = DIM // NUM_HEADS
        key = jax.random.key(seed)
        ks = jax.random.split(key, 5)
        s = 1.0 / np.sqrt(DIM)
        x = jax.random.normal(ks[0], (4, 512, DIM), dtype=jnp.float32)
        Wq = jax.random.uniform(ks[1], (NUM_HEADS, DIM), minval=-s, maxval=s, dtype=jnp.float32)
        Wk = jax.random.uniform(ks[2], (NUM_HEADS, DIM), minval=-s, maxval=s, dtype=jnp.float32)
        Wv = jax.random.uniform(ks[3], (DIM, DIM), minval=-s, maxval=s, dtype=jnp.float32)
        Wo = jax.random.uniform(ks[4], (DIM, DIM), minval=-s, maxval=s, dtype=jnp.float32)
        return {'x': x, 'Wq': Wq, 'Wk': Wk, 'Wv': Wv, 'Wo': Wo}
    _L0_attn_in = _L0_attn_setup()

    def _L0_ffn_setup():
        import jax, jax.numpy as jnp
        import numpy as np
        B, T = (1, 64)
        DIM = 256
        MOE_INTER = 176
        N_EXPERTS = 64
        TOPK = 6
        N_SHARED = 2
        SHARED_INTER = N_SHARED * MOE_INTER
        CAPACITY = 128
        ROUTE_SCALE = 1.0
        key = jax.random.key(seed)
        ks = jax.random.split(key, 8)

        def w(k, shape, fan_in):
            return jax.random.normal(k, shape, jnp.float32) * fan_in ** (-0.5)
        return {'x': jax.random.normal(ks[0], (B, T, DIM), jnp.float32), 'gate_w': w(ks[1], (N_EXPERTS, DIM), DIM), 'w1': w(ks[2], (N_EXPERTS, MOE_INTER, DIM), DIM), 'w2': w(ks[3], (N_EXPERTS, DIM, MOE_INTER), MOE_INTER), 'w3': w(ks[4], (N_EXPERTS, MOE_INTER, DIM), DIM), 'sw1': w(ks[5], (SHARED_INTER, DIM), DIM), 'sw2': w(ks[6], (DIM, SHARED_INTER), SHARED_INTER), 'sw3': w(ks[7], (SHARED_INTER, DIM), DIM)}
    _L0_ffn_in = _L0_ffn_setup()

    def _L1_attn_setup():
        import jax, jax.numpy as jnp
        import numpy as np
        B, T, C = (4, 256, 256)
        H = 32
        N = C // H
        N_LAYER = 12
        LAYER_ID = 6
        EPS = 1e-05 * 144
        key = jax.random.key(seed)
        ks = jax.random.split(key, 8)
        r01 = LAYER_ID / N_LAYER
        r1a0 = 1.0 - LAYER_ID / N_LAYER
        ddd = jnp.arange(C, dtype=jnp.float32) / C
        time_maa_k = (ddd ** r1a0).reshape(1, 1, C)
        time_maa_v = time_maa_k + 0.3 * r01
        time_maa_r = (ddd ** (0.5 * r1a0)).reshape(1, 1, C)
        time_maa_g = time_maa_r
        h = jnp.arange(H, dtype=jnp.float32) / (H - 1)
        time_decay = (-6.0 + 5.0 * h ** (0.7 + 0.3 * r01)).reshape(H, 1)
        zigzag = (((jnp.arange(H) + 1) % 3).astype(jnp.float32) - 1.0) * 0.1
        time_faaaa = (r01 * (1.0 - h) + zigzag).reshape(H, 1)

        def W(k):
            return jax.random.normal(k, (C, C), dtype=jnp.float32) * 0.02
        return {'x': jax.random.normal(ks[0], (B, T, C), dtype=jnp.float32), 'time_maa_k': time_maa_k, 'time_maa_v': time_maa_v, 'time_maa_r': time_maa_r, 'time_maa_g': time_maa_g, 'time_decay': time_decay, 'time_faaaa': time_faaaa, 'Wr': W(ks[1]), 'Wk': W(ks[2]), 'Wv': W(ks[3]), 'Wg': W(ks[4]), 'Wo': W(ks[5]), 'gamma': jnp.ones((C,), jnp.float32), 'beta': jnp.zeros((C,), jnp.float32)}
    _L1_attn_in = _L1_attn_setup()

    def _L1_ffn_setup():
        import jax, jax.numpy as jnp
        import numpy as np
        B, S, D, H = (8, 512, 256, 640)

        def ternarize_weight(w):
            abs_mean = jnp.maximum(jnp.mean(jnp.abs(w)), 1e-05)
            thr = 0.7 * abs_mean
            one = jnp.ones((), dtype=w.dtype)
            q = jnp.where(w > thr, one, jnp.where(w < -thr, -one, jnp.zeros((), dtype=w.dtype)))
            return w + jax.lax.stop_gradient(q * abs_mean - w)
        key = jax.random.key(seed)
        k1, k2, k3 = jax.random.split(key, 3)
        x = jax.random.normal(k1, (B, S, D), dtype=jnp.float32)
        w_fc = jax.random.normal(k2, (H, D), dtype=jnp.float32) / np.sqrt(D).astype(np.float32)
        w_proj = jax.random.normal(k3, (D, H), dtype=jnp.float32) / np.sqrt(H).astype(np.float32)
        return {'x': x, 'w_fc': w_fc, 'w_proj': w_proj}
    _L1_ffn_in = _L1_ffn_setup()
    _d = {'L0_attn_x': _L0_attn_in['x'], 'L0_attn_Wq': _L0_attn_in['Wq'], 'L0_attn_Wk': _L0_attn_in['Wk'], 'L0_attn_Wv': _L0_attn_in['Wv'], 'L0_attn_Wo': _L0_attn_in['Wo'], 'L0_ffn_gate_w': _L0_ffn_in['gate_w'], 'L0_ffn_w1': _L0_ffn_in['w1'], 'L0_ffn_w2': _L0_ffn_in['w2'], 'L0_ffn_w3': _L0_ffn_in['w3'], 'L0_ffn_sw1': _L0_ffn_in['sw1'], 'L0_ffn_sw2': _L0_ffn_in['sw2'], 'L0_ffn_sw3': _L0_ffn_in['sw3'], 'L1_attn_time_maa_k': _L1_attn_in['time_maa_k'], 'L1_attn_time_maa_v': _L1_attn_in['time_maa_v'], 'L1_attn_time_maa_r': _L1_attn_in['time_maa_r'], 'L1_attn_time_maa_g': _L1_attn_in['time_maa_g'], 'L1_attn_time_decay': _L1_attn_in['time_decay'], 'L1_attn_time_faaaa': _L1_attn_in['time_faaaa'], 'L1_attn_Wr': _L1_attn_in['Wr'], 'L1_attn_Wk': _L1_attn_in['Wk'], 'L1_attn_Wv': _L1_attn_in['Wv'], 'L1_attn_Wg': _L1_attn_in['Wg'], 'L1_attn_Wo': _L1_attn_in['Wo'], 'L1_attn_gamma': _L1_attn_in['gamma'], 'L1_attn_beta': _L1_attn_in['beta'], 'L1_ffn_w_fc': _L1_ffn_in['w_fc'], 'L1_ffn_w_proj': _L1_ffn_in['w_proj']}
    _x0 = _d['L0_attn_x']
    _d['L0_attn_x'] = jax.random.normal(jax.random.fold_in(jax.random.key(seed), 1), (2, 512, 256), dtype=_x0.dtype)
    del _x0
    return _d

def reference(L0_attn_x, L0_attn_Wq, L0_attn_Wk, L0_attn_Wv, L0_attn_Wo, L0_ffn_gate_w, L0_ffn_w1, L0_ffn_w2, L0_ffn_w3, L0_ffn_sw1, L0_ffn_sw2, L0_ffn_sw3, L1_attn_time_maa_k, L1_attn_time_maa_v, L1_attn_time_maa_r, L1_attn_time_maa_g, L1_attn_time_decay, L1_attn_time_faaaa, L1_attn_Wr, L1_attn_Wk, L1_attn_Wv, L1_attn_Wg, L1_attn_Wo, L1_attn_gamma, L1_attn_beta, L1_ffn_w_fc, L1_ffn_w_proj):

    def _L0_attn_ref(x, Wq, Wk, Wv, Wo):
        import jax, jax.numpy as jnp
        import numpy as np
        DIM = 256
        NUM_HEADS = 128
        TOP_K = 32
        D_HEAD_V = DIM // NUM_HEADS
        B, S, _ = x.shape
        H, dv, k = (NUM_HEADS, D_HEAD_V, TOP_K)
        q = jnp.einsum('bsd,hd->bhs', x, Wq)
        keys = jnp.einsum('bsd,hd->bhs', x, Wk)
        v = jnp.einsum('bsd,ed->bse', x, Wv).reshape(B, S, H, dv).transpose(0, 2, 1, 3)
        k_idx = jnp.argsort(keys, axis=-1)
        k_sorted = jnp.take_along_axis(keys, k_idx, axis=-1)
        v_sorted = jnp.take_along_axis(v, k_idx[..., None], axis=2)
        top_keys = k_sorted[:, :, -k:]
        bot_keys = k_sorted[:, :, :k]
        top_vals = v_sorted[:, :, -k:, :]
        bot_vals = v_sorted[:, :, :k, :]
        attn_top = jax.nn.softmax(q[..., None] * top_keys[:, :, None, :], axis=-1)
        attn_bot = jax.nn.softmax(q[..., None] * bot_keys[:, :, None, :], axis=-1)
        out_top = jnp.einsum('bhsk,bhkd->bhsd', attn_top, top_vals)
        out_bot = jnp.einsum('bhsk,bhkd->bhsd', attn_bot, bot_vals)
        q_pos = (q > 0).astype(x.dtype)[..., None]
        out = q_pos * out_top + (1.0 - q_pos) * out_bot
        out = out.transpose(0, 2, 1, 3).reshape(B, S, H * dv)
        return jnp.einsum('bsd,ed->bse', out, Wo)

    def _L0_ffn_ref(x, gate_w, w1, w2, w3, sw1, sw2, sw3):
        import jax, jax.numpy as jnp
        import numpy as np
        B, T = (1, 64)
        DIM = 256
        MOE_INTER = 176
        N_EXPERTS = 64
        TOPK = 6
        N_SHARED = 2
        SHARED_INTER = N_SHARED * MOE_INTER
        CAPACITY = 128
        ROUTE_SCALE = 1.0
        Bb, Tt, D = x.shape
        xf = x.reshape(-1, D)
        N = xf.shape[0]
        logits = xf @ gate_w.T
        scores = jax.nn.softmax(logits, axis=-1)
        gate_vals, idx = jax.lax.top_k(scores, TOPK)
        gate_vals = gate_vals * ROUTE_SCALE
        E = gate_w.shape[0]
        fe = idx.reshape(-1)
        ft = jnp.repeat(jnp.arange(N), TOPK)
        onehot = (fe[:, None] == jnp.arange(E)[None, :]).astype(jnp.int32)
        pos = jnp.take_along_axis(jnp.cumsum(onehot, axis=0) - 1, fe[:, None], axis=1)[:, 0]
        keep = pos < CAPACITY
        buf = jnp.full((E, CAPACITY), N, dtype=jnp.int32)
        buf = buf.at[fe, pos].set(ft.astype(jnp.int32), mode='drop')
        xpad = jnp.concatenate([xf, jnp.zeros((1, D), xf.dtype)], axis=0)
        xe = xpad[buf]
        h = jax.nn.silu(jnp.einsum('ecd,eid->eci', xe, w1)) * jnp.einsum('ecd,eid->eci', xe, w3)
        ye = jnp.einsum('eci,edi->ecd', h, w2)
        pc = jnp.minimum(pos, CAPACITY - 1)
        op = ye[fe, pc] * keep[:, None].astype(ye.dtype)
        routed = (op * gate_vals.reshape(-1)[:, None]).reshape(N, TOPK, D).sum(axis=1)
        z = jax.nn.silu(xf @ sw1.T) * (xf @ sw3.T) @ sw2.T
        return (routed + z).reshape(Bb, Tt, D)

    def _L1_attn_ref(x, time_maa_k, time_maa_v, time_maa_r, time_maa_g, time_decay, time_faaaa, Wr, Wk, Wv, Wg, Wo, gamma, beta):
        import jax, jax.numpy as jnp
        import numpy as np
        B, T, C = (4, 256, 256)
        H = 32
        N = C // H
        N_LAYER = 12
        LAYER_ID = 6
        EPS = 1e-05 * 144
        B, T, C = x.shape
        Hh = time_decay.shape[0]
        Nn = C // Hh
        Q = 32 if T % 32 == 0 else 128 if T % 128 == 0 else T
        nC = T // Q
        xx = jnp.pad(x, ((0, 0), (1, 0), (0, 0)))[:, :T] - x
        xk = x + xx * time_maa_k
        xv = x + xx * time_maa_v
        xr = x + xx * time_maa_r
        xg = x + xx * time_maa_g
        r = (xr @ Wr.T).reshape(B, T, Hh, Nn).transpose(0, 2, 1, 3)
        k = (xk @ Wk.T).reshape(B, T, Hh, Nn).transpose(0, 2, 3, 1)
        v = (xv @ Wv.T).reshape(B, T, Hh, Nn).transpose(0, 2, 1, 3)
        g = jax.nn.silu(xg @ Wg.T)
        w = jnp.exp(-jnp.exp(time_decay))
        u = time_faaaa
        ws = (w ** Q).reshape(1, Hh, 1, 1)
        qa = jnp.arange(Q)
        wk = (w ** (Q - 1 - qa)[None, :]).reshape(1, Hh, 1, Q)
        wb = (w ** qa[None, :]).reshape(1, Hh, Q, 1)
        i = qa[:, None]
        j = qa[None, :]
        pw = w.reshape(Hh, 1, 1) ** jnp.maximum(i - j - 1, 0)[None]
        w_mat = jnp.where(i > j, pw, jnp.where(i == j, u.reshape(Hh, 1, 1), jnp.zeros((), x.dtype))).reshape(1, Hh, Q, Q)
        rr = r.reshape(B, Hh, nC, Q, Nn).transpose(2, 0, 1, 3, 4)
        kk = k.reshape(B, Hh, Nn, nC, Q).transpose(3, 0, 1, 2, 4)
        vv = v.reshape(B, Hh, nC, Q, Nn).transpose(2, 0, 1, 3, 4)

        def step(state, inp):
            rc, kc, vc = inp
            att = rc @ kc * w_mat
            yc = att @ vc + rc @ state * wb
            new_state = ws * state + kc * wk @ vc
            return (new_state, yc)
        state0 = jnp.zeros((B, Hh, Nn, Nn), x.dtype)
        _, ys = jax.lax.scan(step, state0, (rr, kk, vv))
        y = ys.transpose(1, 0, 3, 2, 4).reshape(B, T, Hh, Nn)
        mu = jnp.mean(y, axis=-1, keepdims=True)
        var = jnp.mean(jnp.square(y - mu), axis=-1, keepdims=True)
        yn = ((y - mu) / jnp.sqrt(var + EPS)).reshape(B, T, C) * gamma + beta
        out = yn * g @ Wo.T
        return out

    def _L1_ffn_ref(x, w_fc, w_proj):
        import jax, jax.numpy as jnp
        import numpy as np
        B, S, D, H = (8, 512, 256, 640)

        def ternarize_weight(w):
            abs_mean = jnp.maximum(jnp.mean(jnp.abs(w)), 1e-05)
            thr = 0.7 * abs_mean
            one = jnp.ones((), dtype=w.dtype)
            q = jnp.where(w > thr, one, jnp.where(w < -thr, -one, jnp.zeros((), dtype=w.dtype)))
            return w + jax.lax.stop_gradient(q * abs_mean - w)
        h = jnp.einsum('bsd,hd->bsh', x, ternarize_weight(w_fc))
        h = jnp.square(jax.nn.relu(h))
        return jnp.einsum('bsh,dh->bsd', h, ternarize_weight(w_proj))
    x = L0_attn_x
    xn = _layernorm(x, axis=-1)
    x = x + _L0_attn_ref(xn, L0_attn_Wq, L0_attn_Wk, L0_attn_Wv, L0_attn_Wo) + _L0_ffn_ref(xn, L0_ffn_gate_w, L0_ffn_w1, L0_ffn_w2, L0_ffn_w3, L0_ffn_sw1, L0_ffn_sw2, L0_ffn_sw3)
    xn = _layernorm(x, axis=-1)
    x = x + _L1_attn_ref(xn, L1_attn_time_maa_k, L1_attn_time_maa_v, L1_attn_time_maa_r, L1_attn_time_maa_g, L1_attn_time_decay, L1_attn_time_faaaa, L1_attn_Wr, L1_attn_Wk, L1_attn_Wv, L1_attn_Wg, L1_attn_Wo, L1_attn_gamma, L1_attn_beta) + _L1_ffn_ref(xn, L1_ffn_w_fc, L1_ffn_w_proj)
    return x

_drawn_inputs = setup_inputs


def setup_inputs(seed=0):
    import zlib

    import numpy as np

    out = dict(_drawn_inputs(seed))
    spreads = {'L1_attn_gamma': (1.0, 0.6), 'L1_attn_beta': (0.0, 0.8)}
    factors = {'L1_attn_time_maa_k': 4.642,
     'L1_attn_time_maa_v': 5.671,
     'L1_attn_time_maa_r': 5.733,
     'L1_attn_time_maa_g': 6.39,
     'L1_attn_time_decay': 3.429,
     'L1_attn_time_faaaa': 8.0}
    for name, (base, spread) in spreads.items():
        noise = np.random.default_rng([zlib.crc32(name.encode()), seed]).standard_normal(out[name].shape)
        drawn = base * np.exp(spread * noise) if base else spread * noise
        out[name] = jnp.asarray(drawn.astype(out[name].dtype))
    for name, factor in factors.items():
        out[name] = (out[name] * factor).astype(out[name].dtype)
    return out
```

```python
import numpy as np
import concourse.bass as bass
from concourse import mybir
from contextlib import ExitStack

F32 = mybir.dt.float32
BF16 = mybir.dt.bfloat16
I32 = mybir.dt.int32
U32 = mybir.dt.uint32
ALU = mybir.AluOpType
ACT = mybir.ActivationFunctionType
AX = mybir.AxisListType.X

P = 128
B, S, D = 2, 512, 256
N = B * S
NT = N // P
TPB = NT // B
DC = D // P
LN_EPS = 1e-5

H0, TOPK, DV = 128, 32, 2
Q4 = P // TOPK
HG = H0 // Q4
PARTS = 3
ROWS = PARTS * PARTS * 2 * Q4
COLS = 1 + 2 * DV

E, INTER, KSEL, CAP = 64, 176, 6, 128
SHARED = 2 * INTER
IC = INTER // 2
SROWS = [128, 128, SHARED - 256]
TAB = D + E
PAD = N + CAP

H1, HN = 32, 8
HH = P // HN
GN_EPS = 1e-5 * 144
FF = 640
FC = FF // P

CONST = {}
for _name, _n in (("ident", P), ("pdist", P), ("steps", P), ("heads", P), ("tokinv", NT), ("vrow", 4), ("slot", 1),
                  ("jdec", 1), ("quad", 4)):
    CONST[_name] = (sum(n for _, n in CONST.values()), _n)
NCONST = sum(n for _, n in CONST.values())


def constants():
    p = np.arange(P)[:, None]
    i = np.arange(P)[None, :]
    cols = {
        "ident": p == i,
        "pdist": np.maximum(i - p - 1, 0),
        "steps": i + 0 * p,
        "heads": p // HN == i // HN,
        "tokinv": N - (p + P * np.arange(NT)[None, :]),
        "vrow": H0 * np.array([[S - 1, 0, S + S - 1, S]]) + p,
        "slot": p,
        "jdec": P - 1 - p,
        "quad": (p % 32) // HN == np.arange(4)[None, :],
    }
    return np.concatenate([np.broadcast_to(cols[k], (P, n)) for k, (_, n) in CONST.items()], 1).astype(np.float32)


def block_kernel(nc, x, consts, w_qk, w_v, w_gate, w_sh13, w_sh2, w_o0, w_13, w_2, maa, td_row, td_col, u_row,
                 w_rkvgo, gamma, beta, w_fc, w_pj, out):
    x_v = x.rearrange("b (t p) d -> p (b t) d", p=P)
    out_v = out.rearrange("b (t p) d -> p (b t) d", p=P)

    tok_tab = nc.dram_tensor("tok_tab", (PAD, TAB), F32, kind="Internal").ap()
    val_tab = nc.dram_tensor("val_tab", (N * H0, DV), F32, kind="Internal").ap()
    q_dram = nc.dram_tensor("q_dram", (2, PARTS, H0, N), BF16, kind="Internal").ap()
    k_dram = nc.dram_tensor("k_dram", (PARTS, H0, B, 2, TOPK), BF16, kind="Internal").ap()
    routed = [nc.dram_tensor(f"routed{i}", (PAD, D), F32, kind="Internal").ap() for i in range(2)]

    ctx = ExitStack()
    with ctx:
        def sb(name, shape, dt=F32):
            return ctx.enter_context(nc.sbuf_tensor(name, shape, dt))

        def sem(name):
            return ctx.enter_context(nc.semaphore(name))

        xs = sb("xs", [P, NT, D])
        xn = sb("xn", [P, NT, TAB])
        xnT = sb("xnT", [P, DC, N])
        cst = sb("cst", [P, NCONST])
        ones = sb("ones", [P, P])
        gb = sb("gb", [P, 2, D])
        wb = sb("wb", [P, 2, P])
        stats = sb("stats", [P, NT, 6])
        mv = sb("mv", [P, NT, 2])
        rstd = sb("rstd", [P, 2, NT])
        rsm = sb("rsm", [P, 3, NT])
        tsum = sb("tsum", [P, 8])
        gst = sb("gst", [P, 3, TPB * H1])
        nat_tmp = sb("nat_tmp", [P, 2, E])

        def const(name):
            at, n = CONST[name]
            return cst[:, at:at + n]

        ident = const("ident")

        BIGW = 44000
        big = sb("big", [P, BIGW])
        used = [0]

        def carve(words, rows=P, at=None):
            start = used[0] if at is None else at
            if at is None:
                used[0] += words
            assert start + words <= BIGW, (start, words)
            return big[0:rows, start:start + words]

        def v3(ap, a, n):
            return ap.rearrange("p (a n) -> p a n", a=a)

        wqk = v3(carve(DC * 256), DC, 256)
        wv = v3(carve(DC * D), DC, D)
        wg = v3(carve(DC * E), DC, E)
        wsh13 = v3(carve(DC * 2 * SHARED), DC, 2 * SHARED)
        early_weights = used[0]
        wsh2 = v3(carve(3 * D), 3, D)
        wo0 = v3(carve(DC * D), DC, D)
        qparts_at = used[0]
        qparts = carve(2 * PARTS * N // 2).bitcast(BF16).rearrange("p (s a n) -> p s a n", s=2, a=PARTS)
        oT = v3(carve(DC * N, at=qparts_at), DC, N)
        keys_at = used[0]
        keys = carve(B * 2 * S).rearrange("p (b s n) -> p b s n", b=B, s=2)
        th_sh = v3(carve(2 * S, at=keys_at), 2, S)
        ge_sh = v3(carve(2 * S, at=keys_at + 2 * S), 2, S)
        onat = v3(carve(NT * D, at=keys_at), NT, D)
        topv = carve(B * 2 * TOPK).rearrange("p (b s n) -> p b s n", b=B, s=2)
        topi = carve(B * 2 * TOPK).bitcast(U32).rearrange("p (b s n) -> p b s n", b=B, s=2)
        dkf = carve(B * 2 * TOPK)
        dkparts = v3(carve(PARTS * 64).bitcast(BF16), PARTS, B * 2 * TOPK)
        vidx = carve(B * 2 * TOPK).bitcast(I32).rearrange("p (b s n) -> p b s n", b=B, s=2)
        vidxT = carve(B * 2 * HG).bitcast(I32)
        vals = carve(B * 2 * HG * DV).rearrange("p (b s g d) -> p b s g d", b=B, s=2, g=HG)
        qx_at = used[0]
        qx = v3(carve(HG * S // 2, ROWS).bitcast(BF16), HG, S)
        racc = [v3(carve(NT * D, at=qx_at + i * NT * D), NT, D) for i in range(2)]
        sc = v3(carve(NT * (E + 2), at=qx_at), NT, E + 2)
        sr = v3(carve(NT * (E + 2), at=qx_at + 528), NT, E + 2)
        skey = v3(carve(NT * E, at=qx_at + 1056), NT, E)
        lg = v3(carve(NT * E, at=qx_at + 1568), NT, E)
        qs = carve(N, at=qx_at + 2080)
        qpos = carve(N, at=qx_at + 2080 + N)
        sk_at = used[0]
        sk = carve(B * HG * P // 2, ROWS).bitcast(BF16).rearrange("p (b g n) -> p b g n", b=B, g=HG)
        sk_all = carve(B * HG * P // 2, at=sk_at)
        vp_at = used[0]
        vp = carve(B * HG * 32).rearrange("p (b g c) -> p b g c", b=B, g=HG)
        vp_all = carve(B * HG * 32, at=vp_at)
        ex_at = used[0]
        ex = v3(carve(8 * S), 8, S)
        avT = v3(carve(2 * S), 2, S)
        W13 = DC * 2 * INTER
        w13r = [v3(carve(W13, at=ex_at + r * (W13 + 2 * D)), DC, 2 * INTER) for r in range(4)]
        w2r = [v3(carve(2 * D, IC, at=ex_at + r * (W13 + 2 * D) + W13), 2, D) for r in range(4)]
        assert 4 * (W13 + 2 * D) <= 10 * S
        nat_at = used[0]
        nat = carve(TPB * 8 * P).rearrange("p (t g m) -> p t g m", t=TPB, g=8)
        vnat = v3(carve(NT * D, at=nat_at), NT, D)
        slotk = carve(N, E, at=nat_at + NT * D)
        slots = carve(CAP, E, at=nat_at + NT * D + N)
        qmask = v3(carve(NT * H0), NT, H0)
        hs = v3(carve(3 * N), 3, N)
        sidx = carve(E).bitcast(I32)
        rt8 = v3(carve(NT * 8), NT, 8)
        zero = carve(TAB)
        moe_at = used[0]
        xe = v3(carve(4 * TAB), 4, TAB)
        xeT = carve(2 * D).rearrange("p (r c n) -> p r c n", r=2, c=DC)
        th = v3(carve(2 * INTER), 2, INTER)
        ge = v3(carve(2 * INTER), 2, INTER)
        hm = v3(carve(2 * INTER), 2, INTER)
        heT = carve(2 * 2 * P, IC).rearrange("p (r c n) -> p r c n", r=2, c=2)
        ye = v3(carve(2 * D), 2, D)
        den_at = used[0]
        den = carve(3 * TPB * H0).rearrange("p (k t h) -> p k t h", k=3, t=TPB)

        w_fc1 = v3(carve(DC * FF, at=0), DC, FF)
        w_pj1 = v3(carve(FC * D, at=DC * FF), FC, D)
        assert DC * FF + FC * D <= early_weights
        w5 = carve(5 * DC * D, at=moe_at).rearrange("p (k c n) -> p k c n", k=5, c=DC)
        used[0] = moe_at + 5 * DC * D
        yTs = v3(carve(2 * P), 2, P)
        state = v3(carve(2 * P), 2, P)
        kvt = carve(P)
        edrow = carve(H1)
        edcol = carve(2)
        urow = carve(H1)
        wall = carve(2)
        maat = carve(8)
        kdec = carve(H1)
        assert used[0] <= den_at
        gnt = carve(TPB * D, at=den_at)
        used[0] = early_weights
        mix_at = used[0]
        mix = v3(carve(2 * DC * N), 2, DC * N)
        aring = v3(carve(8 * S, at=mix_at), 8, S)
        vpr_at = used[0]
        vpr = carve(2 * 8 * 160).rearrange("p (r g c) -> p r g c", r=2, g=8)
        dif = v3(carve(DC * N, at=vpr_at), DC, N)
        kq = carve(2 * 4 * N).rearrange("p (f q n) -> p f q n", f=2, q=4)
        rq_at = used[0]
        rq = carve(2 * 4 * N).rearrange("p (f h n) -> p f h n", f=2, h=4)
        hf = v3(carve(FC * N, at=rq_at), FC, N)
        rw = v3(carve(2 * N), 2, N)
        kn = v3(carve(NT * D), NT, D)
        vn = v3(carve(NT * D), NT, D)
        gn = v3(carve(NT * D), NT, D)
        wmask = carve(H1 * P).rearrange("p (h n) -> p h n", h=H1)
        assert used[0] <= moe_at, (used[0], moe_at)

        PS = [ctx.enter_context(nc.psum_tensor(f"ps{i}", [P, 512], F32)) for i in range(8)]

        s_x = [sem(f"x_loaded{i}") for i in range(B)]
        s_const = sem("const_loaded")
        s_wqkg = sem("wqkg_loaded")
        s_wv = sem("wv_loaded")
        s_wsh = sem("wshared_loaded")
        s_wo0 = sem("wo0_loaded")
        s_fill = sem("fills_done")
        s_var = sem("variance_ready")
        s_rstd = sem("rstd_ready")
        s_xn = sem("xn_ready")
        s_xnTp = sem("xnT_in_psum")
        s_xnT = sem("xnT_copied")
        s_kp = sem("k_in_psum")
        s_qp = sem("q_in_psum")
        s_lgp = sem("logits_in_psum")
        s_vp = sem("v_in_psum")
        s_v = sem("v_copied")
        s_kq = sem("kq_copied")
        s_lgs = sem("logits_shifted")
        s_lge = sem("logits_exp")
        s_gate = sem("gates_ready")
        s_skTp = sem("slotkeys_in_psum")
        s_skT = sem("slotkeys_copied")
        s_slots = sem("slots_ready")
        s_slotsTp = sem("slotsT_in_psum")
        s_sidx = sem("slot_tokens_ready")
        s_dk = sem("dk_parts_ready")
        s_vidx = sem("value_rows_ready")
        s_qpart = sem("q_parts_ready")
        s_qmp = sem("qT_in_psum")
        s_qm = sem("qmask_ready")
        s_shp = sem("shared_in_psum")
        s_sht = sem("shared_tanh")
        s_hs = sem("shared_hidden_ready")
        s_tab = sem("token_table_stored")
        s_vtab = sem("value_table_stored")
        s_kst = sem("dk_stored")
        s_skl = sem("sk_loaded")
        s_qst = sem("q_stored")
        s_qxl = [sem(f"qx_loaded{i}") for i in range(B)]
        s_vg = sem("values_gathered")
        s_xe = [sem(f"xe_gathered{i}") for i in range(4)]
        s_wm = [sem(f"expert_weights{i}") for i in range(4)]
        s_xeTp = sem("xeT_in_psum")
        s_xeT = sem("xeT_copied")
        s_hp = sem("h_in_psum")
        s_th = sem("tanh_done")
        s_ge = sem("silu_done")
        s_hm = sem("hidden_done")
        s_hTp = sem("hT_in_psum")
        s_hT = sem("hT_copied")
        s_yp = sem("y_in_psum")
        s_y = sem("y_scaled")
        s_sc = [sem(f"routed_added{i}") for i in range(2)]
        s_vpr = sem("values_placed")
        s_lp = sem("attn_logits_in_psum")
        s_ex = sem("attn_exp_done")
        s_av = sem("attn_out_in_psum")
        s_avT = sem("attn_out_copied")
        s_natp = sem("attn_nat_in_psum")
        s_nat = sem("attn_nat_copied")
        s_on = sem("attn_norm_done")
        s_oTp = sem("oT_in_psum")
        s_oT = sem("oT_copied")
        s_racc = sem("routed_loaded")
        s_res = sem("routed_summed")
        s_x1p = sem("x1_in_psum")
        s_x1 = sem("x1_ready")
        s_wff = sem("ff_weights_loaded")
        s_w5 = sem("w5_loaded")
        s_l1c = sem("block1_rows_loaded")
        s_gb = sem("gamma_beta_loaded")
        s_abs = sem("weight_abs_summed")
        s_absp = sem("weight_abs_in_psum")
        s_tern = sem("ternary_ready")
        s_ed = sem("decay_exp")
        s_edn = sem("decay_negated")
        s_wm1 = sem("decay_tables_exp")
        s_wmc = sem("decay_mask_causal")
        s_ffp = sem("ff_in_psum")
        s_relu = sem("ff_relu_done")
        s_sq = sem("ff_square_done")
        s_mix = sem("mix_ready")
        s_kTp = sem("k1T_in_psum")
        s_kT = sem("k1T_copied")
        s_knp = sem("k1_nat_in_psum")
        s_kn = sem("k1_nat_scaled")
        s_ffd = sem("ff_down_in_psum")
        s_x2 = sem("x2_ready")
        s_rTp = sem("r1T_in_psum")
        s_rq = sem("r1_masked")
        s_rw = sem("r1_decayed")
        s_v1p = sem("v1_in_psum")
        s_v1 = sem("v1_copied")
        s_gp = sem("g1_in_psum")
        s_gt = sem("g1_tanh")
        s_g = sem("g1_ready")
        s_a1p = sem("scores_in_psum")
        s_a1 = sem("scores_masked")
        s_vd = sem("v1_placed")
        s_yTp = sem("yT_in_psum")
        s_yT = sem("yT_copied")
        s_kvp = sem("kv_in_psum")
        s_st = sem("state_ready")
        s_ynp = sem("y_nat_in_psum")
        s_yn = sem("y_nat_copied")
        s_gv = sem("group_var_ready")
        s_gs = sem("group_std_ready")
        s_z = sem("z_ready")
        s_zTp = sem("zT_in_psum")
        s_zT = sem("zT_copied")
        s_op = sem("out_in_psum")
        s_o = sem("out_ready")
        s_out = sem("out_stored")
        s_dve = sem("vector_chain")
        s_act = sem("scalar_chain")

        NPAIR = 3 * B
        NG = B * 8
        SLOTS = 4
        UNITS = B * TPB * 2

        block = ctx.enter_context(nc.Block())

        @block.sync
        def _(sp):
            for b in range(B):
                sp.dma_start(xs[:, b * TPB:(b + 1) * TPB, :], x_v[:, b * TPB:(b + 1) * TPB, :]).then_inc(s_x[b], 16)
            sp.dma_start(cst[:, :], consts).then_inc(s_const, 16)
            sp.dma_start(wqk, w_qk).then_inc(s_wqkg, 16)
            sp.dma_start(wg, w_gate).then_inc(s_wqkg, 16)
            sp.dma_start(wv, w_v).then_inc(s_wv, 16)
            sp.dma_start(wsh13, w_sh13).then_inc(s_wsh, 16)
            sp.dma_start(wsh2[:, 0:2, :], w_sh2[0:256, :].rearrange("(c p) n -> p c n", p=P)).then_inc(s_wsh, 16)
            sp.dma_start(wsh2[0:SROWS[2], 2, :], w_sh2[256:SHARED, :]).then_inc(s_wsh, 16)
            sp.dma_start(wo0, w_o0).then_inc(s_wo0, 16)
            sp.wait_ge(s_fill, 1)
            sp.dma_start(tok_tab[N:PAD, :], zero).then_inc(s_tab, 16)
            for e in range(SLOTS):
                sp.dma_start(w13r[e], w_13[e]).then_inc(s_wm[e], 16)
                sp.dma_start(w2r[e], w_2[e]).then_inc(s_wm[e], 16)
            sp.wait_ge(s_gate, 1)
            sp.dma_start(tok_tab[0:N, :].rearrange("(t p) d -> p t d", p=P), xn[:, :, :]).then_inc(s_tab, 16)
            sp.wait_ge(s_v, NT)
            sp.dma_start(val_tab.rearrange("(t p h) d -> p t (h d)", p=P, h=H0), vnat).then_inc(s_vtab, 16)
            sp.wait_ge(s_dk, 1)
            sp.dma_start(k_dram.rearrange("a h b s j -> h a (b s j)"), dkparts).then_inc(s_kst, 16)
            sp.wait_ge(s_kst, 16)
            sp.wait_ge(s_fill, 2)
            for a in range(PARTS):
                for side in range(2):
                    for h4 in range(Q4):
                        first = a * 24 + side * Q4 + h4
                        for b in range(B):
                            sp.dma_start(sk[first:first + 17:8, b, :, TOPK * h4:TOPK * (h4 + 1)],
                                         k_dram[:, HG * h4:HG * (h4 + 1), b, side, :]).then_inc(s_skl, 16)
            sp.wait_ge(s_qpart, 2)
            sp.dma_start(q_dram.rearrange("s a h n -> h s a n"), qparts).then_inc(s_qst, 16)
            sp.wait_ge(s_qst, 16)

            def load_q(b):
                for a in range(PARTS):
                    for ap in range(PARTS):
                        for side in range(2):
                            first = a * 24 + ap * 8 + side * 4
                            sp.dma_start(qx[first:first + 4, :, :],
                                         q_dram[side, a, :, b * S:(b + 1) * S].rearrange("(q g) n -> q g n", q=Q4))\
                              .then_inc(s_qxl[b], 16)

            sp.wait_ge(s_skTp, 2)
            load_q(0)
            sp.wait_ge(s_shp, NPAIR)
            sp.dma_start(w_fc1, w_fc).then_inc(s_wff, 16)
            sp.dma_start(w_pj1, w_pj).then_inc(s_wff, 16)
            w13_v = w_13.rearrange("(g u) p c n -> u p g (c n)", u=SLOTS)
            w2_v = w_2.rearrange("(g u) p c n -> u p g (c n)", u=SLOTS)
            with sp.Fori(1, E // SLOTS) as g:
                for u in range(SLOTS):
                    sp.wait_ge(s_yp, g * SLOTS + (u - SLOTS + 1))
                    sp.dma_start(w13r[u].rearrange("p c n -> p (c n)").unsqueeze(1), w13_v[u, :, bass.ds(g, 1), :])\
                      .then_inc(s_wm[u], 16)
                    sp.dma_start(w2r[u].rearrange("p c n -> p (c n)").unsqueeze(1), w2_v[u, :, bass.ds(g, 1), :])\
                      .then_inc(s_wm[u], 16)
            sp.wait_ge(s_y, E)
            sp.dma_start(w5, w_rkvgo).then_inc(s_w5, 16)
            sp.dma_start(edrow, td_row.partition_broadcast(P)).then_inc(s_l1c, 16)
            sp.dma_start(urow, u_row.partition_broadcast(P)).then_inc(s_l1c, 16)
            sp.dma_start(edcol, td_col).then_inc(s_l1c, 16)
            sp.dma_start(maat, maa).then_inc(s_l1c, 16)
            sp.dma_start(gb[:, 0, :], gamma.partition_broadcast(P)).then_inc(s_gb, 16)
            sp.dma_start(gb[:, 1, :], beta.partition_broadcast(P)).then_inc(s_gb, 16)
            sp.wait_ge(s_lp, NG * 2)
            load_q(1)
            sp.wait_ge(s_lp, NG * 4)
            for i in range(2):
                sp.wait_ge(s_sc[i], 16 * (1 + E // 2))
                sp.dma_start(racc[i], routed[i][0:N, :].rearrange("(t p) d -> p t d", p=P)).then_inc(s_racc, 16)
            for t in range(NT):
                sp.wait_ge(s_o, t + 1)
                sp.dma_start(out_v[:, t, :], xs[:, t, :]).then_inc(s_out, 16)
            sp.wait_ge(s_out, 16 * NT)

        @block.gpsimd
        def _(pool):
            nc.gpsimd.memset(zero, 0.0).then_inc(s_fill, 1)
            nc.gpsimd.memset(sk_all, 0.0).then_inc(s_fill, 1)
            nc.gpsimd.memset(vp_all, 0.0).then_inc(s_fill, 1)
            nc.gpsimd.memset(ones[:, :], 1.0)
            nc.gpsimd.memset(rsm[:, 2, :], -0.5).then_inc(s_fill, 1)
            pool.wait_ge(s_fill, 4)
            for h4 in range(Q4):
                r = slice(32 * h4, 32 * h4 + 32)
                last = nc.gpsimd.memset(vp[r, :, :, COLS * h4:COLS * h4 + 1], 1.0)
            last.then_inc(s_fill, 1)
            pool.wait_ge(s_fill, 5)

            for i in range(2):
                nc.gpsimd.dma_start(routed[i].rearrange("(r p) d -> p r d", p=P),
                                    zero[:, 0:D].rearrange("p (a d) -> p a d", a=1).broadcast_to([P, PAD // P, D]))\
                  .then_inc(s_sc[i], 16)

            def rsqrt(n):
                pool.wait_ge(s_var, n)
                nc.gpsimd.tensor_tensor(rstd[:, 1, :], rstd[:, 0, :], rsm[:, 2, :], ALU.pow).then_inc(s_rstd, 1)

            rsqrt(1)

            def value_gather(n):
                b, rest = divmod(n, 2 * HG)
                side, g = divmod(rest, HG)
                nc.gpsimd.indirect_dma_start(vals[:, b, side, g, :], None, val_tab,
                                             bass.IndirectOffsetOnAxis(ap=vidxT[:, n:n + 1], axis=0))\
                  .then_inc(s_vg, 16)

            def token_gather(e):
                if e >= SLOTS:
                    pool.wait_ge(s_y, e - SLOTS + 1)
                nc.gpsimd.indirect_dma_start(xe[:, e % SLOTS, :], None, tok_tab,
                                             bass.IndirectOffsetOnAxis(ap=sidx[:, e:e + 1], axis=0))\
                  .then_inc(s_xe[e % SLOTS], 16)

            def routed_add(e):
                pool.wait_ge(s_y, e + 1)
                pool.wait_ge(s_sc[e % 2], 16 * (1 + e // 2))
                nc.gpsimd.indirect_dma_start(routed[e % 2], bass.IndirectOffsetOnAxis(ap=sidx[:, e:e + 1], axis=0),
                                             ye[:, e % 2, :], None, compute_op=ALU.add)\
                  .then_inc(s_sc[e % 2], 16)

            NV = B * 2 * HG
            FIRST = 56
            pool.wait_ge(s_vidx, 1)
            pool.wait_ge(s_vtab, 16)
            done = 0
            while done < FIRST:
                value_gather(done)
                done += 1
            pool.wait_ge(s_sidx, 1)
            pool.wait_ge(s_tab, 32)
            for e in range(3):
                token_gather(e)
            for e in range(E):
                if e + 3 < E:
                    token_gather(e + 3)
                routed_add(e)
                if done < NV:
                    value_gather(done)
                    done += 1
            while done < NV:
                value_gather(done)
                done += 1

            pool.wait_ge(s_racc, 32)
            nc.gpsimd.tensor_tensor(racc[0], racc[0], racc[1], ALU.add).then_inc(s_res, 1)
            rsqrt(2)
            pool.wait_ge(s_wm1, 1)
            nc.gpsimd.affine_select(out=wmask, in_=wmask, compare_op=ALU.is_ge, fill=0.0, base=-1,
                                    pattern=[[0, H1], [1, P]], channel_multiplier=-1).then_inc(s_wmc, 1)
            pool.wait_ge(s_x1, NT)
            nc.gpsimd.memset(kq, 0.0).then_inc(s_wmc, 1)
            pool.wait_ge(s_mix, 4)
            pool.wait_ge(s_v1, NT)
            nc.gpsimd.memset(vpr, 0.0).then_inc(s_vd, 1)
            pool.wait_ge(s_vd, 1)
            for t in range(NT):
                if t >= 2:
                    pool.wait_ge(s_yTp, 2 * (t - 1))
                dst = vpr[:, t % 2, :, :].rearrange("p g (a c) -> p g a c", a=4)[:, :, :, 0:HN]
                nc.gpsimd.tensor_copy(dst, vn[:, t, :].rearrange("p (g a c) -> p g a c", g=8, a=4)).then_inc(s_vd, 1)

        @block.scalar
        def _(act):
            def xnT_copies(base):
                for t in range(NT):
                    act.wait_ge(s_xnTp, base + t + 1)
                    nc.scalar.activation(xnT[:, :, t * P:(t + 1) * P],
                                         PS[t % 2][:, 0:D].rearrange("p (c n) -> p c n", c=DC), ACT.Copy)\
                      .then_inc(s_xnT, 1)

            xnT_copies(0)
            act.wait_ge(s_lgs, 1)
            nc.scalar.activation(sc[:, :, 0:E], lg, ACT.Exp).then_inc(s_lge, 1)
            for t in range(NT):
                act.wait_ge(s_vp, t + 1)
                nc.scalar.activation(vnat[:, t, :], PS[(0, 1, 7)[t % 3]][:, 0:D], ACT.Copy).then_inc(s_v, 1)
            for k in range(2):
                act.wait_ge(s_skTp, k + 1)
                nc.scalar.activation(slotk[:, k * 512:(k + 1) * 512], PS[6 + k][0:E, :], ACT.Copy).then_inc(s_skT, 1)
            act.wait_ge(s_dk, 1)
            for i in range(NPAIR):
                act.wait_ge(s_shp, i + 1)
                if i >= 2:
                    act.wait_ge(s_hs, i - 1)
                rows = SROWS[i // B]
                nc.scalar.activation(th_sh[0:rows, i % 2, :], PS[2 + 2 * (i % 2)][0:rows, :], ACT.Tanh, scale=0.5)\
                  .then_inc(s_sht, 1)

            def tokens_in(e, u):
                act.wait_ge(s_xeTp, e + 1)
                nc.scalar.activation(xeT[:, u % 2, :, :], PS[u % 2][:, 0:D].rearrange("p (c n) -> p c n", c=DC),
                                     ACT.Copy).then_inc(s_xeT, 1)
                act.wait_ge(s_hp, e + 1)
                nc.scalar.activation(th[:, u % 2, :], PS[2 + u % 2][:, 0:INTER], ACT.Tanh, scale=0.5)\
                  .then_inc(s_th, 1)

            def scale_out(e, u, free, gate):
                act.wait_ge(s_yp, e + 1)
                act.wait_ge(s_sc[u % 2], free)
                nc.scalar.activation(ye[:, u % 2, :], PS[6 + u % 2][:, 0:D], ACT.Copy, scale=gate).then_inc(s_y, 1)

            tokens_in(0, 0)
            gates = xe[:, :, D:TAB].rearrange("p r (g u) -> p r u g", u=SLOTS)
            with act.Fori(0, E // SLOTS - 1) as g:
                for u in range(SLOTS):
                    tokens_in(g * SLOTS + (u + 1), u + 1)
                    scale_out(g * SLOTS + u, u, g * 32 + 16 * (1 + u // 2), gates[:, u, u, bass.ds(g, 1)])
            for e in range(E - SLOTS, E):
                if e + 1 < E:
                    tokens_in(e + 1, e + 1)
                scale_out(e, e, 16 * (1 + e // 2), xe[:, e % SLOTS, D + e:D + e + 1])

            act.wait_ge(s_wff, 32)
            act.wait_ge(s_sidx, 1)
            nat_flat = big[:, nat_at:nat_at + DC * FF]
            nc.scalar.activation(nat_flat, w_fc1.rearrange("p c n -> p (c n)"), ACT.Abs, accum_out=tsum[:, 0:1])\
              .then_inc(s_act, 1)
            act.wait_ge(s_act, 1)
            nc.scalar.activation(nat_flat, w_pj1.rearrange("p c n -> p (c n)"), ACT.Abs, accum_out=tsum[:, 1:2])\
              .then_inc(s_abs, 1)

            def place_values(b):
                act.wait_ge(s_vg, 16 * 2 * HG * (b + 1))
                act.wait_ge(s_fill, 5)
                for h4 in range(Q4):
                    r = slice(32 * h4, 32 * h4 + 32)
                    for side in range(2):
                        c = COLS * h4 + 1 + DV * side
                        last = nc.scalar.activation(vp[r, b, :, c:c + DV], vals[r, b, side, :, :], ACT.Copy)
                last.then_inc(s_vpr, 1)

            for b in range(B):
                place_values(b)
                for n in range(32 * b, 32 * b + 32):
                    act.wait_ge(s_lp, n + 1)
                    if n >= 8:
                        act.wait_ge(s_av, n // 4 - 1)
                    nc.scalar.activation(ex[:, n % 8, :], PS[n % 4][:, :], ACT.Exp).then_inc(s_ex, 1)
            for t in range(NT):
                act.wait_ge(s_oTp, t + 1)
                nc.scalar.activation(oT[:, :, t * P:(t + 1) * P], PS[t % 2][:, 0:D].rearrange("p (c n) -> p c n", c=DC),
                                     ACT.Copy).then_inc(s_oT, 1)

            act.wait_ge(s_l1c, 64)
            nc.scalar.activation(edrow, edrow, ACT.Exp).then_inc(s_ed, 1)
            nc.scalar.activation(edcol, edcol, ACT.Exp).then_inc(s_ed, 1)
            act.wait_ge(s_edn, 1)
            nc.scalar.activation(kdec, edrow, ACT.Exp, scale=const("jdec"))
            nc.scalar.activation(wall, edcol, ACT.Exp, scale=float(P))
            for f in range(2):
                nc.scalar.activation(wb[:, f, :], const("steps"), ACT.Exp, scale=edcol[:, f:f + 1])
            act.wait_ge(s_x1, NT)
            for h in range(H1):
                last = nc.scalar.activation(wmask[:, h, :], const("pdist"), ACT.Exp, scale=edrow[:, h:h + 1])
            last.then_inc(s_wm1, 1)
            xnT_copies(NT)
            for i in range(2 * FC):
                act.wait_ge(s_ffp, i + 1)
                nc.scalar.activation(hf[:, i // 2, (i % 2) * S:(i % 2 + 1) * S], PS[2 + i % 6][:, :], ACT.Relu)\
                  .then_inc(s_relu, 1)
            act.wait_ge(s_wmc, 2)
            for i in range(4):
                f, n = divmod(i, 2)
                act.wait_ge(s_kTp, i + 1)
                for q in range(4):
                    r = slice(32 * q, 32 * q + 32)
                    last = nc.scalar.activation(kq[r, f, q, n * S:(n + 1) * S], PS[i][r, :], ACT.Copy)
                last.then_inc(s_kT, 1)
            act.wait_ge(s_x2, NT)
            for i in range(4):
                f, n = divmod(i, 2)
                act.wait_ge(s_rTp, i + 1)
                for h in range(4):
                    last = nc.scalar.activation(rq[:, f, h, n * S:(n + 1) * S], PS[i][:, :], ACT.Copy,
                                                scale=const("quad")[:, h:h + 1])
                last.then_inc(s_rq, 1)
            for t in range(NT):
                act.wait_ge(s_v1p, t + 1)
                nc.scalar.activation(vn[:, t, :], PS[4 + t % 4][:, 0:D], ACT.Copy).then_inc(s_v1, 1)
            for t in range(NT):
                act.wait_ge(s_gp, t + 1)
                nc.scalar.activation(gn[:, t, :], PS[t % 4][:, 0:D], ACT.Tanh, scale=0.5).then_inc(s_gt, 1)
            for t in range(NT):
                for f in range(2):
                    u = 2 * t + f
                    act.wait_ge(s_yTp, u + 1)
                    if t >= 1 and f == 0:
                        act.wait_ge(s_ynp, t)
                    nc.scalar.activation(yTs[:, f, 0:P], PS[4 + u % 2][:, 0:P], ACT.Copy).then_inc(s_yT, 1)
                act.wait_ge(s_ynp, t + 1)
                nc.scalar.activation(xn[:, t, 0:D], PS[7][:, 0:D], ACT.Copy).then_inc(s_yn, 1)
                if t == TPB or t == NT - 1:
                    act.wait_ge(s_gv, 1 + t // (NT - 1))
                    nc.scalar.activation(gst[:, 1, :], gst[:, 0, :], ACT.Sqrt).then_inc(s_gs, 1)
            for t in range(NT):
                act.wait_ge(s_zTp, t + 1)
                nc.scalar.activation(xnT[:, :, t * P:(t + 1) * P], PS[t % 2][:, 0:D].rearrange("p (c n) -> p c n", c=DC),
                                     ACT.Copy).then_inc(s_zT, 1)

        @block.vector
        def _(dve):
            steps = [0]

            def note(ins):
                steps[0] += 1
                ins.then_inc(s_dve, 1)

            def settle():
                dve.wait_ge(s_dve, steps[0])

            def link(ins):
                note(ins)
                settle()

            def wide(ap, *shape):
                return ap.broadcast_to([P, *shape])

            def layernorm(n):
                for t in range(NT):
                    if n == 0 and t % TPB == 0:
                        dve.wait_ge(s_x[t // TPB], 16)
                    note(nc.vector.bn_stats(stats[:, t, :], xs[:, t, :]))
                settle()
                for t in range(NT):
                    note(nc.vector.bn_aggr(mv[:, t, :], stats[:, t, :]))
                settle()
                nc.vector.tensor_scalar(rstd[:, 0, :], mv[:, :, 1], LN_EPS, None, ALU.add).then_inc(s_var, 1)
                dve.wait_ge(s_rstd, n + 1)
                for t in range(NT):
                    nc.vector.tensor_scalar(xn[:, t, 0:D], xs[:, t, :], mv[:, t, 0:1], rstd[:, 1, t:t + 1],
                                            ALU.subtract, ALU.mult).then_inc(s_xn, 1)

            layernorm(0)
            dve.wait_ge(s_const, 16)

            dve.wait_ge(s_kp, 1)
            for b in range(B):
                note(nc.vector.tensor_copy(keys[:, b, 0, :], PS[2 + b][:, ::-1]))
                note(nc.vector.tensor_scalar(keys[:, b, 1, :], PS[2 + b][:, :], -1.0, None, ALU.mult))
            dve.wait_ge(s_qp, 1)
            for b in range(B):
                note(nc.vector.tensor_scalar(qpos[:, b * S:(b + 1) * S], PS[4 + b][:, :], 0.0, None, ALU.max))
                last = nc.vector.tensor_scalar(qs[:, b * S:(b + 1) * S], PS[4 + b][:, :], 0.0, None, ALU.min)
                if b < B - 1:
                    note(last)
            last.then_inc(s_kq, 1)

            dve.wait_ge(s_lgp, 1)
            lp = PS[6][:, :].rearrange("p (t e) -> p t e", t=NT)
            note(nc.vector.memset(sc[:, :, E:E + 2], -1.0))
            link(nc.vector.tensor_reduce(rsm[:, 0, :], lp, AX, ALU.max))
            nc.vector.tensor_tensor(lg, lp, rsm[:, 0, :].unsqueeze(2).broadcast_to([P, NT, E]), ALU.subtract)\
              .then_inc(s_lgs, 1)
            dve.wait_ge(s_lge, 1)
            link(nc.vector.tensor_reduce(rsm[:, 0, :], sc[:, :, 0:E], AX, ALU.add))
            link(nc.vector.reciprocal(rsm[:, 1, :], rsm[:, 0, :]))
            link(nc.vector.tensor_tensor(sc[:, :, 0:E], sc[:, :, 0:E],
                                         rsm[:, 1, :].unsqueeze(2).broadcast_to([P, NT, E]), ALU.mult))
            for t in range(NT):
                note(nc.vector.max(rt8[:, t, :], sc[:, t, 0:E]))
            settle()
            link(nc.vector.memset(rt8[:, :, KSEL:8], -1.0))
            for t in range(NT):
                note(nc.vector.match_replace(sr[:, t, :], rt8[:, t, :], sc[:, t, :], -2.0))
            settle()
            link(nc.vector.tensor_scalar(lg, sr[:, :, 0:E], -1.5, None, ALU.is_lt))
            note(nc.vector.tensor_tensor(skey, lg, const("tokinv").unsqueeze(2).broadcast_to([P, NT, E]), ALU.mult))
            nc.vector.tensor_tensor(xn[:, :, D:TAB], lg, sc[:, :, 0:E], ALU.mult).then_inc(s_gate, 1)

            settle()
            sides = [(b, side) for b in range(B) for side in range(2)]
            for r in range(TOPK // 8):
                c = slice(8 * r, 8 * r + 8)
                for b, side in sides:
                    note(nc.vector.max(topv[:, b, side, c], keys[:, b, side, :]))
                settle()
                for b, side in sides:
                    note(nc.vector.max_index(topi[:, b, side, c], topv[:, b, side, c], keys[:, b, side, :]))
                settle()
                if r < TOPK // 8 - 1:
                    for b, side in sides:
                        note(nc.vector.match_replace(keys[:, b, side, :], topv[:, b, side, c], keys[:, b, side, :],
                                                     -3.0e38))
                    settle()
            for n, (b, side) in enumerate(sides):
                note(nc.vector.tensor_scalar(vidx[:, b, side, :], topi[:, b, side, :], float(H0 if side else -H0),
                                             const("vrow")[:, n:n + 1], ALU.mult, ALU.add))
            settle()
            nc.vector.transpose(vidxT.bitcast(U32), vidx.rearrange("p b s n -> p (b s n)").bitcast(U32))\
              .then_inc(s_vidx, 1)
            dk4 = dkf.rearrange("p (b s n) -> p b s n", b=B, s=2)
            note(nc.vector.tensor_tensor(dk4[:, :, 0, :], topv[:, :, 0, :],
                                         topv[:, :, 0, 0:1].broadcast_to([P, B, TOPK]), ALU.subtract))
            link(nc.vector.tensor_tensor(dk4[:, :, 1, :], topv[:, :, 1, 0:1].broadcast_to([P, B, TOPK]),
                                         topv[:, :, 1, :], ALU.subtract))

            def split(src, parts):
                link(nc.vector.tensor_copy(parts[0], src))
                link(nc.vector.tensor_tensor(src, src, parts[0], ALU.subtract))
                link(nc.vector.tensor_copy(parts[1], src))
                return nc.vector.tensor_tensor(parts[2], src, parts[1], ALU.subtract)

            split(dkf, [dkparts[:, a, :] for a in range(PARTS)]).then_inc(s_dk, 1)
            dve.wait_ge(s_kq, 1)
            dve.wait_ge(s_qmp, 2)
            for side, src in ((0, qpos), (1, qs)):
                split(src, [qparts[:, side, a, :] for a in range(PARTS)]).then_inc(s_qpart, 1)
            for k in range(2):
                nc.vector.tensor_scalar(qmask[:, 4 * k:4 * k + 4, :],
                                        PS[k][:, :].rearrange("p (t h) -> p t h", t=4), 0.0, None, ALU.is_gt)\
                  .then_inc(s_qm, 1)

            dve.wait_ge(s_skT, 2)
            for r in range(CAP // 8):
                c = slice(8 * r, 8 * r + 8)
                link(nc.vector.max(slots[:, c], slotk))
                if r < CAP // 8 - 1:
                    link(nc.vector.match_replace(slotk, slots[:, c], slotk, 0.0))
            nc.vector.tensor_scalar(slots[:, 0:1], slots[:, 0:1], 0.0, None, ALU.add).then_inc(s_slots, 1)
            dve.wait_ge(s_slotsTp, 1)
            note(nc.vector.tensor_scalar(nat_tmp[:, 0, :], PS[6][:, 0:E], 0.0, const("slot"), ALU.is_equal, ALU.mult))
            link(nc.vector.tensor_scalar(nat_tmp[:, 1, :], PS[6][:, 0:E], -1.0, float(N), ALU.mult, ALU.add))
            nc.vector.tensor_tensor(sidx, nat_tmp[:, 0, :], nat_tmp[:, 1, :], ALU.add).then_inc(s_sidx, 1)

            for i in range(NPAIR):
                rows = SROWS[i // B]
                k = 2 * (i % 2)
                dve.wait_ge(s_sht, i + 1)
                link(nc.vector.scalar_tensor_tensor(ge_sh[0:rows, i % 2, :], th_sh[0:rows, i % 2, :], 1.0,
                                                    PS[2 + k][0:rows, :], ALU.add, ALU.mult))
                nc.vector.scalar_tensor_tensor(hs[0:rows, i // B, (i % B) * S:(i % B + 1) * S],
                                               ge_sh[0:rows, i % 2, :], 0.5, PS[3 + k][0:rows, :],
                                               ALU.mult, ALU.mult).then_inc(s_hs, 1)

            def hidden(e, u):
                dve.wait_ge(s_th, e + 1)
                nc.vector.scalar_tensor_tensor(ge[:, u % 2, :], th[:, u % 2, :], 1.0, PS[2 + u % 2][:, 0:INTER],
                                               ALU.add, ALU.mult).then_inc(s_ge, 1)
                dve.wait_ge(s_ge, e + 1)
                nc.vector.scalar_tensor_tensor(hm[:, u % 2, :], ge[:, u % 2, :], 0.5,
                                               PS[2 + u % 2][:, INTER:2 * INTER], ALU.mult, ALU.mult)\
                  .then_inc(s_hm, 1)

            def hidden_T(e, u):
                dve.wait_ge(s_hTp, e + 1)
                nc.vector.tensor_copy(heT[:, u % 2, :, :], PS[4 + u % 2][0:IC, 0:2 * P].rearrange("p (c n) -> p c n", c=2))\
                  .then_inc(s_hT, 1)

            hidden(0, 0)
            with dve.Fori(0, E // SLOTS - 1) as g:
                for u in range(SLOTS):
                    hidden_T(g * SLOTS + u, u)
                    hidden(g * SLOTS + (u + 1), u + 1)
            for e in range(E - SLOTS, E):
                hidden_T(e, e)
                if e + 1 < E:
                    hidden(e + 1, e + 1)

            dve.wait_ge(s_absp, 1)
            link(nc.vector.tensor_scalar(tsum[:, 2:4], PS[5][:, 0:2], 1.0 / (FF * D), 1e-5, ALU.mult, ALU.max))
            link(nc.vector.tensor_scalar(tsum[:, 4:6], tsum[:, 2:4], 0.7, None, ALU.mult))
            link(nc.vector.tensor_scalar(tsum[:, 6:8], tsum[:, 4:6], -1.0, None, ALU.mult))
            link(nc.vector.tensor_scalar(tsum[:, 2:4], tsum[:, 2:4], -1.0, None, ALU.mult))
            tern_t = big[:, nat_at:nat_at + DC * FF]
            for k, w in enumerate((w_fc1.rearrange("p c n -> p (c n)"), w_pj1.rearrange("p c n -> p (c n)"))):
                link(nc.vector.tensor_scalar(tern_t, w, tsum[:, 4 + k:5 + k], None, ALU.is_gt))
                link(nc.vector.scalar_tensor_tensor(tern_t, w, tsum[:, 6 + k:7 + k], tern_t, ALU.is_lt, ALU.subtract))
                link(nc.vector.scalar_tensor_tensor(tern_t, tern_t, tsum[:, 2 + k:3 + k], w, ALU.mult, ALU.subtract))
                ins = nc.vector.tensor_tensor(w, tern_t, w, ALU.add)
                if k == 0:
                    link(ins)
                else:
                    ins.then_inc(s_tern, 1)
            dve.wait_ge(s_tern, 1)

            def out_copy(g):
                dve.wait_ge(s_av, g + 1)
                if g >= 2:
                    dve.wait_ge(s_natp, g - 1)
                nc.vector.tensor_copy(avT[:, g % 2, :], PS[4 + g % 2][:, :]).then_inc(s_avT, 1)

            def nat_copy(g):
                dve.wait_ge(s_natp, g + 1)
                nc.vector.tensor_copy(nat[:, :, g % 8, :], PS[6 + g % 2][:, :].rearrange("p (t m) -> p t m", t=TPB))\
                  .then_inc(s_nat, 1)

            for b in range(B):
                for g in range(8 * b, 8 * b + 8):
                    out_copy(g)
                    if g > 8 * b:
                        nat_copy(g - 1)
                nat_copy(8 * b + 7)
                dve.wait_ge(s_nat, 8 * (b + 1))
                dve.wait_ge(s_qm, 2)

                def part(c):
                    v = nat.rearrange("p t g (a m) -> p (t g a) m", a=4)
                    return v[:, :, c:c + 3 * COLS + 1:COLS]

                flat = [den[:, k, :, :].rearrange("p t h -> p (t h)").rearrange("p (x a) -> p x a", a=Q4)
                        for k in range(3)]
                sel = qmask[:, b * TPB:(b + 1) * TPB, :].rearrange("p t (a g) -> p t g a", a=Q4)
                k3 = [f.rearrange("p (t g) a -> p t g a", t=TPB) for f in flat]
                link(nc.vector.reciprocal(flat[0], part(0)))
                link(nc.vector.tensor_tensor(k3[1], k3[0], sel, ALU.mult))
                link(nc.vector.tensor_tensor(flat[2], flat[0], flat[1], ALU.subtract))
                for d in range(DV):
                    o = onat[:, b * TPB:(b + 1) * TPB, :].rearrange("p t (a g d) -> p t g a d", a=Q4, d=DV)[:, :, :, :, d]
                    top = part(1 + d).rearrange("p (t g) a -> p t g a", t=TPB)
                    note(nc.vector.tensor_tensor(o, top, k3[1], ALU.mult))
                    link(nc.vector.tensor_tensor(flat[0], part(1 + DV + d), flat[2], ALU.mult))
                    ins = nc.vector.tensor_tensor(o, o, k3[0], ALU.add)
                    if d == DV - 1:
                        ins.then_inc(s_on, 1)
                    else:
                        link(ins)

            dve.wait_ge(s_res, 1)
            for t in range(NT):
                note(nc.vector.tensor_tensor(xs[:, t, :], xs[:, t, :], racc[0][:, t, :], ALU.add))
            settle()
            for t in range(NT):
                dve.wait_ge(s_x1p, t + 1)
                nc.vector.tensor_tensor(xs[:, t, :], PS[2 + t % 2][:, 0:D], xs[:, t, :], ALU.add).then_inc(s_x1, 1)
            dve.wait_ge(s_x1, NT)

            layernorm(1)
            dve.wait_ge(s_ed, 2)
            note(nc.vector.tensor_scalar(edrow, edrow, 1e30, -1.0, ALU.min, ALU.mult))
            nc.vector.tensor_scalar(edcol, edcol, 1e30, -1.0, ALU.min, ALU.mult).then_inc(s_edn, 1)
            def square(i):
                dve.wait_ge(s_relu, i + 1)
                h = hf[:, i // 2, (i % 2) * S:(i % 2 + 1) * S]
                nc.vector.tensor_tensor(h, h, h, ALU.mult).then_inc(s_sq, 1)

            dve.wait_ge(s_xnT, 2 * NT)
            for c in range(DC):
                src = xnT[:, c, :].rearrange("p (b n) -> p b n", b=B)
                dst = dif[:, c, :].rearrange("p (b n) -> p b n", b=B)
                note(nc.vector.tensor_tensor(dst[:, :, 1:S], src[:, :, 0:S - 1], src[:, :, 1:S], ALU.subtract))
                note(nc.vector.tensor_scalar(dst[:, :, 0:1], src[:, :, 0:1], -1.0, None, ALU.mult))
            settle()

            def mixture(k):
                for c in range(DC):
                    ins = nc.vector.scalar_tensor_tensor(mix[:, k % 2, c * N:(c + 1) * N], dif[:, c, :],
                                                         maat[:, 2 * k + c:2 * k + c + 1], xnT[:, c, :],
                                                         ALU.mult, ALU.add)
                    if c < DC - 1:
                        note(ins)
                ins.then_inc(s_mix, 1)

            dve.wait_ge(s_l1c, 64)
            mixture(0)
            mixture(1)
            for i in range(2 * FC):
                square(i)
            dve.wait_ge(s_edn, 1)
            for t in range(NT):
                dve.wait_ge(s_knp, t + 1)
                if t == 0:
                    dve.wait_ge(s_wm1, 1)
                nc.vector.tensor_tensor(kn[:, t, :].rearrange("p (h n) -> p h n", n=HN),
                                        PS[4 + t % 4][:, 0:D].rearrange("p (h n) -> p h n", n=HN),
                                        kdec.unsqueeze(2).broadcast_to([P, H1, HN]), ALU.mult).then_inc(s_kn, 1)
            mixture(2)
            dve.wait_ge(s_gb, 32)
            for t in range(NT):
                dve.wait_ge(s_ffd, t + 1)
                nc.vector.tensor_tensor(xs[:, t, :], PS[4 + t % 4][:, 0:D], xs[:, t, :], ALU.add).then_inc(s_x2, 1)
            for i in range(4):
                f, n = divmod(i, 2)
                dve.wait_ge(s_rq, i + 1)
                nc.vector.tensor_tensor(rw[:, f, n * S:(n + 1) * S].rearrange("p (t n) -> p t n", n=P),
                                        PS[i][:, :].rearrange("p (t n) -> p t n", n=P),
                                        wb[:, f, :].unsqueeze(1).broadcast_to([P, TPB, P]), ALU.mult).then_inc(s_rw, 1)
            mixture(3)
            dve.wait_ge(s_wmc, 1)
            for h in range(H1):
                note(nc.vector.scalar_tensor_tensor(wmask[:, h, :], ident, urow[:, h:h + 1], wmask[:, h, :],
                                                    ALU.mult, ALU.add))
            settle()
            for t in range(NT):
                dve.wait_ge(s_gt, t + 1)
                nc.vector.scalar_tensor_tensor(gn[:, t, :], gn[:, t, :], 1.0, PS[t % 4][:, 0:D], ALU.add, ALU.mult)\
                  .then_inc(s_g, 1)

            def state_update(u):
                f = u % 2
                dve.wait_ge(s_kvp, (u // 8) * 6 + u % 8 + 1)
                link(nc.vector.tensor_tensor(kvt, PS[6][:, 0:P], const("heads"), ALU.mult))
                nc.vector.scalar_tensor_tensor(state[:, f, :], state[:, f, :], wall[:, f:f + 1], kvt,
                                               ALU.mult, ALU.add).then_inc(s_st, 1)

            def group_norm(b):
                y = xn[:, b * TPB:(b + 1) * TPB, 0:D].rearrange("p t (h n) -> p t h n", n=HN)
                g1 = [gst[:, k, :].rearrange("p (t h) -> p t h", t=TPB) for k in range(3)]
                sq = gnt.rearrange("p (t h n) -> p t h n", t=TPB, n=HN)
                dve.wait_ge(s_yn, TPB * (b + 1))
                link(nc.vector.tensor_reduce(g1[0], y, AX, ALU.add))
                link(nc.vector.tensor_scalar(gst[:, 1, :], gst[:, 0, :], 1.0 / HN, None, ALU.mult))
                for t in range(TPB):
                    note(nc.vector.tensor_tensor(y[:, t], y[:, t], g1[1][:, t].unsqueeze(2).broadcast_to([P, H1, HN]),
                                                 ALU.subtract))
                settle()
                for t in range(TPB):
                    note(nc.vector.tensor_tensor(sq[:, t], y[:, t], y[:, t], ALU.mult))
                settle()
                link(nc.vector.tensor_reduce(g1[0], sq, AX, ALU.add))
                nc.vector.tensor_scalar(gst[:, 0, :], gst[:, 0, :], 1.0 / HN, GN_EPS, ALU.mult, ALU.add)\
                  .then_inc(s_gv, 1)
                dve.wait_ge(s_gs, b + 1)
                link(nc.vector.reciprocal(gst[:, 1, :], gst[:, 1, :]))
                link(nc.vector.tensor_tensor(gst[:, 2, :], gst[:, 1, :], gst[:, 1, :], ALU.mult))
                link(nc.vector.tensor_tensor(gst[:, 2, :], gst[:, 2, :], gst[:, 0, :], ALU.mult))
                link(nc.vector.tensor_scalar(gst[:, 2, :], gst[:, 2, :], -0.5, 1.5, ALU.mult, ALU.add))
                link(nc.vector.tensor_tensor(gst[:, 1, :], gst[:, 1, :], gst[:, 2, :], ALU.mult))
                for t in range(TPB):
                    note(nc.vector.tensor_tensor(y[:, t], y[:, t], g1[1][:, t].unsqueeze(2).broadcast_to([P, H1, HN]),
                                                 ALU.mult))
                settle()
                for k, op in ((0, ALU.mult), (1, ALU.add)):
                    for t in range(b * TPB, (b + 1) * TPB):
                        note(nc.vector.tensor_tensor(xn[:, t, 0:D], xn[:, t, 0:D], gb[:, k, :], op))
                    settle()
                for t in range(b * TPB, (b + 1) * TPB):
                    nc.vector.scalar_tensor_tensor(xn[:, t, 0:D], xn[:, t, 0:D], 0.5, gn[:, t, :], ALU.mult, ALU.mult)\
                      .then_inc(s_z, 1)

            for u in range(UNITS):
                if u % 8 == 0:
                    if u:
                        dve.wait_ge(s_yTp, u)
                    nc.vector.memset(state, 0.0).then_inc(s_st, 1)
                    dve.wait_ge(s_st, 7 * (u // 8) + 1)
                f = u % 2
                for q in range(4):
                    a = 4 * u + q
                    dve.wait_ge(s_a1p, a + 1)
                    if a >= 8:
                        dve.wait_ge(s_yTp, u - 1)
                    heads = slice(HH * f + 4 * q, HH * f + 4 * q + 4)
                    nc.vector.tensor_tensor(aring[:, a % 8, :].rearrange("p (h n) -> p h n", h=4),
                                            PS[q][:, :].rearrange("p (h n) -> p h n", h=4), wmask[:, heads, :],
                                            ALU.mult).then_inc(s_a1, 1)
                if u >= 1 and (u - 1) % 8 < 6:
                    state_update(u - 1)
                if u == 8 + 3:
                    group_norm(0)
            group_norm(1)
            for t in range(NT):
                dve.wait_ge(s_op, t + 1)
                nc.vector.tensor_tensor(xs[:, t, :], PS[4 + t % 4][:, 0:D], xs[:, t, :], ALU.add).then_inc(s_o, 1)

        @block.tensor
        def _(pe):
            def product(o, pairs):
                for n, (w, m) in enumerate(pairs):
                    last = nc.tensor.matmul(o, w, m, start=(n == 0), stop=(n == len(pairs) - 1))
                return last

            def transposes(src, bank, done):
                for c in range(DC):
                    last = nc.tensor.transpose(bank[:, c * P:(c + 1) * P], src[:, c * P:(c + 1) * P], ident)
                last.then_inc(done, 1)

            def xn_transposes(base):
                for t in range(NT):
                    pe.wait_ge(s_xn, base + t + 1)
                    if base + t >= 2:
                        pe.wait_ge(s_xnT, base + t - 1)
                    transposes(xn[:, t, 0:D], PS[t % 2], s_xnTp)

            def tok(t):
                return slice(t * P, (t + 1) * P)

            def half(b):
                return slice(b * S, (b + 1) * S)

            pe.wait_ge(s_const, 16)
            xn_transposes(0)
            pe.wait_ge(s_wqkg, 32)
            pe.wait_ge(s_xnT, NT)
            for k, done in ((1, s_kp), (0, s_qp)):
                for b in range(B):
                    last = product(PS[(4, 2)[k] + b][:, :],
                                   [(wqk[:, c, k * H0:(k + 1) * H0], xnT[:, c, half(b)]) for c in range(DC)])
                last.then_inc(done, 1)
            for t in range(NT):
                last = product(PS[6][:, t * E:(t + 1) * E], [(xnT[:, c, tok(t)], wg[:, c, :]) for c in range(DC)])
            last.then_inc(s_lgp, 1)
            pe.wait_ge(s_wv, 16)
            for t in range(NT):
                if t >= 3:
                    pe.wait_ge(s_v, t - 2)
                product(PS[(0, 1, 7)[t % 3]][:, 0:D], [(xnT[:, c, tok(t)], wv[:, c, :]) for c in range(DC)])\
                    .then_inc(s_vp, 1)
            pe.wait_ge(s_kq, 1)
            pe.wait_ge(s_v, NT)
            for k in range(2):
                for t in range(4):
                    last = nc.tensor.transpose(PS[k][:, tok(t)], qpos[:, tok(4 * k + t)], ident)
                last.then_inc(s_qmp, 1)
            pe.wait_ge(s_gate, 1)
            for k in range(2):
                for t in range(4):
                    last = nc.tensor.transpose(PS[6 + k][0:E, tok(t)], skey[:, 4 * k + t, :], ident)
                last.then_inc(s_skTp, 1)

            def shared_up(i):
                rows, c0 = SROWS[i // B], P * (i // B)
                if i >= 2:
                    pe.wait_ge(s_hs, i - 1)
                for k in range(2):
                    last = product(PS[2 + 2 * (i % 2) + k][0:rows, :],
                                   [(wsh13[:, c, k * SHARED + c0:k * SHARED + c0 + rows], xnT[:, c, half(i % B)])
                                    for c in range(DC)])
                last.then_inc(s_shp, 1)

            pe.wait_ge(s_wsh, 48)
            shared_up(0)
            shared_up(1)
            pe.wait_ge(s_slots, 1)
            pe.wait_ge(s_skT, 2)
            nc.tensor.transpose(PS[6][:, 0:E], slots, ident[0:E, 0:E]).then_inc(s_slotsTp, 1)
            for i in range(2, NPAIR):
                shared_up(i)

            def tokens_T(u, gathered):
                pe.wait_ge(s_xe[u % SLOTS], gathered)
                transposes(xe[:, u % SLOTS, 0:D], PS[u % 2], s_xeTp)

            def up(e, u, loaded):
                pe.wait_ge(s_wm[u % SLOTS], loaded)
                pe.wait_ge(s_xeT, e + 1)
                product(PS[2 + u % 2][:, 0:2 * INTER],
                        [(xeT[:, u % 2, c, :], w13r[u % SLOTS][:, c, :]) for c in range(DC)]).then_inc(s_hp, 1)

            def hidden_T(e, u):
                pe.wait_ge(s_hm, e + 1)
                for c in range(2):
                    last = nc.tensor.transpose(PS[4 + u % 2][0:IC, c * P:(c + 1) * P],
                                               hm[:, u % 2, c * IC:(c + 1) * IC], ident)
                last.then_inc(s_hTp, 1)

            def down(e, u):
                pe.wait_ge(s_hT, e + 1)
                product(PS[6 + u % 2][:, 0:D], [(heT[:, u % 2, c, :], w2r[u % SLOTS][:, c, :]) for c in range(2)])\
                    .then_inc(s_yp, 1)

            pe.wait_ge(s_hs, NPAIR)
            pe.wait_ge(s_qm, 2)
            pe.wait_ge(s_sidx, 1)
            tokens_T(0, 16)
            up(0, 0, 32)
            with pe.Fori(0, E // SLOTS - 1) as g:
                for u in range(SLOTS):
                    tokens_T(u + 1, g * 16 + 16 * (1 + (u + 1) // SLOTS))
                    hidden_T(g * SLOTS + u, u)
                    up(g * SLOTS + (u + 1), u + 1, g * 32 + 32 * (1 + (u + 1) // SLOTS))
                    down(g * SLOTS + u, u)
            for e in range(E - SLOTS, E):
                if e + 1 < E:
                    tokens_T(e + 1, 16 * (1 + (e + 1) // SLOTS))
                hidden_T(e, e)
                if e + 1 < E:
                    up(e + 1, e + 1, 32 * (1 + (e + 1) // SLOTS))
                down(e, e)

            pe.wait_ge(s_abs, 1)
            pe.wait_ge(s_fill, 4)
            pe.wait_ge(s_hT, E)
            nc.tensor.matmul(PS[5][:, 0:2], ones[:, :], tsum[:, 0:2], start=True, stop=True).then_inc(s_absp, 1)

            def logits(n):
                b, g = divmod(n, HG)
                if n % HG == 0:
                    pe.wait_ge(s_qxl[b], 16 * 2 * PARTS * PARTS)
                if n >= 4:
                    pe.wait_ge(s_ex, n - 3)
                nc.tensor.matmul(PS[n % 4][:, :], sk[:, b, g, :], qx[:, g, :], start=True, stop=True).then_inc(s_lp, 1)

            def weighted(g):
                b = g // 8
                if g % 8 == 0:
                    pe.wait_ge(s_vpr, b + 1)
                if g >= 2:
                    pe.wait_ge(s_avT, g - 1)
                pe.wait_ge(s_ex, 4 * g + 4)
                for c in range(4):
                    n = 4 * g + c
                    last = nc.tensor.matmul(PS[4 + g % 2][32 * c:32 * c + 32, :], vp[:, b, n % HG, :], ex[:, n % 8, :],
                                            start=True, stop=True, skip_group_check=True)
                last.then_inc(s_av, 1)

            def to_natural(g):
                pe.wait_ge(s_avT, g + 1)
                if g >= 2:
                    pe.wait_ge(s_nat, g - 1)
                for t in range(TPB):
                    last = nc.tensor.transpose(PS[6 + g % 2][:, tok(t)], avT[:, g % 2, tok(t)], ident)
                last.then_inc(s_natp, 1)

            pe.wait_ge(s_skl, 16 * PARTS * 2 * Q4 * B)
            pe.wait_ge(s_y, E)
            pe.wait_ge(s_tern, 1)
            for c in range(4):
                logits(c)
            for g in range(NG):
                if g + 1 < NG:
                    for c in range(4):
                        logits(4 * (g + 1) + c)
                weighted(g)
                if g >= 1:
                    to_natural(g - 1)
            to_natural(NG - 1)

            for t in range(NT):
                if t % TPB == 0:
                    pe.wait_ge(s_on, t // TPB + 1)
                if t == 0:
                    pe.wait_ge(s_ex, 4 * NG)
                if t >= 2:
                    pe.wait_ge(s_oT, t - 1)
                transposes(onat[:, t, :], PS[t % 2], s_oTp)
            pe.wait_ge(s_wo0, 16)
            for t in range(NT):
                pe.wait_ge(s_oT, t + 1)
                if t >= 2:
                    pe.wait_ge(s_x1, t - 1)
                product(PS[2 + t % 2][:, 0:D],
                        [(oT[:, c, tok(t)], wo0[:, c, :]) for c in range(DC)] +
                        [(hs[0:SROWS[c], c, tok(t)], wsh2[0:SROWS[c], c, :]) for c in range(3)]).then_inc(s_x1p, 1)

            xn_transposes(NT)
            pe.wait_ge(s_xnT, 2 * NT)
            pe.wait_ge(s_nat, NG)
            for i in range(2 * FC):
                if i >= 6:
                    pe.wait_ge(s_relu, i - 5)
                product(PS[2 + i % 6][:, :],
                        [(w_fc1[:, c, (i // 2) * P:(i // 2 + 1) * P], xnT[:, c, half(i % 2)]) for c in range(DC)])\
                    .then_inc(s_ffp, 1)

            def mixed(k, c, cols):
                return mix[:, k % 2, c * N + cols.start:c * N + cols.stop]

            def project_T(k, w, bank_free, done):
                for i in range(4):
                    f, n = divmod(i, 2)
                    bank_free(i)
                    product(PS[i][:, :], [(w5[:, w, c, f * P:(f + 1) * P], mixed(k, c, half(n))) for c in range(DC)])\
                        .then_inc(done, 1)

            def project(k, w, bank, bank_free, done):
                for t in range(NT):
                    bank_free(t)
                    product(PS[bank + t % 4][:, 0:D], [(mixed(k, c, tok(t)), w5[:, w, c, :]) for c in range(DC)])\
                        .then_inc(done, 1)

            pe.wait_ge(s_w5, 16)
            pe.wait_ge(s_relu, 2 * FC)
            pe.wait_ge(s_mix, 1)
            project_T(0, 1, lambda i: None, s_kTp)
            project(0, 1, 4, lambda t: pe.wait_ge(s_kn, t - 3) if t >= 4 else None, s_knp)
            pe.wait_ge(s_sq, 2 * FC)
            for t in range(NT):
                pe.wait_ge(s_kn, min(t + 5, NT))
                if t >= 4:
                    pe.wait_ge(s_x2, t - 3)
                product(PS[4 + t % 4][:, 0:D], [(hf[:, c, tok(t)], w_pj1[:, c, :]) for c in range(FC)]).then_inc(s_ffd, 1)
            pe.wait_ge(s_mix, 2)
            project_T(1, 0, lambda i: pe.wait_ge(s_kT, i + 1), s_rTp)

            def v_bank(t):
                pe.wait_ge(s_x2, min(t + 5, NT))
                if t >= 4:
                    pe.wait_ge(s_v1, t - 3)

            pe.wait_ge(s_mix, 3)
            project(2, 2, 4, v_bank, s_v1p)

            def g_bank(t):
                if t < 4:
                    pe.wait_ge(s_rq, t + 1)
                    pe.wait_ge(s_rw, t + 1)
                else:
                    pe.wait_ge(s_g, t - 3)

            pe.wait_ge(s_mix, 4)
            project(3, 3, 0, g_bank, s_gp)

            def scores(u):
                t, f = divmod(u, 2)
                for q in range(4):
                    a = 4 * u + q
                    if a >= 4:
                        pe.wait_ge(s_a1, a - 3)
                    nc.tensor.matmul(PS[q][:, :], kq[:, f, q, tok(t)], rq[:, f, :, tok(t)], start=True, stop=True)\
                      .then_inc(s_a1p, 1)

            def outputs(u):
                t, f = divmod(u, 2)
                b, g = divmod(t, TPB)
                y = PS[4 + u % 2]
                if u >= 2:
                    pe.wait_ge(s_yT, u - 1)
                pe.wait_ge(s_st, 7 * b + max(1, 2 * g + f))
                nc.tensor.matmul(y[:, 0:P], state[:, f, :], rw[:, f, tok(t)], start=True, stop=False,
                                 skip_group_check=True)
                pe.wait_ge(s_a1, 4 * u + 4)
                pe.wait_ge(s_vd, t + 2)
                for h in range(4):
                    for q in range(4):
                        last = nc.tensor.matmul(y[32 * q:32 * q + 32, 0:P], vpr[:, t % 2, 4 * f + q, 32 * h:32 * h + 32],
                                                aring[:, (4 * u + q) % 8, h * P:(h + 1) * P], start=False,
                                                stop=(h == 3), skip_group_check=True)
                last.then_inc(s_yTp, 1)

            def state_product(u):
                t, f = divmod(u, 2)
                b, g = divmod(t, TPB)
                if g < TPB - 1:
                    n = 6 * b + 2 * g + f
                    if n:
                        pe.wait_ge(s_st, n + b + (1 if n % 6 else 0))
                    nc.tensor.matmul(PS[6][:, 0:P], kn[:, t, f * P:(f + 1) * P], vn[:, t, f * P:(f + 1) * P],
                                     start=True, stop=True).then_inc(s_kvp, 1)

            def y_natural(t):
                pe.wait_ge(s_yT, 2 * t + 2)
                if t >= 1:
                    pe.wait_ge(s_yn, t)
                for f in range(2):
                    last = nc.tensor.transpose(PS[7][:, f * P:(f + 1) * P], yTs[:, f, 0:P], ident)
                last.then_inc(s_ynp, 1)

            pe.wait_ge(s_g, NT)
            pe.wait_ge(s_v1, NT)
            scores(0)
            for u in range(UNITS):
                if u + 1 < UNITS:
                    scores(u + 1)
                outputs(u)
                state_product(u)
                if u >= 2 and u % 2 == 0:
                    y_natural(u // 2 - 1)
            y_natural(NT - 1)

            for t in range(NT):
                pe.wait_ge(s_z, t + 1)
                if t == 0:
                    pe.wait_ge(s_a1, 4 * UNITS)
                if t >= 2:
                    pe.wait_ge(s_zT, t - 1)
                transposes(xn[:, t, 0:D], PS[t % 2], s_zTp)
                if t >= 1:
                    final(t - 1) if False else None
            for t in range(NT):
                pe.wait_ge(s_zT, t + 1)
                if t == 0:
                    pe.wait_ge(s_yT, UNITS)
                    pe.wait_ge(s_st, 14)
                    pe.wait_ge(s_yn, NT)
                if t >= 4:
                    pe.wait_ge(s_o, t - 3)
                product(PS[4 + t % 4][:, 0:D], [(xnT[:, c, tok(t)], w5[:, 4, c, :]) for c in range(DC)]).then_inc(s_op, 1)


def kernel(**inputs):
    import concourse.bacc as bacc
    from concourse.bass_utils import run_bass_kernel_spmd

    a = {k: np.asarray(v) for k, v in inputs.items()}

    def chunks(w):
        c = w.shape[0] // P
        return np.ascontiguousarray(w.reshape(c, P, w.shape[1]).transpose(1, 0, 2))

    w1, w3 = a["L0_ffn_w1"], a["L0_ffn_w3"]
    w13 = np.concatenate([w1, w3], 1).transpose(0, 2, 1).reshape(E, DC, P, 2 * INTER).transpose(0, 2, 1, 3)
    w2 = a["L0_ffn_w2"].transpose(0, 2, 1).reshape(E, 2, IC, D).transpose(0, 2, 1, 3)
    maa = np.stack([a[f"L1_attn_time_maa_{k}"].reshape(DC, P) for k in "krvg"], 0)
    td = a["L1_attn_time_decay"].reshape(H1)
    arrays = {
        "x": a["L0_attn_x"],
        "consts": constants(),
        "w_qk": chunks(np.concatenate([a["L0_attn_Wq"], a["L0_attn_Wk"]], 0).T),
        "w_v": chunks(a["L0_attn_Wv"].T),
        "w_gate": chunks(a["L0_ffn_gate_w"].T),
        "w_sh13": chunks(np.concatenate([a["L0_ffn_sw1"], a["L0_ffn_sw3"]], 0).T),
        "w_sh2": a["L0_ffn_sw2"].T,
        "w_o0": chunks(a["L0_attn_Wo"].T),
        "w_13": w13,
        "w_2": w2,
        "maa": maa.transpose(2, 0, 1).reshape(P, 8),
        "td_row": td,
        "td_col": np.repeat(td, HN).reshape(2, P).T,
        "u_row": a["L1_attn_time_faaaa"].reshape(H1),
        "w_rkvgo": np.stack([chunks(a[f"L1_attn_W{k}"].T) for k in "rkvgo"], 1),
        "gamma": a["L1_attn_gamma"],
        "beta": a["L1_attn_beta"],
        "w_fc": chunks(a["L1_ffn_w_fc"].T),
        "w_pj": chunks(a["L1_ffn_w_proj"].T),
    }
    nc = bacc.Bacc("TRN2", target_bir_lowering=False, num_devices=1)
    arrays = {f"in_{k}": np.ascontiguousarray(v) for k, v in arrays.items()}
    args = [nc.dram_tensor(k, v.shape, mybir.dt.from_np(v.dtype), kind="ExternalInput").ap() for k, v in arrays.items()]
    out = nc.dram_tensor("out", (B, S, D), F32, kind="ExternalOutput").ap()
    block_kernel(nc, *args, out)
    r = run_bass_kernel_spmd(nc, [arrays], core_ids=[0])
    return r.results[0]["out"]
```

```python
import numpy as np
import concourse.bass as bass
from concourse import mybir
from contextlib import ExitStack

F32 = mybir.dt.float32
BF16 = mybir.dt.bfloat16
I32 = mybir.dt.int32
U32 = mybir.dt.uint32
ALU = mybir.AluOpType
ACT = mybir.ActivationFunctionType
AX = mybir.AxisListType.X

P = 128
B, S, D = 2, 512, 256
N = B * S
NT = N // P
TPB = NT // B
DC = D // P
LN_EPS = 1e-5

H0, TOPK, DV = 128, 32, 2
Q4 = P // TOPK
HG = H0 // Q4
PARTS = 3
ROWS = PARTS * PARTS * 2 * Q4
COLS = 1 + 2 * DV

E, INTER, KSEL, CAP = 64, 176, 6, 128
SHARED = 2 * INTER
IC = INTER // 2
SROWS = [128, 128, SHARED - 256]
TAB = D + E
PAD = N + CAP

H1, HN = 32, 8
HH = P // HN
GN_EPS = 1e-5 * 144
FF = 640
FC = FF // P

CONST = {}
for _name, _n in (("ident", P), ("pdist", P), ("steps", P), ("heads", P), ("tokinv", NT), ("vrow", 4), ("slot", 1),
                  ("jdec", 1), ("quad", 4)):
    CONST[_name] = (sum(n for _, n in CONST.values()), _n)
NCONST = sum(n for _, n in CONST.values())


def constants():
    p = np.arange(P)[:, None]
    i = np.arange(P)[None, :]
    cols = {
        "ident": p == i,
        "pdist": np.maximum(i - p - 1, 0),
        "steps": i + 0 * p,
        "heads": p // HN == i // HN,
        "tokinv": N - (p + P * np.arange(NT)[None, :]),
        "vrow": H0 * np.array([[S - 1, 0, S + S - 1, S]]) + p,
        "slot": p,
        "jdec": P - 1 - p,
        "quad": (p % 32) // HN == np.arange(4)[None, :],
    }
    return np.concatenate([np.broadcast_to(cols[k], (P, n)) for k, (_, n) in CONST.items()], 1).astype(np.float32)


def block_kernel(nc, x, consts, w_qk, w_v, w_gate, w_sh13, w_sh2, w_o0, w_13, w_2, maa, td_row, td_col, u_row,
                 w_rkvgo, gamma, beta, w_fc, w_pj, out):
    x_v = x.rearrange("b (t p) d -> p (b t) d", p=P)
    out_v = out.rearrange("b (t p) d -> p (b t) d", p=P)

    tok_tab = nc.dram_tensor("tok_tab", (PAD, TAB), F32, kind="Internal").ap()
    val_tab = nc.dram_tensor("val_tab", (N * H0, DV), F32, kind="Internal").ap()
    q_dram = nc.dram_tensor("q_dram", (PARTS, B, 8, 2 * Q4, 4, S), BF16, kind="Internal").ap()
    k_dram = nc.dram_tensor("k_dram", (PARTS, H0, B, 2, TOPK), BF16, kind="Internal").ap()
    routed = [nc.dram_tensor(f"routed{i}", (PAD, D), F32, kind="Internal").ap() for i in range(2)]

    ctx = ExitStack()
    with ctx:
        def sb(name, shape, dt=F32):
            return ctx.enter_context(nc.sbuf_tensor(name, shape, dt))

        def sem(name):
            return ctx.enter_context(nc.semaphore(name))

        xs = sb("xs", [P, NT, D])
        xn = sb("xn", [P, NT, TAB])
        xnT = sb("xnT", [P, DC, N])
        cst = sb("cst", [P, NCONST])
        ones = sb("ones", [P, P])
        gb = sb("gb", [P, 2, D])
        wb = sb("wb", [P, 2, P])
        stats = sb("stats", [P, NT, 6])
        mv = sb("mv", [P, NT, 2])
        rstd = sb("rstd", [P, 2, NT])
        rsm = sb("rsm", [P, 3, NT])
        tsum = sb("tsum", [P, 8])
        gst = sb("gst", [P, 3, TPB * H1])
        nat_tmp = sb("nat_tmp", [P, 2, E])

        def const(name):
            at, n = CONST[name]
            return cst[:, at:at + n]

        ident = const("ident")

        BIGW = 44000
        big = sb("big", [P, BIGW])
        used = [0]

        def carve(words, rows=P, at=None):
            start = used[0] if at is None else at
            if at is None:
                used[0] += words
            assert start + words <= BIGW, (start, words)
            return big[0:rows, start:start + words]

        def v3(ap, a, n):
            return ap.rearrange("p (a n) -> p a n", a=a)

        w_fc1 = v3(carve(DC * FF), DC, FF)
        w_pj1 = v3(carve(FC * D), FC, D)
        early = used[0]
        wqk = v3(carve(DC * 256), DC, 256)
        wv = v3(carve(DC * D), DC, D)
        wg = v3(carve(DC * E), DC, E)
        wsh13 = v3(carve(DC * 2 * SHARED), DC, 2 * SHARED)
        wsh2 = v3(carve(3 * D), 3, D)
        wo0 = v3(carve(DC * D), DC, D)
        qparts_at = used[0]
        qparts = carve(2 * PARTS * N // 2).bitcast(BF16).rearrange("p (s a n) -> p s a n", s=2, a=PARTS)
        oT = v3(carve(DC * N, at=qparts_at), DC, N)
        keys_at = used[0]
        keys = carve(B * 2 * S).rearrange("p (b s n) -> p b s n", b=B, s=2)
        onat = v3(carve(NT * D, at=keys_at), NT, D)
        topv = carve(B * 2 * TOPK).rearrange("p (b s n) -> p b s n", b=B, s=2)
        topi = carve(B * 2 * TOPK).bitcast(U32).rearrange("p (b s n) -> p b s n", b=B, s=2)
        dkf = carve(B * 2 * TOPK)
        dkparts = v3(carve(PARTS * 64).bitcast(BF16), PARTS, B * 2 * TOPK)
        vidx = carve(B * 2 * TOPK).bitcast(I32).rearrange("p (b s n) -> p b s n", b=B, s=2)
        vidxT = carve(B * 2 * HG).bitcast(I32)
        vals = carve(B * 2 * HG * DV).rearrange("p (k s g d) -> p k s g d", k=B * 8, s=2, g=4)
        vps = carve(4 * 32).rearrange("p (g c) -> p g c", g=4)
        qx = v3(carve(4 * S // 2, ROWS).bitcast(BF16), 4, S)
        rt_at = used[0]
        sc = v3(carve(NT * (E + 2)), NT, E + 2)
        sr = v3(carve(NT * (E + 2)), NT, E + 2)
        skey = v3(carve(NT * E), NT, E)
        lg = v3(carve(NT * E), NT, E)
        sk_at = used[0]
        sk = carve(B * HG * P // 2, ROWS).bitcast(BF16).rearrange("p (g n) -> p g n", g=B * HG)
        sk_all = carve(B * HG * P // 2, at=sk_at)
        racc = [v3(carve(NT * D, at=sk_at + i * NT * D), NT, D) for i in range(2)]
        ex_at = used[0]
        ex = v3(carve(4 * S), 4, S)
        avT = carve(S)
        sg = v3(carve(2 * S, at=ex_at), 2, S)
        sh1 = v3(carve(2 * S, at=ex_at + 2 * S), 2, S)
        W13 = DC * 2 * INTER
        ring_at = used[0]
        carve(4 * (W13 + 2 * D))
        w13r = [v3(carve(W13, at=ring_at + r * (W13 + 2 * D)), DC, 2 * INTER) for r in range(4)]
        w2r = [v3(carve(2 * D, IC, at=ring_at + r * (W13 + 2 * D) + W13), 2, D) for r in range(4)]
        q32 = v3(carve(2 * N, at=ring_at), 2, N)
        qrest = v3(carve(2 * N, at=ring_at + 2 * N), 2, N)
        nat_at = used[0]
        nat = carve(TPB * 8 * P).rearrange("p (t g m) -> p t g m", t=TPB, g=8)
        vnat = v3(carve(NT * D, at=nat_at), NT, D)
        slotk = carve(N, E, at=nat_at + NT * D)
        slots = carve(CAP, E, at=nat_at + NT * D + N)
        qmask = v3(carve(NT * H0), NT, H0)
        hs = v3(carve(3 * N), 3, N)
        sidx = carve(E).bitcast(I32)
        rt8 = v3(carve(NT * 8), NT, 8)
        zero = carve(TAB)
        tern_t = carve(160)
        carve(max(0, 2560 + 35328 - used[0]))
        moe_at = used[0]
        xe = v3(carve(4 * TAB), 4, TAB)
        xeT = carve(2 * D).rearrange("p (r c n) -> p r c n", r=2, c=DC)
        th = v3(carve(2 * INTER), 2, INTER)
        ge = v3(carve(2 * INTER), 2, INTER)
        hm = v3(carve(2 * INTER), 2, INTER)
        heT = carve(2 * 2 * P, IC).rearrange("p (r c n) -> p r c n", r=2, c=2)
        ye = v3(carve(2 * D), 2, D)
        den_at = used[0]
        den = carve(3 * TPB * H0).rearrange("p (k t h) -> p k t h", k=3, t=TPB)

        w5 = carve(5 * DC * D, at=moe_at).rearrange("p (k c n) -> p k c n", k=5, c=DC)
        used[0] = moe_at + 5 * DC * D
        yTs = v3(carve(2 * P), 2, P)
        state = v3(carve(2 * P), 2, P)
        kvt = carve(P)
        edrow = carve(H1)
        edcol = carve(2)
        urow = carve(H1)
        wall = carve(2)
        maat = carve(8)
        kdec = carve(H1)
        assert used[0] <= den_at
        gnt = carve(TPB * D, at=den_at)
        used[0] = early
        mix_at = used[0]
        mix = v3(carve(2 * DC * N), 2, DC * N)
        aring = v3(carve(8 * S, at=mix_at), 8, S)
        vpr_at = used[0]
        vpr = carve(2 * 8 * 160).rearrange("p (r g c) -> p r g c", r=2, g=8)
        dif = v3(carve(DC * N, at=vpr_at), DC, N)
        kq = carve(2 * 4 * N).rearrange("p (f q n) -> p f q n", f=2, q=4)
        rq_at = used[0]
        rq = carve(2 * 4 * N).rearrange("p (f h n) -> p f h n", f=2, h=4)
        hf = v3(carve(FC * N, at=rq_at), FC, N)
        rw = v3(carve(2 * N), 2, N)
        kn = v3(carve(NT * D), NT, D)
        vn = v3(carve(NT * D), NT, D)
        gn = v3(carve(NT * D), NT, D)
        wmask = carve(H1 * P).rearrange("p (h n) -> p h n", h=H1)
        assert used[0] <= moe_at, (used[0], moe_at)

        PS = [ctx.enter_context(nc.psum_tensor(f"ps{i}", [P, 512], F32)) for i in range(8)]

        s_x = [sem(f"x_loaded{i}") for i in range(B)]
        s_const = sem("const_loaded")
        s_wqkg = sem("wqkg_loaded")
        s_wv = sem("wv_loaded")
        s_wsh = sem("wshared_loaded")
        s_wo0 = sem("wo0_loaded")
        s_fill = sem("fills_done")
        s_var = sem("variance_ready")
        s_rstd = sem("rstd_ready")
        s_xn = sem("xn_ready")
        s_xnTp = sem("xnT_in_psum")
        s_xnT = sem("xnT_copied")
        s_kp = sem("k_in_psum")
        s_qp = sem("q_in_psum")
        s_lgp = sem("logits_in_psum")
        s_vp = sem("v_in_psum")
        s_v = sem("v_copied")
        s_keys = sem("keys_copied")
        s_q32 = sem("q_halves_copied")
        s_qp0 = sem("q_parts_first")
        s_qr = sem("q_rest")
        s_shc = sem("shared_banks_copied")
        s_shg = sem("shared_silu_done")
        s_lgs = sem("logits_shifted")
        s_lge = sem("logits_exp")
        s_gate = sem("gates_ready")
        s_skTp = sem("slotkeys_in_psum")
        s_skT = sem("slotkeys_copied")
        s_slots = sem("slots_ready")
        s_slotsTp = sem("slotsT_in_psum")
        s_sidx = sem("slot_tokens_ready")
        s_dk = sem("dk_parts_ready")
        s_vidx = sem("value_rows_ready")
        s_qpart = sem("q_parts_ready")
        s_qmp = sem("qT_in_psum")
        s_qm = sem("qmask_ready")
        s_shp = sem("shared_in_psum")
        s_sht = sem("shared_tanh")
        s_hs = sem("shared_hidden_ready")
        s_tab = sem("token_table_stored")
        s_vtab = sem("value_table_stored")
        s_kst = sem("dk_stored")
        s_skl = sem("sk_loaded")
        s_qst = sem("q_stored")
        s_qxl = sem("qx_loaded")
        s_vg = sem("values_gathered")
        s_xe = [sem(f"xe_gathered{i}") for i in range(4)]
        s_wm = [sem(f"expert_weights{i}") for i in range(4)]
        s_xeTp = sem("xeT_in_psum")
        s_xeT = sem("xeT_copied")
        s_hp = sem("h_in_psum")
        s_th = sem("tanh_done")
        s_ge = sem("silu_done")
        s_hm = sem("hidden_done")
        s_hTp = sem("hT_in_psum")
        s_hT = sem("hT_copied")
        s_yp = sem("y_in_psum")
        s_y = sem("y_scaled")
        s_sc = [sem(f"routed_added{i}") for i in range(2)]
        s_vpr = sem("values_placed")
        s_lp = sem("attn_logits_in_psum")
        s_ex = sem("attn_exp_done")
        s_av = sem("attn_out_in_psum")
        s_avT = sem("attn_out_copied")
        s_natp = sem("attn_nat_in_psum")
        s_nat = sem("attn_nat_copied")
        s_on = sem("attn_norm_done")
        s_oTp = sem("oT_in_psum")
        s_oT = sem("oT_copied")
        s_racc = sem("routed_loaded")
        s_res = sem("routed_summed")
        s_x1p = sem("x1_in_psum")
        s_x1 = sem("x1_ready")
        s_wff = sem("ff_weights_loaded")
        s_w5 = sem("w5_loaded")
        s_l1c = sem("block1_rows_loaded")
        s_gb = sem("gamma_beta_loaded")
        s_abs = sem("weight_abs_summed")
        s_absp = sem("weight_abs_in_psum")
        s_tern = sem("ternary_steps")
        s_tsum = sem("thresholds_ready")
        s_ed = sem("decay_exp")
        s_edn = sem("decay_negated")
        s_wm1 = sem("decay_tables_exp")
        s_wmc = sem("decay_mask_causal")
        s_ffp = sem("ff_in_psum")
        s_relu = sem("ff_relu_done")
        s_sq = sem("ff_square_done")
        s_mix = sem("mix_ready")
        s_kTp = sem("k1T_in_psum")
        s_kT = sem("k1T_copied")
        s_knp = sem("k1_nat_in_psum")
        s_kn = sem("k1_nat_scaled")
        s_ffd = sem("ff_down_in_psum")
        s_x2 = sem("x2_ready")
        s_rTp = sem("r1T_in_psum")
        s_rq = sem("r1_masked")
        s_rw = sem("r1_decayed")
        s_v1p = sem("v1_in_psum")
        s_v1 = sem("v1_copied")
        s_gp = sem("g1_in_psum")
        s_gt = sem("g1_tanh")
        s_g = sem("g1_ready")
        s_a1p = sem("scores_in_psum")
        s_a1 = sem("scores_masked")
        s_vd = sem("v1_placed")
        s_yTp = sem("yT_in_psum")
        s_yT = sem("yT_copied")
        s_kvp = sem("kv_in_psum")
        s_st = sem("state_ready")
        s_ynp = sem("y_nat_in_psum")
        s_yn = sem("y_nat_copied")
        s_gv = sem("group_var_ready")
        s_gs = sem("group_std_ready")
        s_z = sem("z_ready")
        s_zTp = sem("zT_in_psum")
        s_zT = sem("zT_copied")
        s_op = sem("out_in_psum")
        s_o = sem("out_ready")
        s_out = sem("out_stored")
        s_dve = sem("vector_chain")

        NPAIR = 3 * B
        NG = B * 8
        SLOTS = 4
        UNITS = B * TPB * 2

        block = ctx.enter_context(nc.Block())

        @block.sync
        def _(sp):
            for b in range(B):
                sp.dma_start(xs[:, b * TPB:(b + 1) * TPB, :], x_v[:, b * TPB:(b + 1) * TPB, :]).then_inc(s_x[b], 16)
            sp.dma_start(cst[:, :], consts).then_inc(s_const, 16)
            sp.dma_start(wqk, w_qk).then_inc(s_wqkg, 16)
            sp.dma_start(wg, w_gate).then_inc(s_wqkg, 16)
            sp.dma_start(wv, w_v).then_inc(s_wv, 16)
            sp.dma_start(wsh13, w_sh13).then_inc(s_wsh, 16)
            sp.dma_start(wsh2[:, 0:2, :], w_sh2[0:256, :].rearrange("(c p) n -> p c n", p=P)).then_inc(s_wsh, 16)
            sp.dma_start(wsh2[0:SROWS[2], 2, :], w_sh2[256:SHARED, :]).then_inc(s_wsh, 16)
            sp.dma_start(wo0, w_o0).then_inc(s_wo0, 16)
            sp.dma_start(w_fc1, w_fc).then_inc(s_wff, 16)
            sp.dma_start(w_pj1, w_pj).then_inc(s_wff, 16)
            sp.wait_ge(s_fill, 1)
            sp.dma_start(tok_tab[N:PAD, :], zero).then_inc(s_tab, 16)
            sp.wait_ge(s_v, NT)
            sp.dma_start(val_tab.rearrange("(t p h) d -> p t (h d)", p=P, h=H0), vnat).then_inc(s_vtab, 16)
            sp.wait_ge(s_qpart, 2)
            for side in range(2):
                for a in range(PARTS):
                    for b in range(B):
                        for h4 in range(Q4):
                            sp.dma_start(q_dram[a, b, :, side * Q4 + h4, :, :],
                                         qparts[HG * h4:HG * (h4 + 1), side, a, b * S:(b + 1) * S])\
                              .then_inc(s_qst, 16)

            def weights(u, group):
                sp.dma_start(w13r[u].rearrange("p c n -> p (c n)").unsqueeze(1), w13_v[u, :, group, :])\
                  .then_inc(s_wm[u], 16)
                sp.dma_start(w2r[u].rearrange("p c n -> p (c n)").unsqueeze(1), w2_v[u, :, group, :])\
                  .then_inc(s_wm[u], 16)

            w13_v = w_13.rearrange("(g u) p c n -> u p g (c n)", u=SLOTS)
            w2_v = w_2.rearrange("(g u) p c n -> u p g (c n)", u=SLOTS)
            for u in range(SLOTS):
                weights(u, slice(0, 1))
            sp.wait_ge(s_dk, 1)
            sp.dma_start(k_dram.rearrange("a h b s j -> h a (b s j)"), dkparts).then_inc(s_kst, 16)
            sp.wait_ge(s_kst, 16)
            sp.wait_ge(s_fill, 2)
            for a in range(PARTS):
                for side in range(2):
                    for h4 in range(Q4):
                        first = a * 24 + side * Q4 + h4
                        for b in range(B):
                            sp.dma_start(sk[first:first + 17:8, b * HG:(b + 1) * HG, TOPK * h4:TOPK * (h4 + 1)],
                                         k_dram[:, HG * h4:HG * (h4 + 1), b, side, :]).then_inc(s_skl, 16)
            sp.wait_ge(s_gate, 1)
            sp.dma_start(tok_tab[0:N, :].rearrange("(t p) d -> p t d", p=P), xn[:, :, :]).then_inc(s_tab, 16)
            q_v = q_dram.rearrange("a b g r c n -> a r (b g) (c n)")

            def q_rows(group):
                for a in range(PARTS):
                    src = q_v[a, :, group, :]
                    for ap in range(PARTS):
                        first = (a * PARTS + ap) * 2 * Q4
                        sp.dma_start(qx[first:first + 2 * Q4, :, :].rearrange("r c n -> r (c n)").unsqueeze(1), src)\
                          .then_inc(s_qxl, 16)

            sp.wait_ge(s_qst, 16 * 2 * PARTS * B * Q4)
            q_rows(slice(0, 1))
            with sp.Fori(1, E // SLOTS) as g:
                for u in range(SLOTS):
                    sp.wait_ge(s_yp, g * SLOTS + (u - SLOTS + 1))
                    weights(u, bass.ds(g, 1))
                    if u == 1:
                        sp.wait_ge(s_lp, g * 4)
                        q_rows(bass.ds(g, 1))
            sp.wait_ge(s_y, E)
            sp.dma_start(w5, w_rkvgo).then_inc(s_w5, 16)
            sp.dma_start(edrow, td_row.partition_broadcast(P)).then_inc(s_l1c, 16)
            sp.dma_start(urow, u_row.partition_broadcast(P)).then_inc(s_l1c, 16)
            sp.dma_start(edcol, td_col).then_inc(s_l1c, 16)
            sp.dma_start(maat, maa).then_inc(s_l1c, 16)
            sp.dma_start(gb[:, 0, :], gamma.partition_broadcast(P)).then_inc(s_gb, 16)
            sp.dma_start(gb[:, 1, :], beta.partition_broadcast(P)).then_inc(s_gb, 16)
            sp.wait_ge(s_lp, NG * 4)
            for i in range(2):
                sp.wait_ge(s_sc[i], 16 * (1 + E // 2))
                sp.dma_start(racc[i], routed[i][0:N, :].rearrange("(t p) d -> p t d", p=P)).then_inc(s_racc, 16)
            for t in range(NT):
                sp.wait_ge(s_o, t + 1)
                sp.dma_start(out_v[:, t, :], xs[:, t, :]).then_inc(s_out, 16)
            sp.wait_ge(s_out, 16 * NT)

        @block.gpsimd
        def _(pool):
            nc.gpsimd.memset(zero, 0.0).then_inc(s_fill, 1)
            nc.gpsimd.memset(sk_all, 0.0).then_inc(s_fill, 1)
            nc.gpsimd.memset(vps, 0.0).then_inc(s_fill, 1)
            nc.gpsimd.memset(ones[:, :], 1.0)
            nc.gpsimd.memset(rsm[:, 2, :], -0.5).then_inc(s_fill, 1)
            pool.wait_ge(s_fill, 4)
            for h4 in range(Q4):
                last = nc.gpsimd.memset(vps[32 * h4:32 * h4 + 32, :, COLS * h4:COLS * h4 + 1], 1.0)
            last.then_inc(s_fill, 1)
            pool.wait_ge(s_fill, 5)
            for i in range(2):
                nc.gpsimd.dma_start(routed[i].rearrange("(r p) d -> p r d", p=P),
                                    zero[:, 0:D].rearrange("p (a d) -> p a d", a=1).broadcast_to([P, PAD // P, D]))\
                  .then_inc(s_sc[i], 16)

            def rsqrt(n, half):
                t = slice(half * TPB, (half + 1) * TPB)
                pool.wait_ge(s_var, B * n + half + 1)
                nc.gpsimd.tensor_tensor(rstd[:, 1, t], rstd[:, 0, t], rsm[:, 2, t], ALU.pow).then_inc(s_rstd, 1)

            for half in range(B):
                rsqrt(0, half)

            def shared_hidden(i):
                rows = SROWS[i // B]
                h = hs[0:rows, i // B, (i % B) * S:(i % B + 1) * S]
                pool.wait_ge(s_sht, i + 1)
                nc.gpsimd.tensor_tensor(sg[0:rows, i % 2, :], sg[0:rows, i % 2, :], sh1[0:rows, i % 2, :], ALU.mult)\
                  .then_inc(s_shg, 1)
                pool.wait_ge(s_shg, i + 1)
                nc.gpsimd.tensor_tensor(h, h, sg[0:rows, i % 2, :], ALU.mult).then_inc(s_hs, 1)

            pool.wait_ge(s_qp0, 1)
            for side in range(2):
                nc.gpsimd.tensor_tensor(qrest[:, side, :], q32[:, side, :], qparts[:, side, 0, :], ALU.subtract)\
                  .then_inc(s_qr, 1)
            shared_hidden(0)
            shared_hidden(1)
            pool.wait_ge(s_qp0, 2)
            for side in range(2):
                nc.gpsimd.tensor_tensor(qparts[:, side, 2, :], qrest[:, side, :], qparts[:, side, 1, :], ALU.subtract)\
                  .then_inc(s_qpart, 1)
            for i in range(2, NPAIR):
                shared_hidden(i)

            def value_gather(n):
                group, rest = divmod(n, 8)
                side, c = divmod(rest, 4)
                b, g4 = divmod(group, 8)
                col = (2 * b + side) * HG + 4 * g4 + c
                nc.gpsimd.indirect_dma_start(vals[:, group, side, c, :], None, val_tab,
                                             bass.IndirectOffsetOnAxis(ap=vidxT[:, col:col + 1], axis=0))\
                  .then_inc(s_vg, 16)

            def token_gather(e):
                if e >= SLOTS:
                    pool.wait_ge(s_y, e - SLOTS + 1)
                nc.gpsimd.indirect_dma_start(xe[:, e % SLOTS, :], None, tok_tab,
                                             bass.IndirectOffsetOnAxis(ap=sidx[:, e:e + 1], axis=0))\
                  .then_inc(s_xe[e % SLOTS], 16)

            def routed_add(e):
                pool.wait_ge(s_y, e + 1)
                pool.wait_ge(s_sc[e % 2], 16 * (1 + e // 2))
                nc.gpsimd.indirect_dma_start(routed[e % 2], bass.IndirectOffsetOnAxis(ap=sidx[:, e:e + 1], axis=0),
                                             ye[:, e % 2, :], None, compute_op=ALU.add)\
                  .then_inc(s_sc[e % 2], 16)

            NV = B * 2 * HG
            FIRST = 40
            pool.wait_ge(s_vidx, 1)
            pool.wait_ge(s_vtab, 16)
            done = 0
            while done < FIRST:
                value_gather(done)
                done += 1
            pool.wait_ge(s_sidx, 1)
            pool.wait_ge(s_tab, 32)
            for e in range(3):
                token_gather(e)
            for e in range(E):
                if e + 3 < E:
                    token_gather(e + 3)
                for _ in range(2 if e % 2 else 1):
                    if done < NV:
                        value_gather(done)
                        done += 1
                routed_add(e)
            assert done == NV
            for half in range(B):
                rsqrt(1, half)
            pool.wait_ge(s_wm1, 1)
            nc.gpsimd.affine_select(out=wmask, in_=wmask, compare_op=ALU.is_ge, fill=0.0, base=-1,
                                    pattern=[[0, H1], [1, P]], channel_multiplier=-1).then_inc(s_wmc, 1)
            pool.wait_ge(s_xn, NT + 1)
            nc.gpsimd.memset(kq, 0.0).then_inc(s_wmc, 1)
            pool.wait_ge(s_mix, 4)
            pool.wait_ge(s_v1, NT)
            nc.gpsimd.memset(vpr, 0.0).then_inc(s_vd, 1)
            pool.wait_ge(s_vd, 1)
            for t in range(NT):
                if t >= 2:
                    pool.wait_ge(s_yTp, 2 * (t - 1))
                dst = vpr[:, t % 2, :, :].rearrange("p g (a c) -> p g a c", a=4)[:, :, :, 0:HN]
                nc.gpsimd.tensor_copy(dst, vn[:, t, :].rearrange("p (g a c) -> p g a c", g=8, a=4)).then_inc(s_vd, 1)

        @block.scalar
        def _(act):
            def xnT_copies(base):
                for t in range(NT):
                    act.wait_ge(s_xnTp, base + t + 1)
                    nc.scalar.activation(xnT[:, :, t * P:(t + 1) * P],
                                         PS[t % 2][:, 0:D].rearrange("p (c n) -> p c n", c=DC), ACT.Copy)\
                      .then_inc(s_xnT, 1)

            xnT_copies(0)
            act.wait_ge(s_kp, 1)
            for b in range(B):
                nc.scalar.activation(keys[:, b, 0, :], PS[2 + b][:, ::-1], ACT.Copy)
                nc.scalar.activation(keys[:, b, 1, :], PS[2 + b][:, :], ACT.Copy, scale=-1.0).then_inc(s_keys, 1)
            act.wait_ge(s_qp, 1)
            for b in range(B):
                for side in range(2):
                    last = nc.scalar.activation(q32[:, side, b * S:(b + 1) * S], PS[4 + b][:, :], ACT.Relu,
                                                scale=1.0 - 2.0 * side)
                last.then_inc(s_q32, 1)
            act.wait_ge(s_q32, B)
            nc.scalar.activation(qparts[:, :, 0, :], q32, ACT.Copy).then_inc(s_qp0, 1)
            for t in range(NT):
                act.wait_ge(s_vp, t + 1)
                nc.scalar.activation(vnat[:, t, :], PS[(0, 1, 7)[t % 3]][:, 0:D], ACT.Copy).then_inc(s_v, 1)

            def shared_in(i):
                rows = SROWS[i // B]
                k = 2 + 2 * (i % 2)
                act.wait_ge(s_shp, i + 1)
                if i >= 2:
                    act.wait_ge(s_hs, i - 1)
                nc.scalar.activation(sg[0:rows, i % 2, :], PS[k][0:rows, :], ACT.Tanh, scale=0.5)
                nc.scalar.activation(sh1[0:rows, i % 2, :], PS[k][0:rows, :], ACT.Copy)
                nc.scalar.activation(hs[0:rows, i // B, (i % B) * S:(i % B + 1) * S], PS[k + 1][0:rows, :], ACT.Copy)\
                  .then_inc(s_shc, 1)
                act.wait_ge(s_shc, i + 1)
                nc.scalar.activation(sg[0:rows, i % 2, :], sg[0:rows, i % 2, :], ACT.Copy, scale=0.5, bias=0.5)\
                  .then_inc(s_sht, 1)

            shared_in(0)
            shared_in(1)
            act.wait_ge(s_qr, 2)
            nc.scalar.activation(qparts[:, :, 1, :], qrest, ACT.Copy).then_inc(s_qp0, 1)
            for i in range(2, NPAIR):
                shared_in(i)
            act.wait_ge(s_wff, 32)
            act.wait_ge(s_hs, NPAIR)
            act.wait_ge(s_skl, 0) if False else None
            absd = big[:, ex_at:ex_at + DC * FF]
            nc.scalar.activation(absd, w_fc1.rearrange("p c n -> p (c n)"), ACT.Abs, accum_out=tsum[:, 0:1])\
              .then_inc(s_abs, 1)
            act.wait_ge(s_abs, 1)
            nc.scalar.activation(absd, w_pj1.rearrange("p c n -> p (c n)"), ACT.Abs, accum_out=tsum[:, 1:2])\
              .then_inc(s_abs, 1)
            act.wait_ge(s_lgs, 1)
            nc.scalar.activation(sc[:, :, 0:E], lg, ACT.Exp).then_inc(s_lge, 1)
            for k in range(2):
                act.wait_ge(s_skTp, k + 1)
                nc.scalar.activation(slotk[:, k * 512:(k + 1) * 512], PS[6 + k][0:E, :], ACT.Copy).then_inc(s_skT, 1)

            def tokens_in(e, u, between=lambda: None):
                act.wait_ge(s_xeTp, e + 1)
                nc.scalar.activation(xeT[:, u % 2, :, :], PS[0][:, 0:D].rearrange("p (c n) -> p c n", c=DC),
                                     ACT.Copy).then_inc(s_xeT, 1)
                between()
                act.wait_ge(s_hp, e + 1)
                nc.scalar.activation(th[:, u % 2, :], PS[1][:, 0:INTER], ACT.Tanh, scale=0.5).then_inc(s_th, 1)

            def scale_out(e, u, free, gate):
                act.wait_ge(s_yp, e + 1)
                act.wait_ge(s_sc[u % 2], free)
                nc.scalar.activation(ye[:, u % 2, :], PS[3][:, 0:D], ACT.Copy, scale=gate).then_inc(s_y, 1)

            def exps(g, u):
                for c in (2 * u, 2 * u + 1):
                    act.wait_ge(s_lp, g * 4 + (c + 1))
                    nc.scalar.activation(ex[:, c, :], PS[4 + c % 2][:, :], ACT.Exp).then_inc(s_ex, 1)

            def place_values(g, group):
                act.wait_ge(s_vg, g * 128 + 128)
                for h4 in range(Q4):
                    r = slice(32 * h4, 32 * h4 + 32)
                    c = COLS * h4 + 1
                    last = nc.scalar.activation(
                        vps[r, :, c:c + 2 * DV].rearrange("p g (s d) -> p s g d", s=2),
                        vals[r, group, :, :, :].rearrange("p k s g d -> p (k s) g d"), ACT.Copy)
                last.then_inc(s_vpr, 1)

            def unit(g, u, gate, group, last=False):
                e = g * SLOTS + u
                attention = (lambda: exps(g, u)) if u < 2 else (lambda: None)
                if last:
                    attention()
                else:
                    tokens_in(g * SLOTS + (u + 1), u + 1, attention)
                if u == 1:
                    place_values(g, group)
                scale_out(e, u, g * 32 + 16 * (1 + u // 2), gate)

            act.wait_ge(s_fill, 5)
            gates = xe[:, :, D:TAB].rearrange("p r (g u) -> p r u g", u=SLOTS)
            tokens_in(0, 0)
            with act.Fori(0, NG - 1) as g:
                for u in range(SLOTS):
                    unit(g, u, gates[:, u, u, bass.ds(g, 1)], bass.ds(g, 1))
            for u in range(SLOTS):
                unit(NG - 1, u, gates[:, u, u, NG - 1:NG], slice(NG - 1, NG), u == SLOTS - 1)

            for t in range(NT):
                act.wait_ge(s_oTp, t + 1)
                nc.scalar.activation(oT[:, :, t * P:(t + 1) * P], PS[t % 2][:, 0:D].rearrange("p (c n) -> p c n", c=DC),
                                     ACT.Copy).then_inc(s_oT, 1)

            act.wait_ge(s_l1c, 64)
            nc.scalar.activation(edrow, edrow, ACT.Exp).then_inc(s_ed, 1)
            nc.scalar.activation(edcol, edcol, ACT.Exp).then_inc(s_ed, 1)
            act.wait_ge(s_edn, 1)
            nc.scalar.activation(kdec, edrow, ACT.Exp, scale=const("jdec"))
            nc.scalar.activation(wall, edcol, ACT.Exp, scale=float(P))
            for f in range(2):
                nc.scalar.activation(wb[:, f, :], const("steps"), ACT.Exp, scale=edcol[:, f:f + 1])
            act.wait_ge(s_xn, NT + 1)
            for h in range(H1):
                last = nc.scalar.activation(wmask[:, h, :], const("pdist"), ACT.Exp, scale=edrow[:, h:h + 1])
            last.then_inc(s_wm1, 1)
            xnT_copies(NT)
            for i in range(2 * FC):
                act.wait_ge(s_ffp, i + 1)
                nc.scalar.activation(hf[:, i // 2, (i % 2) * S:(i % 2 + 1) * S], PS[2 + i % 6][:, :], ACT.Relu)\
                  .then_inc(s_relu, 1)
            act.wait_ge(s_wmc, 2)
            for i in range(4):
                f, n = divmod(i, 2)
                act.wait_ge(s_kTp, i + 1)
                for q in range(4):
                    r = slice(32 * q, 32 * q + 32)
                    last = nc.scalar.activation(kq[r, f, q, n * S:(n + 1) * S], PS[i][r, :], ACT.Copy)
                last.then_inc(s_kT, 1)
            act.wait_ge(s_x2, NT)
            for i in range(4):
                f, n = divmod(i, 2)
                act.wait_ge(s_rTp, i + 1)
                for h in range(4):
                    last = nc.scalar.activation(rq[:, f, h, n * S:(n + 1) * S], PS[i][:, :], ACT.Copy,
                                                scale=const("quad")[:, h:h + 1])
                last.then_inc(s_rq, 1)
            for t in range(NT):
                act.wait_ge(s_v1p, t + 1)
                nc.scalar.activation(vn[:, t, :], PS[4 + t % 4][:, 0:D], ACT.Copy).then_inc(s_v1, 1)
            for t in range(NT):
                act.wait_ge(s_gp, t + 1)
                nc.scalar.activation(gn[:, t, :], PS[t % 4][:, 0:D], ACT.Tanh, scale=0.5).then_inc(s_gt, 1)
            for t in range(NT):
                for f in range(2):
                    u = 2 * t + f
                    act.wait_ge(s_yTp, u + 1)
                    if t >= 1 and f == 0:
                        act.wait_ge(s_ynp, t)
                    nc.scalar.activation(yTs[:, f, 0:P], PS[4 + u % 2][:, 0:P], ACT.Copy).then_inc(s_yT, 1)
                act.wait_ge(s_ynp, t + 1)
                nc.scalar.activation(xn[:, t, 0:D], PS[7][:, 0:D], ACT.Copy).then_inc(s_yn, 1)
                if t == TPB or t == NT - 1:
                    act.wait_ge(s_gv, 1 + t // (NT - 1))
                    nc.scalar.activation(gst[:, 1, :], gst[:, 0, :], ACT.Sqrt).then_inc(s_gs, 1)
            for t in range(NT):
                act.wait_ge(s_zTp, t + 1)
                nc.scalar.activation(xnT[:, :, t * P:(t + 1) * P], PS[t % 2][:, 0:D].rearrange("p (c n) -> p c n", c=DC),
                                     ACT.Copy).then_inc(s_zT, 1)

        @block.vector
        def _(dve):
            steps = [0]

            def note(ins):
                steps[0] += 1
                ins.then_inc(s_dve, 1)

            def settle():
                dve.wait_ge(s_dve, steps[0])

            def link(ins):
                note(ins)
                settle()

            def wide(ap, *shape):
                return ap.broadcast_to([P, *shape])

            def layernorm(n):
                for half in range(B):
                    tiles = range(half * TPB, (half + 1) * TPB)
                    if n == 0:
                        dve.wait_ge(s_x[half], 16)
                    for t in tiles:
                        note(nc.vector.bn_stats(stats[:, t, :], xs[:, t, :]))
                    settle()
                    for t in tiles:
                        note(nc.vector.bn_aggr(mv[:, t, :], stats[:, t, :]))
                    settle()
                    nc.vector.tensor_scalar(rstd[:, 0, tiles.start:tiles.stop], mv[:, tiles.start:tiles.stop, 1],
                                            LN_EPS, None, ALU.add).then_inc(s_var, 1)
                for half in range(B):
                    dve.wait_ge(s_rstd, B * n + half + 1)
                    for t in range(half * TPB, (half + 1) * TPB):
                        nc.vector.tensor_scalar(xn[:, t, 0:D], xs[:, t, :], mv[:, t, 0:1], rstd[:, 1, t:t + 1],
                                                ALU.subtract, ALU.mult).then_inc(s_xn, 1)

            layernorm(0)
            dve.wait_ge(s_const, 16)
            dve.wait_ge(s_keys, B)
            settle()
            sides = [(b, side) for b in range(B) for side in range(2)]
            for r in range(TOPK // 8):
                c = slice(8 * r, 8 * r + 8)
                for b, side in sides:
                    note(nc.vector.max(topv[:, b, side, c], keys[:, b, side, :]))
                settle()
                for b, side in sides:
                    note(nc.vector.max_index(topi[:, b, side, c], topv[:, b, side, c], keys[:, b, side, :]))
                settle()
                if r < TOPK // 8 - 1:
                    for b, side in sides:
                        note(nc.vector.match_replace(keys[:, b, side, :], topv[:, b, side, c], keys[:, b, side, :],
                                                     -3.0e38))
                    settle()
            for n, (b, side) in enumerate(sides):
                note(nc.vector.tensor_scalar(vidx[:, b, side, :], topi[:, b, side, :], float(H0 if side else -H0),
                                             const("vrow")[:, n:n + 1], ALU.mult, ALU.add))
            settle()
            nc.vector.transpose(vidxT.bitcast(U32), vidx.rearrange("p b s n -> p (b s n)").bitcast(U32))\
              .then_inc(s_vidx, 1)
            top = topv.rearrange("p b s n -> p (b s) n")
            link(nc.vector.tensor_tensor(dkf.rearrange("p (x n) -> p x n", n=TOPK), top,
                                         top[:, :, 0:1].broadcast_to([P, B * 2, TOPK]), ALU.subtract))

            def split(src, parts):
                link(nc.vector.tensor_copy(parts[0], src))
                link(nc.vector.tensor_tensor(src, src, parts[0], ALU.subtract))
                link(nc.vector.tensor_copy(parts[1], src))
                return nc.vector.tensor_tensor(parts[2], src, parts[1], ALU.subtract)

            split(dkf, [dkparts[:, a, :] for a in range(PARTS)]).then_inc(s_dk, 1)
            dve.wait_ge(s_lgp, 1)
            lp = PS[6][:, :].rearrange("p (t e) -> p t e", t=NT)
            note(nc.vector.memset(sc[:, :, E:E + 2], -1.0))
            link(nc.vector.tensor_reduce(rsm[:, 0, :], lp, AX, ALU.max))
            nc.vector.tensor_tensor(lg, lp, rsm[:, 0, :].unsqueeze(2).broadcast_to([P, NT, E]), ALU.subtract)\
              .then_inc(s_lgs, 1)
            dve.wait_ge(s_lge, 1)
            link(nc.vector.tensor_reduce(rsm[:, 0, :], sc[:, :, 0:E], AX, ALU.add))
            link(nc.vector.reciprocal(rsm[:, 1, :], rsm[:, 0, :]))
            link(nc.vector.tensor_tensor(sc[:, :, 0:E], sc[:, :, 0:E],
                                         rsm[:, 1, :].unsqueeze(2).broadcast_to([P, NT, E]), ALU.mult))
            for t in range(NT):
                note(nc.vector.max(rt8[:, t, :], sc[:, t, 0:E]))
            settle()
            link(nc.vector.memset(rt8[:, :, KSEL:8], -1.0))
            for t in range(NT):
                note(nc.vector.match_replace(sr[:, t, :], rt8[:, t, :], sc[:, t, :], -2.0))
            settle()
            link(nc.vector.tensor_scalar(lg, sr[:, :, 0:E], -1.5, None, ALU.is_lt))
            note(nc.vector.tensor_tensor(skey, lg, const("tokinv").unsqueeze(2).broadcast_to([P, NT, E]), ALU.mult))
            nc.vector.tensor_tensor(xn[:, :, D:TAB], lg, sc[:, :, 0:E], ALU.mult).then_inc(s_gate, 1)

            for k in range(2):
                dve.wait_ge(s_qmp, k + 1)
                nc.vector.tensor_scalar(qmask[:, 4 * k:4 * k + 4, :],
                                        PS[k][:, :].rearrange("p (t h) -> p t h", t=4), 0.0, None, ALU.is_gt)\
                  .then_inc(s_qm, 1)

            dve.wait_ge(s_skT, 2)
            for r in range(CAP // 8):
                c = slice(8 * r, 8 * r + 8)
                link(nc.vector.max(slots[:, c], slotk))
                if r < CAP // 8 - 1:
                    link(nc.vector.match_replace(slotk, slots[:, c], slotk, 0.0))
            nc.vector.tensor_scalar(slots[:, 0:1], slots[:, 0:1], 0.0, None, ALU.add).then_inc(s_slots, 1)
            dve.wait_ge(s_slotsTp, 1)
            note(nc.vector.tensor_scalar(nat_tmp[:, 0, :], PS[6][:, 0:E], 0.0, const("slot"), ALU.is_equal, ALU.mult))
            link(nc.vector.tensor_scalar(nat_tmp[:, 1, :], PS[6][:, 0:E], -1.0, float(N), ALU.mult, ALU.add))
            nc.vector.tensor_tensor(sidx, nat_tmp[:, 0, :], nat_tmp[:, 1, :], ALU.add).then_inc(s_sidx, 1)

            dve.wait_ge(s_absp, 1)
            link(nc.vector.tensor_scalar(tsum[:, 2:4], PS[6][:, 0:2], 1.0 / (FF * D), 1e-5, ALU.mult, ALU.max))
            link(nc.vector.tensor_scalar(tsum[:, 4:6], tsum[:, 2:4], 0.7, None, ALU.mult))
            link(nc.vector.tensor_scalar(tsum[:, 6:8], tsum[:, 4:6], -1.0, None, ALU.mult))
            nc.vector.tensor_scalar(tsum[:, 2:4], tsum[:, 2:4], -1.0, None, ALU.mult).then_inc(s_tsum, 1)
            dve.wait_ge(s_tsum, 1)

            def hidden(e, u):
                dve.wait_ge(s_th, e + 1)
                nc.vector.scalar_tensor_tensor(ge[:, u % 2, :], th[:, u % 2, :], 1.0, PS[1][:, 0:INTER],
                                               ALU.add, ALU.mult).then_inc(s_ge, 1)
                dve.wait_ge(s_ge, e + 1)
                nc.vector.scalar_tensor_tensor(hm[:, u % 2, :], ge[:, u % 2, :], 0.5,
                                               PS[1][:, INTER:2 * INTER], ALU.mult, ALU.mult).then_inc(s_hm, 1)

            def hidden_T(e, u):
                dve.wait_ge(s_hTp, e + 1)
                nc.vector.tensor_copy(heT[:, u % 2, :, :], PS[2][0:IC, 0:2 * P].rearrange("p (c n) -> p c n", c=2))\
                  .then_inc(s_hT, 1)

            def out_copy(g):
                dve.wait_ge(s_av, g + 1)
                nc.vector.tensor_copy(avT, PS[6][:, :]).then_inc(s_avT, 1)

            def nat_copy(g, col):
                dve.wait_ge(s_natp, g + 1)
                nc.vector.tensor_copy(nat[:, :, col, :].rearrange("p t k m -> p (t k) m"),
                                      PS[7][:, :].rearrange("p (t m) -> p t m", t=TPB)).then_inc(s_nat, 1)

            ff_w = [w.rearrange("p c n -> p (c n)").rearrange("p (k n) -> p k n", k=8) for w in (w_fc1, w_pj1)]

            def ternary(b, g, col):
                w = ff_w[b][:, col, :].rearrange("p k n -> p (k n)")
                for step, make in enumerate((
                        lambda: nc.vector.tensor_scalar(tern_t, w, tsum[:, 4 + b:5 + b], None, ALU.is_gt),
                        lambda: nc.vector.scalar_tensor_tensor(tern_t, w, tsum[:, 6 + b:7 + b], tern_t,
                                                               ALU.is_lt, ALU.subtract),
                        lambda: nc.vector.scalar_tensor_tensor(tern_t, tern_t, tsum[:, 2 + b:3 + b], w,
                                                               ALU.mult, ALU.subtract),
                        lambda: nc.vector.tensor_tensor(w, tern_t, w, ALU.add))):
                    make().then_inc(s_tern, 1)
                    dve.wait_ge(s_tern, g * 4 + (step + 1))

            def group(b, g, col, last=False):
                for u in range(SLOTS):
                    hidden_T(g * SLOTS + u, u)
                    if not (last and u == SLOTS - 1):
                        hidden(g * SLOTS + (u + 1), u + 1)
                    if u == 0:
                        ternary(b, g, col)
                    if u == 2:
                        out_copy(g)
                    if u == 3:
                        nat_copy(g, col)

            def normalise(b):
                dve.wait_ge(s_nat, 8 * (b + 1))
                dve.wait_ge(s_qm, 2)

                def part(c):
                    v = nat.rearrange("p t g (a m) -> p (t g a) m", a=4)
                    return v[:, :, c:c + 3 * COLS + 1:COLS]

                flat = [den[:, k, :, :].rearrange("p t h -> p (t h)").rearrange("p (x a) -> p x a", a=Q4)
                        for k in range(3)]
                sel = qmask[:, b * TPB:(b + 1) * TPB, :].rearrange("p t (a g) -> p t g a", a=Q4)
                k3 = [f.rearrange("p (t g) a -> p t g a", t=TPB) for f in flat]
                link(nc.vector.reciprocal(flat[0], part(0)))
                link(nc.vector.tensor_tensor(k3[1], k3[0], sel, ALU.mult))
                link(nc.vector.tensor_tensor(flat[2], flat[0], flat[1], ALU.subtract))
                for d in range(DV):
                    o = onat[:, b * TPB:(b + 1) * TPB, :].rearrange("p t (a g d) -> p t g a d", a=Q4, d=DV)[:, :, :, :, d]
                    top = part(1 + d).rearrange("p (t g) a -> p t g a", t=TPB)
                    note(nc.vector.tensor_tensor(o, top, k3[1], ALU.mult))
                    link(nc.vector.tensor_tensor(flat[0], part(1 + DV + d), flat[2], ALU.mult))
                    ins = nc.vector.tensor_tensor(o, o, k3[0], ALU.add)
                    if d == DV - 1:
                        ins.then_inc(s_on, 1)
                    else:
                        link(ins)

            hidden(0, 0)
            for b in range(B):
                with dve.Fori(0, 8 - b) as k:
                    group(b, k + 8 * b, bass.ds(k, 1))
                if b == B - 1:
                    group(b, NG - 1, slice(7, 8), last=True)
                normalise(b)

            for t in range(NT):
                dve.wait_ge(s_x1p, t + 1)
                nc.vector.tensor_tensor(xs[:, t, :], PS[2 + t % 2][:, 0:D], xs[:, t, :], ALU.add).then_inc(s_x1, 1)
            dve.wait_ge(s_x1, NT)
            dve.wait_ge(s_racc, 32)
            for i in range(2):
                for t in range(NT):
                    note(nc.vector.tensor_tensor(xs[:, t, :], xs[:, t, :], racc[i][:, t, :], ALU.add))
                settle()

            layernorm(1)
            dve.wait_ge(s_ed, 2)
            note(nc.vector.tensor_scalar(edrow, edrow, 1e30, -1.0, ALU.min, ALU.mult))
            nc.vector.tensor_scalar(edcol, edcol, 1e30, -1.0, ALU.min, ALU.mult).then_inc(s_edn, 1)
            def square(i):
                dve.wait_ge(s_relu, i + 1)
                h = hf[:, i // 2, (i % 2) * S:(i % 2 + 1) * S]
                nc.vector.tensor_tensor(h, h, h, ALU.mult).then_inc(s_sq, 1)

            dve.wait_ge(s_xnT, 2 * NT)
            for c in range(DC):
                src = xnT[:, c, :].rearrange("p (b n) -> p b n", b=B)
                dst = dif[:, c, :].rearrange("p (b n) -> p b n", b=B)
                note(nc.vector.tensor_tensor(dst[:, :, 1:S], src[:, :, 0:S - 1], src[:, :, 1:S], ALU.subtract))
                note(nc.vector.tensor_scalar(dst[:, :, 0:1], src[:, :, 0:1], -1.0, None, ALU.mult))
            settle()

            def mixture(k):
                for c in range(DC):
                    ins = nc.vector.scalar_tensor_tensor(mix[:, k % 2, c * N:(c + 1) * N], dif[:, c, :],
                                                         maat[:, 2 * k + c:2 * k + c + 1], xnT[:, c, :],
                                                         ALU.mult, ALU.add)
                    if c < DC - 1:
                        note(ins)
                ins.then_inc(s_mix, 1)

            dve.wait_ge(s_l1c, 64)
            mixture(0)
            mixture(1)
            for i in range(2 * FC):
                square(i)
            dve.wait_ge(s_edn, 1)
            for t in range(NT):
                dve.wait_ge(s_knp, t + 1)
                if t == 0:
                    dve.wait_ge(s_wm1, 1)
                nc.vector.tensor_tensor(kn[:, t, :].rearrange("p (h n) -> p h n", n=HN),
                                        PS[4 + t % 4][:, 0:D].rearrange("p (h n) -> p h n", n=HN),
                                        kdec.unsqueeze(2).broadcast_to([P, H1, HN]), ALU.mult).then_inc(s_kn, 1)
            mixture(2)
            dve.wait_ge(s_gb, 32)
            for t in range(NT):
                dve.wait_ge(s_ffd, t + 1)
                nc.vector.tensor_tensor(xs[:, t, :], PS[4 + t % 4][:, 0:D], xs[:, t, :], ALU.add).then_inc(s_x2, 1)
            for i in range(4):
                f, n = divmod(i, 2)
                dve.wait_ge(s_rq, i + 1)
                nc.vector.tensor_tensor(rw[:, f, n * S:(n + 1) * S].rearrange("p (t n) -> p t n", n=P),
                                        PS[i][:, :].rearrange("p (t n) -> p t n", n=P),
                                        wb[:, f, :].unsqueeze(1).broadcast_to([P, TPB, P]), ALU.mult).then_inc(s_rw, 1)
            mixture(3)
            dve.wait_ge(s_wmc, 1)
            for h in range(H1):
                note(nc.vector.scalar_tensor_tensor(wmask[:, h, :], ident, urow[:, h:h + 1], wmask[:, h, :],
                                                    ALU.mult, ALU.add))
            settle()
            for t in range(NT):
                dve.wait_ge(s_gt, t + 1)
                nc.vector.scalar_tensor_tensor(gn[:, t, :], gn[:, t, :], 1.0, PS[t % 4][:, 0:D], ALU.add, ALU.mult)\
                  .then_inc(s_g, 1)

            def state_update(u):
                f = u % 2
                dve.wait_ge(s_kvp, (u // 8) * 6 + u % 8 + 1)
                link(nc.vector.tensor_tensor(kvt, PS[6][:, 0:P], const("heads"), ALU.mult))
                nc.vector.scalar_tensor_tensor(state[:, f, :], state[:, f, :], wall[:, f:f + 1], kvt,
                                               ALU.mult, ALU.add).then_inc(s_st, 1)

            def group_norm(b):
                y = xn[:, b * TPB:(b + 1) * TPB, 0:D].rearrange("p t (h n) -> p t h n", n=HN)
                g1 = [gst[:, k, :].rearrange("p (t h) -> p t h", t=TPB) for k in range(3)]
                sq = gnt.rearrange("p (t h n) -> p t h n", t=TPB, n=HN)
                dve.wait_ge(s_yn, TPB * (b + 1))
                link(nc.vector.tensor_reduce(g1[0], y, AX, ALU.add))
                link(nc.vector.tensor_scalar(gst[:, 1, :], gst[:, 0, :], 1.0 / HN, None, ALU.mult))
                for t in range(TPB):
                    note(nc.vector.tensor_tensor(y[:, t], y[:, t], g1[1][:, t].unsqueeze(2).broadcast_to([P, H1, HN]),
                                                 ALU.subtract))
                settle()
                for t in range(TPB):
                    note(nc.vector.tensor_tensor(sq[:, t], y[:, t], y[:, t], ALU.mult))
                settle()
                link(nc.vector.tensor_reduce(g1[0], sq, AX, ALU.add))
                nc.vector.tensor_scalar(gst[:, 0, :], gst[:, 0, :], 1.0 / HN, GN_EPS, ALU.mult, ALU.add)\
                  .then_inc(s_gv, 1)
                dve.wait_ge(s_gs, b + 1)
                link(nc.vector.reciprocal(gst[:, 1, :], gst[:, 1, :]))
                link(nc.vector.tensor_tensor(gst[:, 2, :], gst[:, 1, :], gst[:, 1, :], ALU.mult))
                link(nc.vector.tensor_tensor(gst[:, 2, :], gst[:, 2, :], gst[:, 0, :], ALU.mult))
                link(nc.vector.tensor_scalar(gst[:, 2, :], gst[:, 2, :], -0.5, 1.5, ALU.mult, ALU.add))
                link(nc.vector.tensor_tensor(gst[:, 1, :], gst[:, 1, :], gst[:, 2, :], ALU.mult))
                for t in range(TPB):
                    note(nc.vector.tensor_tensor(y[:, t], y[:, t], g1[1][:, t].unsqueeze(2).broadcast_to([P, H1, HN]),
                                                 ALU.mult))
                settle()
                for k, op in ((0, ALU.mult), (1, ALU.add)):
                    for t in range(b * TPB, (b + 1) * TPB):
                        note(nc.vector.tensor_tensor(xn[:, t, 0:D], xn[:, t, 0:D], gb[:, k, :], op))
                    settle()
                for t in range(b * TPB, (b + 1) * TPB):
                    nc.vector.scalar_tensor_tensor(xn[:, t, 0:D], xn[:, t, 0:D], 0.5, gn[:, t, :], ALU.mult, ALU.mult)\
                      .then_inc(s_z, 1)

            for u in range(UNITS):
                if u % 8 == 0:
                    if u:
                        dve.wait_ge(s_yTp, u)
                    nc.vector.memset(state, 0.0).then_inc(s_st, 1)
                    dve.wait_ge(s_st, 7 * (u // 8) + 1)
                f = u % 2
                for q in range(4):
                    a = 4 * u + q
                    dve.wait_ge(s_a1p, a + 1)
                    if a >= 8:
                        dve.wait_ge(s_yTp, u - 1)
                    heads = slice(HH * f + 4 * q, HH * f + 4 * q + 4)
                    nc.vector.tensor_tensor(aring[:, a % 8, :].rearrange("p (h n) -> p h n", h=4),
                                            PS[q][:, :].rearrange("p (h n) -> p h n", h=4), wmask[:, heads, :],
                                            ALU.mult).then_inc(s_a1, 1)
                if u >= 1 and (u - 1) % 8 < 6:
                    state_update(u - 1)
                if u == 8 + 3:
                    group_norm(0)
            group_norm(1)
            for t in range(NT):
                dve.wait_ge(s_op, t + 1)
                nc.vector.tensor_tensor(xs[:, t, :], PS[4 + t % 4][:, 0:D], xs[:, t, :], ALU.add).then_inc(s_o, 1)

        @block.tensor
        def _(pe):
            def product(o, pairs):
                for n, (w, m) in enumerate(pairs):
                    last = nc.tensor.matmul(o, w, m, start=(n == 0), stop=(n == len(pairs) - 1))
                return last

            def transposes(src, bank, done):
                for c in range(DC):
                    last = nc.tensor.transpose(bank[:, c * P:(c + 1) * P], src[:, c * P:(c + 1) * P], ident)
                last.then_inc(done, 1)

            def xn_transposes(base):
                for t in range(NT):
                    pe.wait_ge(s_xn, base + t + 1)
                    if base + t >= 2:
                        pe.wait_ge(s_xnT, base + t - 1)
                    transposes(xn[:, t, 0:D], PS[t % 2], s_xnTp)

            def tok(t):
                return slice(t * P, (t + 1) * P)

            def half(b):
                return slice(b * S, (b + 1) * S)

            pe.wait_ge(s_const, 16)
            xn_transposes(0)
            pe.wait_ge(s_wqkg, 32)
            pe.wait_ge(s_xnT, NT)
            for k, done in ((1, s_kp), (0, s_qp)):
                for b in range(B):
                    last = product(PS[(4, 2)[k] + b][:, :],
                                   [(wqk[:, c, k * H0:(k + 1) * H0], xnT[:, c, half(b)]) for c in range(DC)])
                last.then_inc(done, 1)
            for t in range(NT):
                last = product(PS[6][:, t * E:(t + 1) * E], [(xnT[:, c, tok(t)], wg[:, c, :]) for c in range(DC)])
            last.then_inc(s_lgp, 1)
            pe.wait_ge(s_wv, 16)
            for t in range(NT):
                if t >= 3:
                    pe.wait_ge(s_v, t - 2)
                product(PS[(0, 1, 7)[t % 3]][:, 0:D], [(xnT[:, c, tok(t)], wv[:, c, :]) for c in range(DC)])\
                    .then_inc(s_vp, 1)
            pe.wait_ge(s_q32, B)
            pe.wait_ge(s_v, NT)
            for k in range(2):
                for t in range(4):
                    last = nc.tensor.transpose(PS[k][:, tok(t)], q32[:, 0, tok(4 * k + t)], ident)
                last.then_inc(s_qmp, 1)
            pe.wait_ge(s_wsh, 48)
            pe.wait_ge(s_keys, B)
            for i in range(NPAIR):
                rows, c0 = SROWS[i // B], P * (i // B)
                if i >= 2:
                    pe.wait_ge(s_shc, i - 1)
                for k in range(2):
                    last = product(PS[2 + 2 * (i % 2) + k][0:rows, :],
                                   [(wsh13[:, c, k * SHARED + c0:k * SHARED + c0 + rows], xnT[:, c, half(i % B)])
                                    for c in range(DC)])
                last.then_inc(s_shp, 1)
            pe.wait_ge(s_gate, 1)
            for k in range(2):
                for t in range(4):
                    last = nc.tensor.transpose(PS[6 + k][0:E, tok(t)], skey[:, 4 * k + t, :], ident)
                last.then_inc(s_skTp, 1)
            pe.wait_ge(s_slots, 1)
            pe.wait_ge(s_skT, 2)
            nc.tensor.transpose(PS[6][:, 0:E], slots, ident[0:E, 0:E]).then_inc(s_slotsTp, 1)
            pe.wait_ge(s_abs, 2)
            pe.wait_ge(s_fill, 4)
            pe.wait_ge(s_sidx, 1)
            nc.tensor.matmul(PS[6][:, 0:2], ones[:, :], tsum[:, 0:2], start=True, stop=True).then_inc(s_absp, 1)

            def tokens_T(u, gathered):
                pe.wait_ge(s_xe[u % SLOTS], gathered)
                transposes(xe[:, u % SLOTS, 0:D], PS[0], s_xeTp)

            def up(e, u, loaded):
                pe.wait_ge(s_wm[u % SLOTS], loaded)
                pe.wait_ge(s_xeT, e + 1)
                product(PS[1][:, 0:2 * INTER],
                        [(xeT[:, u % 2, c, :], w13r[u % SLOTS][:, c, :]) for c in range(DC)]).then_inc(s_hp, 1)

            def hidden_T(e, u):
                pe.wait_ge(s_hm, e + 1)
                for c in range(2):
                    last = nc.tensor.transpose(PS[2][0:IC, c * P:(c + 1) * P],
                                               hm[:, u % 2, c * IC:(c + 1) * IC], ident)
                last.then_inc(s_hTp, 1)

            def down(e, u):
                pe.wait_ge(s_hT, e + 1)
                product(PS[3][:, 0:D], [(heT[:, u % 2, c, :], w2r[u % SLOTS][:, c, :]) for c in range(2)])\
                    .then_inc(s_yp, 1)

            sk_v = sk.rearrange("p (g c) n -> p c g n", c=4)

            def logits(g, c, group):
                if c == 0:
                    pe.wait_ge(s_qxl, g * (16 * PARTS * PARTS) + 16 * PARTS * PARTS)
                if c >= 2:
                    pe.wait_ge(s_ex, g * 4 + (c - 1))
                nc.tensor.matmul(PS[4 + c % 2][:, :], sk_v[:, c, group, :].rearrange("p g n -> p (g n)"), qx[:, c, :],
                                 start=True, stop=True).then_inc(s_lp, 1)

            def weighted(g):
                pe.wait_ge(s_vpr, g + 1)
                pe.wait_ge(s_ex, g * 4 + 4)
                for c in range(4):
                    last = nc.tensor.matmul(PS[6][32 * c:32 * c + 32, :], vps[:, c, :], ex[:, c, :],
                                            start=True, stop=True, skip_group_check=True)
                last.then_inc(s_av, 1)

            def to_natural(g):
                pe.wait_ge(s_avT, g + 1)
                for t in range(TPB):
                    last = nc.tensor.transpose(PS[7][:, tok(t)], avT[:, tok(t)], ident)
                last.then_inc(s_natp, 1)

            def unit(g, u, group, last=False):
                if not last:
                    tokens_T(u + 1, g * 16 + 16 * (1 + (u + 1) // SLOTS))
                if u < 2:
                    logits(g, 2 * u, group)
                    logits(g, 2 * u + 1, group)
                if u == 2:
                    weighted(g)
                if u == 3:
                    to_natural(g)
                hidden_T(g * SLOTS + u, u)
                if not last:
                    up(g * SLOTS + (u + 1), u + 1, g * 32 + 32 * (1 + (u + 1) // SLOTS))
                if last:
                    pe.wait_ge(s_y, E - 1)
                down(g * SLOTS + u, u)

            pe.wait_ge(s_shc, NPAIR)
            pe.wait_ge(s_qm, 2)
            pe.wait_ge(s_skl, 16 * PARTS * 2 * Q4 * B)
            pe.wait_ge(s_tsum, 1)
            tokens_T(0, 16)
            up(0, 0, 32)
            with pe.Fori(0, NG - 1) as g:
                for u in range(SLOTS):
                    unit(g, u, bass.ds(g, 1))
            for u in range(SLOTS):
                unit(NG - 1, u, slice(NG - 1, NG), u == SLOTS - 1)

            for t in range(NT):
                if t % TPB == 0:
                    pe.wait_ge(s_on, t // TPB + 1)
                if t == 0:
                    pe.wait_ge(s_xeT, E)
                    pe.wait_ge(s_y, E)
                if t >= 2:
                    pe.wait_ge(s_oT, t - 1)
                transposes(onat[:, t, :], PS[t % 2], s_oTp)
            pe.wait_ge(s_wo0, 16)
            for t in range(NT):
                pe.wait_ge(s_oT, t + 1)
                if t >= 2:
                    pe.wait_ge(s_x1, t - 1)
                product(PS[2 + t % 2][:, 0:D],
                        [(oT[:, c, tok(t)], wo0[:, c, :]) for c in range(DC)] +
                        [(hs[0:SROWS[c], c, tok(t)], wsh2[0:SROWS[c], c, :]) for c in range(3)]).then_inc(s_x1p, 1)

            xn_transposes(NT)
            pe.wait_ge(s_xnT, 2 * NT)
            pe.wait_ge(s_nat, NG)
            pe.wait_ge(s_tern, 4 * NG)
            for i in range(2 * FC):
                if i >= 6:
                    pe.wait_ge(s_relu, i - 5)
                product(PS[2 + i % 6][:, :],
                        [(w_fc1[:, c, (i // 2) * P:(i // 2 + 1) * P], xnT[:, c, half(i % 2)]) for c in range(DC)])\
                    .then_inc(s_ffp, 1)

            def mixed(k, c, cols):
                return mix[:, k % 2, c * N + cols.start:c * N + cols.stop]

            def project_T(k, w, bank_free, done):
                for i in range(4):
                    f, n = divmod(i, 2)
                    bank_free(i)
                    product(PS[i][:, :], [(w5[:, w, c, f * P:(f + 1) * P], mixed(k, c, half(n))) for c in range(DC)])\
                        .then_inc(done, 1)

            def project(k, w, bank, bank_free, done):
                for t in range(NT):
                    bank_free(t)
                    product(PS[bank + t % 4][:, 0:D], [(mixed(k, c, tok(t)), w5[:, w, c, :]) for c in range(DC)])\
                        .then_inc(done, 1)

            pe.wait_ge(s_w5, 16)
            pe.wait_ge(s_relu, 2 * FC)
            pe.wait_ge(s_mix, 1)
            project_T(0, 1, lambda i: None, s_kTp)
            project(0, 1, 4, lambda t: pe.wait_ge(s_kn, t - 3) if t >= 4 else None, s_knp)
            pe.wait_ge(s_sq, 2 * FC)
            for t in range(NT):
                pe.wait_ge(s_kn, min(t + 5, NT))
                if t >= 4:
                    pe.wait_ge(s_x2, t - 3)
                product(PS[4 + t % 4][:, 0:D], [(hf[:, c, tok(t)], w_pj1[:, c, :]) for c in range(FC)]).then_inc(s_ffd, 1)
            pe.wait_ge(s_mix, 2)
            project_T(1, 0, lambda i: pe.wait_ge(s_kT, i + 1), s_rTp)

            def v_bank(t):
                pe.wait_ge(s_x2, min(t + 5, NT))
                if t >= 4:
                    pe.wait_ge(s_v1, t - 3)

            pe.wait_ge(s_mix, 3)
            project(2, 2, 4, v_bank, s_v1p)

            def g_bank(t):
                if t < 4:
                    pe.wait_ge(s_rq, t + 1)
                    pe.wait_ge(s_rw, t + 1)
                else:
                    pe.wait_ge(s_g, t - 3)

            pe.wait_ge(s_mix, 4)
            project(3, 3, 0, g_bank, s_gp)

            def scores(u):
                t, f = divmod(u, 2)
                for q in range(4):
                    a = 4 * u + q
                    if a >= 4:
                        pe.wait_ge(s_a1, a - 3)
                    nc.tensor.matmul(PS[q][:, :], kq[:, f, q, tok(t)], rq[:, f, :, tok(t)], start=True, stop=True)\
                      .then_inc(s_a1p, 1)

            def outputs(u):
                t, f = divmod(u, 2)
                b, g = divmod(t, TPB)
                y = PS[4 + u % 2]
                if u >= 2:
                    pe.wait_ge(s_yT, u - 1)
                pe.wait_ge(s_st, 7 * b + max(1, 2 * g + f))
                nc.tensor.matmul(y[:, 0:P], state[:, f, :], rw[:, f, tok(t)], start=True, stop=False,
                                 skip_group_check=True)
                pe.wait_ge(s_a1, 4 * u + 4)
                pe.wait_ge(s_vd, t + 2)
                for h in range(4):
                    for q in range(4):
                        last = nc.tensor.matmul(y[32 * q:32 * q + 32, 0:P], vpr[:, t % 2, 4 * f + q, 32 * h:32 * h + 32],
                                                aring[:, (4 * u + q) % 8, h * P:(h + 1) * P], start=False,
                                                stop=(h == 3), skip_group_check=True)
                last.then_inc(s_yTp, 1)

            def state_product(u):
                t, f = divmod(u, 2)
                b, g = divmod(t, TPB)
                if g < TPB - 1:
                    n = 6 * b + 2 * g + f
                    if n:
                        pe.wait_ge(s_st, n + b + (1 if n % 6 else 0))
                    nc.tensor.matmul(PS[6][:, 0:P], kn[:, t, f * P:(f + 1) * P], vn[:, t, f * P:(f + 1) * P],
                                     start=True, stop=True).then_inc(s_kvp, 1)

            def y_natural(t):
                pe.wait_ge(s_yT, 2 * t + 2)
                if t >= 1:
                    pe.wait_ge(s_yn, t)
                for f in range(2):
                    last = nc.tensor.transpose(PS[7][:, f * P:(f + 1) * P], yTs[:, f, 0:P], ident)
                last.then_inc(s_ynp, 1)

            pe.wait_ge(s_g, NT)
            pe.wait_ge(s_v1, NT)
            scores(0)
            for u in range(UNITS):
                if u + 1 < UNITS:
                    scores(u + 1)
                outputs(u)
                state_product(u)
                if u >= 2 and u % 2 == 0:
                    y_natural(u // 2 - 1)
            y_natural(NT - 1)

            for t in range(NT):
                pe.wait_ge(s_z, t + 1)
                if t == 0:
                    pe.wait_ge(s_a1, 4 * UNITS)
                if t >= 2:
                    pe.wait_ge(s_zT, t - 1)
                transposes(xn[:, t, 0:D], PS[t % 2], s_zTp)
                if t >= 1:
                    final(t - 1) if False else None
            for t in range(NT):
                pe.wait_ge(s_zT, t + 1)
                if t == 0:
                    pe.wait_ge(s_yT, UNITS)
                    pe.wait_ge(s_st, 14)
                    pe.wait_ge(s_yn, NT)
                if t >= 4:
                    pe.wait_ge(s_o, t - 3)
                product(PS[4 + t % 4][:, 0:D], [(xnT[:, c, tok(t)], w5[:, 4, c, :]) for c in range(DC)]).then_inc(s_op, 1)


def kernel(**inputs):
    import concourse.bacc as bacc
    from concourse.bass_utils import run_bass_kernel_spmd

    a = {k: np.asarray(v) for k, v in inputs.items()}

    def chunks(w):
        c = w.shape[0] // P
        return np.ascontiguousarray(w.reshape(c, P, w.shape[1]).transpose(1, 0, 2))

    w1, w3 = a["L0_ffn_w1"], a["L0_ffn_w3"]
    w13 = np.concatenate([w1, w3], 1).transpose(0, 2, 1).reshape(E, DC, P, 2 * INTER).transpose(0, 2, 1, 3)
    w2 = a["L0_ffn_w2"].transpose(0, 2, 1).reshape(E, 2, IC, D).transpose(0, 2, 1, 3)
    maa = np.stack([a[f"L1_attn_time_maa_{k}"].reshape(DC, P) for k in "krvg"], 0)
    td = a["L1_attn_time_decay"].reshape(H1)
    arrays = {
        "x": a["L0_attn_x"],
        "consts": constants(),
        "w_qk": chunks(np.concatenate([a["L0_attn_Wq"], a["L0_attn_Wk"]], 0).T),
        "w_v": chunks(a["L0_attn_Wv"].T),
        "w_gate": chunks(a["L0_ffn_gate_w"].T),
        "w_sh13": chunks(np.concatenate([a["L0_ffn_sw1"], a["L0_ffn_sw3"]], 0).T),
        "w_sh2": a["L0_ffn_sw2"].T,
        "w_o0": chunks(a["L0_attn_Wo"].T),
        "w_13": w13,
        "w_2": w2,
        "maa": maa.transpose(2, 0, 1).reshape(P, 8),
        "td_row": td,
        "td_col": np.repeat(td, HN).reshape(2, P).T,
        "u_row": a["L1_attn_time_faaaa"].reshape(H1),
        "w_rkvgo": np.stack([chunks(a[f"L1_attn_W{k}"].T) for k in "rkvgo"], 1),
        "gamma": a["L1_attn_gamma"],
        "beta": a["L1_attn_beta"],
        "w_fc": chunks(a["L1_ffn_w_fc"].T),
        "w_pj": chunks(a["L1_ffn_w_proj"].T),
    }
    nc = bacc.Bacc("TRN2", target_bir_lowering=False, num_devices=1)
    arrays = {f"in_{k}": np.ascontiguousarray(v) for k, v in arrays.items()}
    args = [nc.dram_tensor(k, v.shape, mybir.dt.from_np(v.dtype), kind="ExternalInput").ap() for k, v in arrays.items()]
    out = nc.dram_tensor("out", (B, S, D), F32, kind="ExternalOutput").ap()
    block_kernel(nc, *args, out)
    r = run_bass_kernel_spmd(nc, [arrays], core_ids=[0])
    return r.results[0]["out"]
```

```python
import numpy as np
import concourse.bass as bass
from concourse import mybir
from contextlib import ExitStack

F32 = mybir.dt.float32
BF16 = mybir.dt.bfloat16
I32 = mybir.dt.int32
U32 = mybir.dt.uint32
ALU = mybir.AluOpType
ACT = mybir.ActivationFunctionType
AX = mybir.AxisListType.X

P = 128
B, S, D = 2, 512, 256
N = B * S
NT = N // P
TPB = NT // B
DC = D // P
LN_EPS = 1e-5

H0, TOPK, DV = 128, 32, 2
Q4 = P // TOPK
HG = H0 // Q4
PARTS = 3
ROWS = PARTS * PARTS * 2 * Q4
COLS = 1 + 2 * DV

E, INTER, KSEL, CAP = 64, 176, 6, 128
SHARED = 2 * INTER
IC = INTER // 2
SROWS = [128, 128, SHARED - 256]
TAB = D + E
PAD = N + CAP

H1, HN = 32, 8
HH = P // HN
GN_EPS = 1e-5 * 144
FF = 640
FC = FF // P

CONST = {}
for _name, _n in (("ident", P), ("pdist", P), ("steps", P), ("heads", P), ("tokinv", NT), ("vrow", 4), ("slot", 1),
                  ("jdec", 1), ("quad", 4)):
    CONST[_name] = (sum(n for _, n in CONST.values()), _n)
NCONST = sum(n for _, n in CONST.values())


def constants():
    p = np.arange(P)[:, None]
    i = np.arange(P)[None, :]
    cols = {
        "ident": p == i,
        "pdist": np.maximum(i - p - 1, 0),
        "steps": i + 0 * p,
        "heads": p // HN == i // HN,
        "tokinv": N - (p + P * np.arange(NT)[None, :]),
        "vrow": H0 * np.array([[S - 1, 0, S + S - 1, S]]) + p,
        "slot": p,
        "jdec": P - 1 - p,
        "quad": (p % 32) // HN == np.arange(4)[None, :],
    }
    return np.concatenate([np.broadcast_to(cols[k], (P, n)) for k, (_, n) in CONST.items()], 1).astype(np.float32)


def block_kernel(nc, x, consts, w_qk, w_v, w_gate, w_sh13, w_sh2, w_o0, w_13, w_2, maa, td_row, td_col, u_row,
                 w_rkvgo, gamma, beta, w_fc, w_pj, out):
    x_v = x.rearrange("b (t p) d -> p (b t) d", p=P)
    out_v = out.rearrange("b (t p) d -> p (b t) d", p=P)

    tok_tab = nc.dram_tensor("tok_tab", (PAD, TAB), F32, kind="Internal").ap()
    val_tab = nc.dram_tensor("val_tab", (N * H0, DV), F32, kind="Internal").ap()
    q_dram = nc.dram_tensor("q_dram", (PARTS, 2 * Q4, B, HG, S), BF16, kind="Internal").ap()
    k_dram = nc.dram_tensor("k_dram", (PARTS, 2, B, H0, TOPK), BF16, kind="Internal").ap()
    routed = [nc.dram_tensor(f"routed{i}", (PAD, D), F32, kind="Internal").ap() for i in range(2)]

    ctx = ExitStack()
    with ctx:
        def sb(name, shape, dt=F32):
            return ctx.enter_context(nc.sbuf_tensor(name, shape, dt))

        def sem(name):
            return ctx.enter_context(nc.semaphore(name))

        xs = sb("xs", [P, NT, D])
        xn = sb("xn", [P, NT, TAB])
        xnT = sb("xnT", [P, DC, N])
        cst = sb("cst", [P, NCONST])
        ones = sb("ones", [P, P])
        gb = sb("gb", [P, 2, D])
        wb = sb("wb", [P, 2, P])
        stats = sb("stats", [P, NT, 6])
        mv = sb("mv", [P, NT, 2])
        rstd = sb("rstd", [P, 2, NT])
        rsm = sb("rsm", [P, 3, NT])
        tsum = sb("tsum", [P, 8])
        gst = sb("gst", [P, 3, TPB * H1])
        nat_tmp = sb("nat_tmp", [P, 2, E])

        def const(name):
            at, n = CONST[name]
            return cst[:, at:at + n]

        ident = const("ident")

        BIGW = 44000
        big = sb("big", [P, BIGW])
        used = [0]

        def carve(words, rows=P, at=None):
            start = used[0] if at is None else at
            if at is None:
                used[0] += words
            assert start + words <= BIGW, (start, words)
            return big[0:rows, start:start + words]

        def v3(ap, a, n):
            return ap.rearrange("p (a n) -> p a n", a=a)

        w_fc1 = v3(carve(DC * FF), DC, FF)
        w_pj1 = v3(carve(FC * D), FC, D)
        early = used[0]
        wqk = v3(carve(DC * 256), DC, 256)
        wv = v3(carve(DC * D), DC, D)
        wg = v3(carve(DC * E), DC, E)
        wsh13 = v3(carve(DC * 2 * SHARED), DC, 2 * SHARED)
        wsh2 = v3(carve(3 * D), 3, D)
        wo0 = v3(carve(DC * D), DC, D)
        qparts_at = used[0]
        qparts = carve(2 * PARTS * N // 2).bitcast(BF16).rearrange("p (s a n) -> p s a n", s=2, a=PARTS)
        oT = v3(carve(DC * N, at=qparts_at), DC, N)
        keys_at = used[0]
        keys = carve(B * 2 * S).rearrange("p (b s n) -> p b s n", b=B, s=2)
        onat = v3(carve(NT * D, at=keys_at), NT, D)
        topv = carve(B * 2 * TOPK).rearrange("p (b s n) -> p b s n", b=B, s=2)
        topi = carve(B * 2 * TOPK).bitcast(U32).rearrange("p (b s n) -> p b s n", b=B, s=2)
        dkf = carve(B * 2 * TOPK)
        dkparts = v3(carve(PARTS * 64).bitcast(BF16), PARTS, B * 2 * TOPK)
        vidx = carve(B * 2 * TOPK).bitcast(I32).rearrange("p (b s n) -> p b s n", b=B, s=2)
        vidxT = carve(B * 2 * HG).bitcast(I32)
        vals = carve(B * 2 * HG * DV).rearrange("p (k s g d) -> p k s g d", k=B * 8, s=2, g=4)
        vps = carve(4 * 32).rearrange("p (g c) -> p g c", g=4)
        qx = v3(carve(4 * S // 2, ROWS).bitcast(BF16), 4, S)
        rt_at = used[0]
        sc = v3(carve(NT * (E + 2)), NT, E + 2)
        sr = v3(carve(NT * (E + 2)), NT, E + 2)
        skey = v3(carve(NT * E), NT, E)
        lg = v3(carve(NT * E), NT, E)
        sk_at = used[0]
        sk = carve(B * HG * P // 2, ROWS).bitcast(BF16).rearrange("p (g n) -> p g n", g=B * HG)
        sk_all = carve(B * HG * P // 2, at=sk_at)
        racc = [v3(carve(NT * D, at=sk_at + i * NT * D), NT, D) for i in range(2)]
        ex_at = used[0]
        ex = v3(carve(4 * S), 4, S)
        avT = carve(S)
        W13 = DC * 2 * INTER
        ring_at = used[0]
        carve(4 * (W13 + 2 * D))
        w13r = [v3(carve(W13, at=ring_at + r * (W13 + 2 * D)), DC, 2 * INTER) for r in range(4)]
        w2r = [v3(carve(2 * D, IC, at=ring_at + r * (W13 + 2 * D) + W13), 2, D) for r in range(4)]
        q32 = v3(carve(2 * N, at=ring_at), 2, N)
        qrest = v3(carve(2 * N, at=ring_at + 2 * N), 2, N)
        nat_at = used[0]
        carve(NT * D + S + 2 * CAP)
        vnat = v3(carve(NT * D, at=nat_at), NT, D)
        sgb = v3(carve(3 * S, at=nat_at), 3, S)
        slotk = carve(S, at=nat_at + NT * D)
        slots = carve(CAP, at=nat_at + NT * D + S)
        slotr = carve(CAP, at=nat_at + NT * D + S + CAP)
        qmask = v3(carve(NT * H0), NT, H0)
        hs = v3(carve(3 * N), 3, N)
        sidx = carve(E).bitcast(I32)
        rt8 = v3(carve(NT * 8), NT, 8)
        zero = carve(TAB)
        tern_t = carve(160)
        sh_at = used[0]
        sga = v3(carve(3 * S), 3, S)
        sh1 = v3(carve(3 * S), 3, S)
        carve(max(0, 2624 + 35328 - used[0]))
        moe_at = used[0]
        xe = v3(carve(4 * TAB), 4, TAB)
        xeT = carve(2 * D).rearrange("p (r c n) -> p r c n", r=2, c=DC)
        th = v3(carve(2 * INTER), 2, INTER)
        ge = v3(carve(2 * INTER), 2, INTER)
        hm = v3(carve(2 * INTER), 2, INTER)
        heT = carve(2 * 2 * P, IC).rearrange("p (r c n) -> p r c n", r=2, c=2)
        ye = v3(carve(2 * D), 2, D)
        den_at = used[0]
        den = carve(4 * 4 * 4 * TPB).rearrange("p (k t c a) -> p k t c a", k=4, t=TPB, c=4)
        carve(DC * FF)
        absd = carve(DC * FF, at=den_at)

        w5 = carve(5 * DC * D, at=moe_at).rearrange("p (k c n) -> p k c n", k=5, c=DC)
        used[0] = moe_at + 5 * DC * D
        yTs = v3(carve(2 * P), 2, P)
        state = v3(carve(2 * P), 2, P)
        kvt = carve(P)
        edrow = carve(H1)
        edcol = carve(2)
        urow = carve(H1)
        wall = carve(2)
        maat = carve(8)
        kdec = carve(H1)
        assert used[0] <= den_at
        gnt = carve(TPB * D, at=den_at)
        used[0] = early
        mix_at = used[0]
        mix = v3(carve(2 * DC * N), 2, DC * N)
        aring = v3(carve(8 * S, at=mix_at), 8, S)
        vpr_at = used[0]
        vpr = carve(2 * 8 * 160).rearrange("p (r g c) -> p r g c", r=2, g=8)
        dif = v3(carve(DC * N, at=vpr_at), DC, N)
        kq = carve(2 * 4 * N).rearrange("p (f q n) -> p f q n", f=2, q=4)
        rq_at = used[0]
        rq = carve(2 * 4 * N).rearrange("p (f h n) -> p f h n", f=2, h=4)
        hf = v3(carve(FC * N, at=rq_at), FC, N)
        rw = v3(carve(2 * N), 2, N)
        kn = v3(carve(NT * D), NT, D)
        vn = v3(carve(NT * D), NT, D)
        gn = v3(carve(NT * D), NT, D)
        wmask = carve(H1 * P).rearrange("p (h n) -> p h n", h=H1)
        assert used[0] <= moe_at, (used[0], moe_at)

        PS = [ctx.enter_context(nc.psum_tensor(f"ps{i}", [P, 512], F32)) for i in range(8)]

        s_x = [sem(f"x_loaded{i}") for i in range(B)]
        s_const = sem("const_loaded")
        s_wqkg = sem("wqkg_loaded")
        s_wv = sem("wv_loaded")
        s_wsh = sem("wshared_loaded")
        s_wo0 = sem("wo0_loaded")
        s_fill = sem("fills_done")
        s_var = sem("variance_ready")
        s_rstd = sem("rstd_ready")
        s_xn = sem("xn_ready")
        s_xnTp = sem("xnT_in_psum")
        s_xnT = sem("xnT_copied")
        s_kp = sem("k_in_psum")
        s_qp = sem("q_in_psum")
        s_lgp = sem("logits_in_psum")
        s_vp = sem("v_in_psum")
        s_v = sem("v_copied")
        s_keys = sem("keys_copied")
        s_q32 = sem("q_halves_copied")
        s_qp0 = sem("q_parts_first")
        s_qr = sem("q_rest")
        s_lgs = sem("logits_shifted")
        s_lge = sem("logits_exp")
        s_gate = sem("gates_ready")
        s_skTp = sem("slotkeys_in_psum")
        s_skT = sem("slotkeys_copied")
        s_skey = sem("slotkeys_ready")
        s_slots = sem("slots_ready")
        s_slotr = sem("slots_reversed")
        s_slotsTp = sem("slotsT_in_psum")
        s_sidx = sem("slot_tokens_ready")
        s_dk = sem("dk_parts_ready")
        s_vidx = sem("value_rows_ready")
        s_qpart = sem("q_parts_ready")
        s_qmp = sem("qT_in_psum")
        s_qm = sem("qmask_ready")
        s_shp = sem("shared_in_psum")
        s_sht = sem("shared_tanh")
        s_hs = sem("shared_hidden_ready")
        s_tab = sem("token_table_stored")
        s_vtab = sem("value_table_stored")
        s_kst = sem("dk_stored")
        s_skl = sem("sk_loaded")
        s_qst = sem("q_stored")
        s_qxl = sem("qx_loaded")
        s_vg0 = sem("first_values_gathered")
        s_vg = sem("values_gathered")
        s_xe = [sem(f"xe_gathered{i}") for i in range(4)]
        s_wm = [sem(f"expert_weights{i}") for i in range(4)]
        s_xeTp = sem("xeT_in_psum")
        s_xeT = sem("xeT_copied")
        s_hp = sem("h_in_psum")
        s_th = sem("tanh_done")
        s_ge = sem("silu_done")
        s_hm = sem("hidden_done")
        s_hTp = sem("hT_in_psum")
        s_hT = sem("hT_copied")
        s_yp = sem("y_in_psum")
        s_y = sem("y_scaled")
        s_sc = [sem(f"routed_added{i}") for i in range(2)]
        s_vpr = sem("values_placed")
        s_lp = sem("attn_logits_in_psum")
        s_ex = sem("attn_exp_done")
        s_av = sem("attn_out_in_psum")
        s_avT = sem("attn_out_copied")
        s_natp = sem("attn_nat_in_psum")
        s_nrm = sem("attn_norm_steps")
        s_oTp = sem("oT_in_psum")
        s_oT = sem("oT_copied")
        s_racc = sem("routed_loaded")
        s_res = sem("block0_sums_read")
        s_x1p = sem("x1_in_psum")
        s_x1 = sem("x1_ready")
        s_wff = sem("ff_weights_loaded")
        s_w5 = sem("w5_loaded")
        s_l1c = sem("block1_rows_loaded")
        s_gb = sem("gamma_beta_loaded")
        s_abs = sem("weight_abs_summed")
        s_absp = sem("weight_abs_in_psum")
        s_tern = sem("ternary_steps")
        s_tsum = sem("thresholds_ready")
        s_ed = sem("decay_exp")
        s_edn = sem("decay_negated")
        s_kdec = sem("key_decay_exp")
        s_wm1 = sem("decay_tables_exp")
        s_kqz = sem("k1_zeroed")
        s_wmc = sem("decay_mask_causal")
        s_ffp = sem("ff_in_psum")
        s_relu = sem("ff_relu_done")
        s_sq = sem("ff_square_done")
        s_mix = sem("mix_ready")
        s_kTp = sem("k1T_in_psum")
        s_kf = sem("k1T_whole_copied")
        s_kT = sem("k1T_copied")
        s_knp = sem("k1_nat_in_psum")
        s_kn = sem("k1_nat_scaled")
        s_ffd = sem("ff_down_in_psum")
        s_x2 = sem("x2_ready")
        s_rTp = sem("r1T_in_psum")
        s_rq = sem("r1_masked")
        s_rw = sem("r1_decayed")
        s_v1p = sem("v1_in_psum")
        s_v1 = sem("v1_copied")
        s_gp = sem("g1_in_psum")
        s_gt = sem("g1_tanh")
        s_g = sem("g1_ready")
        s_a1p = sem("scores_in_psum")
        s_a1 = sem("scores_masked")
        s_vd = sem("v1_placed")
        s_yTp = sem("yT_in_psum")
        s_yT = sem("yT_copied")
        s_kvp = sem("kv_in_psum")
        s_st = sem("state_ready")
        s_ynp = sem("y_nat_in_psum")
        s_yn = sem("y_nat_copied")
        s_gv = sem("group_var_ready")
        s_gs = sem("group_std_ready")
        s_gbh = sem("gamma_beta_halved")
        s_gm = sem("group_scaled")
        s_zs = sem("z_steps")
        s_z = sem("z_ready")
        s_zTp = sem("zT_in_psum")
        s_zT = sem("zT_copied")
        s_op = sem("out_in_psum")
        s_o = sem("out_ready")
        s_out = sem("out_stored")
        s_dve = sem("vector_chain")

        NPAIR = 3 * B
        NG = B * 8
        LAST = NG - 1
        x1_at = [(), (), (0,), (1, 2, 3)]
        oT_at = [(), (0, 1, 2), (3, 4, 5), (6, 7)]
        SLOTS = 4
        UNITS = B * TPB * 2

        block = ctx.enter_context(nc.Block())

        @block.sync
        def _(sp):
            for b in range(B):
                sp.dma_start(xs[:, b * TPB:(b + 1) * TPB, :], x_v[:, b * TPB:(b + 1) * TPB, :]).then_inc(s_x[b], 16)
            sp.dma_start(cst[:, :], consts).then_inc(s_const, 16)
            sp.dma_start(wqk, w_qk).then_inc(s_wqkg, 16)
            sp.dma_start(wg, w_gate).then_inc(s_wqkg, 16)
            sp.dma_start(wv, w_v).then_inc(s_wv, 16)
            sp.dma_start(wsh13, w_sh13).then_inc(s_wsh, 16)
            sp.dma_start(wsh2[:, 0:2, :], w_sh2[0:256, :].rearrange("(c p) n -> p c n", p=P)).then_inc(s_wsh, 16)
            sp.dma_start(wsh2[0:SROWS[2], 2, :], w_sh2[256:SHARED, :]).then_inc(s_wsh, 16)
            sp.dma_start(wo0, w_o0).then_inc(s_wo0, 16)
            sp.dma_start(w_fc1, w_fc).then_inc(s_wff, 16)
            sp.dma_start(w_pj1, w_pj).then_inc(s_wff, 16)
            sp.wait_ge(s_fill, 1)
            sp.dma_start(tok_tab[N:PAD, :], zero).then_inc(s_tab, 16)
            sp.wait_ge(s_v, NT)
            sp.dma_start(val_tab.rearrange("(t p h) d -> p t (h d)", p=P, h=H0), vnat).then_inc(s_vtab, 16)
            sp.wait_ge(s_qpart, 2)
            for side in range(2):
                for h4 in range(Q4):
                    for a in range(PARTS):
                        sp.dma_start(q_dram[a, side * Q4 + h4, :, :, :].rearrange("b g n -> g b n"),
                                     qparts[HG * h4:HG * (h4 + 1), side, a, :].rearrange("p (b n) -> p b n", b=B))\
                          .then_inc(s_qst, 16)

            def weights(u, group):
                sp.dma_start(w13r[u].rearrange("p c n -> p (c n)").unsqueeze(1), w13_v[u, :, group, :])\
                  .then_inc(s_wm[u], 16)
                sp.dma_start(w2r[u].rearrange("p c n -> p (c n)").unsqueeze(1), w2_v[u, :, group, :])\
                  .then_inc(s_wm[u], 16)

            w13_v = w_13.rearrange("(g u) p c n -> u p g (c n)", u=SLOTS)
            w2_v = w_2.rearrange("(g u) p c n -> u p g (c n)", u=SLOTS)
            sp.wait_ge(s_gate, 1)
            sp.dma_start(tok_tab[0:N, :].rearrange("(t p) d -> p t d", p=P), xn[:, :, :]).then_inc(s_tab, 16)
            sp.wait_ge(s_dk, 1)
            for b in range(B):
                for side in range(2):
                    n = (2 * b + side) * TOPK
                    sp.dma_start(k_dram[:, side, b, :, :].rearrange("a h j -> h a j"), dkparts[:, :, n:n + TOPK])\
                      .then_inc(s_kst, 16)
            sp.wait_ge(s_kst, 16 * 2 * B)
            sp.wait_ge(s_fill, 2)
            for side in range(2):
                for h4 in range(Q4):
                    for b in range(B):
                        first = side * Q4 + h4
                        sp.dma_start(sk[first:first + 17:8, b * HG:(b + 1) * HG, TOPK * h4:TOPK * (h4 + 1)],
                                     k_dram[:, side, b, HG * h4:HG * (h4 + 1), :]).then_inc(s_skl, 16)
            sp.wait_ge(s_skl, 16 * 2 * Q4 * B)
            for a in range(1, PARTS):
                rows = ROWS // PARTS
                sp.dma_start(sk[a * rows:(a + 1) * rows, :, :].rearrange("r g n -> r (g n)"),
                             sk[0:rows, :, :].rearrange("r g n -> r (g n)")).then_inc(s_skl, 16)
            q_v = q_dram.rearrange("a r b (g c) n -> a r (b g) (c n)", c=4)

            def q_rows(group):
                for a in range(PARTS):
                    for ap in range(PARTS):
                        first = (a * PARTS + ap) * 2 * Q4
                        sp.dma_start(qx[first:first + 2 * Q4, :, :].rearrange("r c n -> r (c n)").unsqueeze(1),
                                     q_v[a, :, group, :]).then_inc(s_qxl, 16)

            sp.wait_ge(s_qst, 16 * 2 * PARTS * Q4)
            q_rows(slice(0, 1))
            sp.wait_ge(s_qmp, 2)
            for u in range(SLOTS):
                weights(u, slice(0, 1))
            sp.wait_ge(s_lp, 4)
            q_rows(slice(1, 2))

            def next_weights(g, u, group):
                sp.wait_ge(s_yp, g * SLOTS + (u - SLOTS + 1))
                weights(u, group)

            with sp.Fori(1, E // SLOTS - 1) as g:
                for u in range(SLOTS):
                    next_weights(g, u, bass.ds(g, 1))
                    if u == 0:
                        sp.wait_ge(s_lp, g * 4 + 4)
                        q_rows(bass.ds(g + 1, 1))
            for u in range(SLOTS):
                next_weights(E // SLOTS - 1, u, slice(E // SLOTS - 1, E // SLOTS))
            sp.wait_ge(s_lp, NG * 4)
            for i in range(2):
                sp.wait_ge(s_sc[i], 16 * (1 + E // 2))
                sp.dma_start(racc[i], routed[i][0:N, :].rearrange("(t p) d -> p t d", p=P)).then_inc(s_racc, 16)
            sp.wait_ge(s_y, E + 1)
            sp.dma_start(w5, w_rkvgo).then_inc(s_w5, 16)
            sp.dma_start(edrow, td_row.partition_broadcast(P)).then_inc(s_l1c, 16)
            sp.dma_start(urow, u_row.partition_broadcast(P)).then_inc(s_l1c, 16)
            sp.dma_start(edcol, td_col).then_inc(s_l1c, 16)
            sp.dma_start(maat, maa).then_inc(s_l1c, 16)
            sp.dma_start(gb[:, 0, :], gamma.partition_broadcast(P)).then_inc(s_gb, 16)
            sp.dma_start(gb[:, 1, :], beta.partition_broadcast(P)).then_inc(s_gb, 16)
            for t in range(NT):
                sp.wait_ge(s_o, t + 1)
                sp.dma_start(out_v[:, t, :], xs[:, t, :]).then_inc(s_out, 16)
            sp.wait_ge(s_out, 16 * NT)

        @block.gpsimd
        def _(pool):
            nc.gpsimd.memset(zero, 0.0).then_inc(s_fill, 1)
            nc.gpsimd.memset(sk_all, 0.0).then_inc(s_fill, 1)
            nc.gpsimd.memset(vps, 0.0).then_inc(s_fill, 1)
            nc.gpsimd.memset(ones[:, :], 1.0)
            nc.gpsimd.memset(rsm[:, 2, :], -0.5).then_inc(s_fill, 1)
            pool.wait_ge(s_fill, 4)
            for h4 in range(Q4):
                last = nc.gpsimd.memset(vps[32 * h4:32 * h4 + 32, :, COLS * h4:COLS * h4 + 1], 1.0)
            last.then_inc(s_fill, 1)
            pool.wait_ge(s_fill, 5)
            for i in range(2):
                nc.gpsimd.dma_start(routed[i].rearrange("(r p) d -> p r d", p=P),
                                    zero[:, 0:D].rearrange("p (a d) -> p a d", a=1).broadcast_to([P, PAD // P, D]))\
                  .then_inc(s_sc[i], 16)

            def rsqrt(n, half):
                t = slice(half * TPB, (half + 1) * TPB)
                pool.wait_ge(s_var, B * n + half + 1)
                nc.gpsimd.tensor_tensor(rstd[:, 1, t], rstd[:, 0, t], rsm[:, 2, t], ALU.pow).then_inc(s_rstd, 1)

            for half in range(B):
                rsqrt(0, half)

            def value_gather(n):
                group, rest = divmod(n, 8)
                if n == NV // B:
                    pool.wait_ge(s_vidx, 2)
                side, c = divmod(rest, 4)
                b, g4 = divmod(group, 8)
                col = (2 * b + side) * HG + 4 * g4 + c
                nc.gpsimd.indirect_dma_start(vals[:, group, side, c, :], None, val_tab,
                                             bass.IndirectOffsetOnAxis(ap=vidxT[:, col:col + 1], axis=0))\
                  .then_inc(s_vg if n >= 8 else s_vg0, 16)

            def token_gather(e):
                if e >= SLOTS:
                    pool.wait_ge(s_y, e - SLOTS + 2)
                nc.gpsimd.indirect_dma_start(xe[:, e % SLOTS, :], None, tok_tab,
                                             bass.IndirectOffsetOnAxis(ap=sidx[:, e:e + 1], axis=0))\
                  .then_inc(s_xe[e % SLOTS], 16)

            def routed_add(e):
                pool.wait_ge(s_y, e + 2)
                pool.wait_ge(s_sc[e % 2], 16 * (1 + e // 2))
                nc.gpsimd.indirect_dma_start(routed[e % 2], bass.IndirectOffsetOnAxis(ap=sidx[:, e:e + 1], axis=0),
                                             ye[:, e % 2, :], None, compute_op=ALU.add)\
                  .then_inc(s_sc[e % 2], 16)

            NV = B * 2 * HG
            FIRST, SECOND = 47, 64
            pool.wait_ge(s_vidx, 1)
            pool.wait_ge(s_vtab, 16)
            done = 0
            while done < FIRST:
                value_gather(done)
                done += 1
            pool.wait_ge(s_sidx, 1)
            pool.wait_ge(s_tab, 32)
            for e in range(SLOTS):
                token_gather(e)
            while done < SECOND:
                value_gather(done)
                done += 1
            for e in range(E):
                routed_add(e)
                if e + SLOTS < E:
                    token_gather(e + SLOTS)
                for _ in range(2 if e % 4 == 1 else 1):
                    if done < NV:
                        value_gather(done)
                        done += 1
            assert done == NV
            for half in range(B):
                rsqrt(1, half)
            pool.wait_ge(s_res, 1)
            nc.gpsimd.memset(kq, 0.0).then_inc(s_kqz, 1)
            pool.wait_ge(s_wm1, 1)
            nc.gpsimd.affine_select(out=wmask, in_=wmask, compare_op=ALU.is_ge, fill=0.0, base=-1,
                                    pattern=[[0, H1], [1, P]], channel_multiplier=-1).then_inc(s_wmc, 1)
            pool.wait_ge(s_mix, 4)
            pool.wait_ge(s_v1, NT)
            nc.gpsimd.memset(vpr, 0.0).then_inc(s_vd, 1)
            pool.wait_ge(s_vd, 1)

            def gated(t):
                z = xn[:, t, 0:D]
                if t == 0:
                    pool.wait_ge(s_gbh, 1)
                    pool.wait_ge(s_g, NT)
                pool.wait_ge(s_gm, t + 1)
                nc.gpsimd.tensor_tensor(z, z, gb[:, 0, :], ALU.mult).then_inc(s_zs, 1)
                pool.wait_ge(s_zs, 2 * t + 1)
                nc.gpsimd.tensor_tensor(z, z, gb[:, 1, :], ALU.add).then_inc(s_zs, 1)
                pool.wait_ge(s_zs, 2 * t + 2)
                nc.gpsimd.tensor_tensor(z, z, gn[:, t, :], ALU.mult).then_inc(s_z, 1)

            for t in range(NT):
                if t >= 2:
                    pool.wait_ge(s_yTp, 2 * (t - 1))
                dst = vpr[:, t % 2, :, :].rearrange("p g (a c) -> p g a c", a=4)[:, :, :, 0:HN]
                nc.gpsimd.tensor_copy(dst, vn[:, t, :].rearrange("p (g a c) -> p g a c", g=8, a=4)).then_inc(s_vd, 1)
                if t >= 4:
                    gated(t - 4)
            for t in range(NT - 4, NT):
                gated(t)

        @block.scalar
        def _(act):
            def xnT_copies(base, tiles=range(NT)):
                for t in tiles:
                    act.wait_ge(s_xnTp, base + t + 1)
                    nc.scalar.activation(xnT[:, :, t * P:(t + 1) * P],
                                         PS[t % 2][:, 0:D].rearrange("p (c n) -> p c n", c=DC), ACT.Copy)\
                      .then_inc(s_xnT, 1)

            for b in range(B):
                xnT_copies(0, range(b * TPB, (b + 1) * TPB))
                act.wait_ge(s_kp, b + 1)
                nc.scalar.activation(keys[:, b, 0, :], PS[2 + b][:, ::-1], ACT.Copy)
                nc.scalar.activation(keys[:, b, 1, :], PS[2 + b][:, :], ACT.Copy, scale=-1.0).then_inc(s_keys, 1)
            for t in range(NT):
                act.wait_ge(s_vp, t + 1)
                nc.scalar.activation(vnat[:, t, :], PS[(0, 1, 7)[t % 3]][:, 0:D], ACT.Copy).then_inc(s_v, 1)
            for b in range(B):
                act.wait_ge(s_qp, b + 1)
                for side in range(2):
                    last = nc.scalar.activation(q32[:, side, b * S:(b + 1) * S], PS[4 + b][:, :], ACT.Relu,
                                                scale=1.0 - 2.0 * side)
                last.then_inc(s_q32, 1)
            act.wait_ge(s_q32, B)
            nc.scalar.activation(qparts[:, :, 0, :], q32, ACT.Copy).then_inc(s_qp0, 1)
            act.wait_ge(s_qr, 2)
            nc.scalar.activation(qparts[:, :, 1, :], qrest, ACT.Copy).then_inc(s_qp0, 1)
            act.wait_ge(s_lgs, 1)
            nc.scalar.activation(sc[:, :, 0:E], lg, ACT.Exp).then_inc(s_lge, 1)
            for k in range(2):
                act.wait_ge(s_qmp, k + 1)
                nc.scalar.activation(qmask[:, 4 * k:4 * k + 4, :], PS[k][:, :].rearrange("p (t h) -> p t h", t=4),
                                     ACT.Sign).then_inc(s_qm, 1)
            act.wait_ge(s_wff, 32)
            nc.scalar.activation(absd, w_fc1.rearrange("p c n -> p (c n)"), ACT.Abs, accum_out=tsum[:, 0:1])\
              .then_inc(s_abs, 1)
            act.wait_ge(s_abs, 1)
            nc.scalar.activation(absd, w_pj1.rearrange("p c n -> p (c n)"), ACT.Abs, accum_out=tsum[:, 1:2])\
              .then_inc(s_abs, 1)

            def shared_tanh(i):
                rows = SROWS[i // B]
                act.wait_ge(s_shp, i + 1)
                if i == 3:
                    act.wait_ge(s_vtab, 16)
                if i < 3:
                    nc.scalar.activation(sh1[0:rows, i, :], PS[2 * i][0:rows, :], ACT.Copy)
                    nc.scalar.activation(hs[0:rows, i // B, (i % B) * S:(i % B + 1) * S], PS[2 * i + 1][0:rows, :],
                                         ACT.Copy)
                nc.scalar.activation((sga, sgb)[i // 3][0:rows, i % 3, :], PS[2 * (i % 3)][0:rows, :], ACT.Tanh,
                                     scale=0.5).then_inc(s_sht, 1)

            act.wait_ge(s_skTp, 1)
            nc.scalar.activation(slotk, PS[6][:, :], ACT.Copy).then_inc(s_skT, 1)
            for i in range(NPAIR):
                shared_tanh(i)
            act.wait_ge(s_slots, 1)
            nc.scalar.activation(slotr, slots[:, ::-1], ACT.Copy).then_inc(s_slotr, 1)

            def tokens_in(e, u):
                act.wait_ge(s_xeTp, e + 1)
                nc.scalar.activation(xeT[:, u % 2, :, :], PS[0][:, 0:D].rearrange("p (c n) -> p c n", c=DC),
                                     ACT.Copy).then_inc(s_xeT, 1)

            def tanh(e, u):
                act.wait_ge(s_hp, e + 1)
                nc.scalar.activation(th[:, u % 2, :], PS[1][:, 0:INTER], ACT.Tanh, scale=0.5).then_inc(s_th, 1)

            def scale_out(e, u, free, gate):
                act.wait_ge(s_yp, e + 1)
                act.wait_ge(s_sc[u % 2], free)
                nc.scalar.activation(ye[:, u % 2, :], PS[3][:, 0:D], ACT.Copy, scale=gate).then_inc(s_y, 1)

            def exps(g, u):
                for c in (2 * u, 2 * u + 1):
                    act.wait_ge(s_lp, g * 4 + (c + 1))
                    nc.scalar.activation(ex[:, c, :], PS[4 + c % 2][:, :], ACT.Exp).then_inc(s_ex, 1)

            def place_values(g, group, first=False):
                if first:
                    act.wait_ge(s_vg0, 128)
                else:
                    act.wait_ge(s_vg, (g - 1) * 128 + 128)
                for h4 in range(Q4):
                    r = slice(32 * h4, 32 * h4 + 32)
                    c = COLS * h4 + 1
                    last = nc.scalar.activation(
                        vps[r, :, c:c + 2 * DV].rearrange("p g (s d) -> p s g d", s=2),
                        vals[r, group, :, :, :].rearrange("p k s g d -> p (k s) g d"), ACT.Copy)
                    if first and h4 == 0:
                        last.then_inc(s_y, 1)
                last.then_inc(s_vpr, 1)

            def unit(g, u, gate, group):
                if g is LAST:
                    for t in oT_at[u]:
                        oT_copy(t)
                elif u < 2:
                    exps(g + 1, u)
                if g is not LAST or u + 1 < SLOTS:
                    tanh(g * SLOTS + (u + 1), u + 1)
                if g is not LAST and u == 1:
                    place_values(g + 1, group)
                if g is not LAST or u + 2 < SLOTS:
                    tokens_in(g * SLOTS + (u + 2), u)
                scale_out(g * SLOTS + u, u, g * 32 + 16 * (1 + u // 2), gate)

            def oT_copy(t):
                act.wait_ge(s_oTp, t + 1)
                nc.scalar.activation(oT[:, :, t * P:(t + 1) * P],
                                     PS[6 + t % 2][:, 0:D].rearrange("p (c n) -> p c n", c=DC),
                                     ACT.Copy).then_inc(s_oT, 1)

            act.wait_ge(s_fill, 5)
            gates = xe[:, :, D:TAB].rearrange("p r (g u) -> p r u g", u=SLOTS)
            place_values(0, slice(0, 1), first=True)
            tokens_in(0, 0)
            tanh(0, 0)
            exps(0, 0)
            exps(0, 1)
            tokens_in(1, 1)
            with act.Fori(0, LAST) as g:
                for u in range(SLOTS):
                    unit(g, u, gates[:, u, u, bass.ds(g, 1)], bass.ds(g + 1, 1))
            for u in range(SLOTS):
                unit(LAST, u, gates[:, u, u, LAST:NG], None)

            act.wait_ge(s_l1c, 64)
            nc.scalar.activation(edrow, edrow, ACT.Exp).then_inc(s_ed, 1)
            nc.scalar.activation(edcol, edcol, ACT.Exp).then_inc(s_ed, 1)
            for b in range(B):
                xnT_copies(NT, range(b * TPB, (b + 1) * TPB))
                if b == 0:
                    act.wait_ge(s_edn, 1)
                    nc.scalar.activation(kdec, edrow, ACT.Exp, scale=const("jdec")).then_inc(s_kdec, 1)
                    nc.scalar.activation(wall, edcol, ACT.Exp, scale=float(P))
                    for f in range(2):
                        nc.scalar.activation(wb[:, f, :], const("steps"), ACT.Exp, scale=edcol[:, f:f + 1])
                if b == 0:
                    act.wait_ge(s_res, 1)
                for f in range(FC):
                    i = b * FC + f
                    act.wait_ge(s_ffp, i + 1)
                    nc.scalar.activation(hf[:, f, b * S:(b + 1) * S], PS[2 + i % 6][:, :], ACT.Relu).then_inc(s_relu, 1)
                    for h in range(4 * i, min(4 * i + 4, H1)):
                        last = nc.scalar.activation(wmask[:, h, :], const("pdist"), ACT.Exp, scale=edrow[:, h:h + 1])
                        if h == H1 - 1:
                            last.then_inc(s_wm1, 1)
            act.wait_ge(s_kqz, 1)
            for i in range(4):
                f, n = divmod(i, 2)
                act.wait_ge(s_kTp, i + 1)
                for q in range(4):
                    r = slice(32 * q, 32 * q + 32)
                    last = nc.scalar.activation(kq[r, f, q, n * S:(n + 1) * S], PS[i][r, :], ACT.Copy)
                last.then_inc(s_kT, 1)
            act.wait_ge(s_x2, NT)
            for i in range(4):
                f, n = divmod(i, 2)
                act.wait_ge(s_rTp, i + 1)
                for h in range(4):
                    last = nc.scalar.activation(rq[:, f, h, n * S:(n + 1) * S], PS[i][:, :], ACT.Copy,
                                                scale=const("quad")[:, h:h + 1])
                last.then_inc(s_rq, 1)
            for t in range(NT):
                act.wait_ge(s_v1p, t + 1)
                nc.scalar.activation(vn[:, t, :], PS[4 + t % 4][:, 0:D], ACT.Copy).then_inc(s_v1, 1)
            for t in range(NT):
                act.wait_ge(s_gp, t + 1)
                nc.scalar.activation(gn[:, t, :], PS[t % 4][:, 0:D], ACT.Tanh, scale=0.5).then_inc(s_gt, 1)
            def group_std(t):
                act.wait_ge(s_gv, t + 1)
                g = [gst[:, k, (t % 4) * H1:(t % 4 + 1) * H1] for k in range(2)]
                nc.scalar.activation(g[1], g[0], ACT.Sqrt).then_inc(s_gs, 1)

            for t in range(NT):
                for f in range(2):
                    u = 2 * t + f
                    act.wait_ge(s_yTp, u + 1)
                    if t >= 1 and f == 0:
                        act.wait_ge(s_ynp, t)
                    nc.scalar.activation(yTs[:, f, 0:P], PS[4 + u % 2][:, 0:P], ACT.Copy).then_inc(s_yT, 1)
                    if t >= 2 and f == 0:
                        group_std(t - 2)
                act.wait_ge(s_ynp, t + 1)
                nc.scalar.activation(xn[:, t, 0:D], PS[7][:, 0:D], ACT.Copy).then_inc(s_yn, 1)
            group_std(NT - 2)
            for t in range(NT):
                if t == 4:
                    group_std(NT - 1)
                act.wait_ge(s_zTp, t + 1)
                nc.scalar.activation(xnT[:, :, t * P:(t + 1) * P], PS[t % 2][:, 0:D].rearrange("p (c n) -> p c n", c=DC),
                                     ACT.Copy).then_inc(s_zT, 1)

        @block.vector
        def _(dve):
            steps = [0]

            def note(ins):
                steps[0] += 1
                ins.then_inc(s_dve, 1)

            def settle():
                dve.wait_ge(s_dve, steps[0])

            def link(ins):
                note(ins)
                settle()

            def wide(ap, *shape):
                return ap.broadcast_to([P, *shape])

            def tiles_of(half):
                return range(half * TPB, (half + 1) * TPB)

            def ln_stats(half):
                for t in tiles_of(half):
                    note(nc.vector.bn_stats(stats[:, t, :], xs[:, t, :]))
                settle()
                ln_aggregate(half)

            def ln_aggregate(half):
                for t in tiles_of(half):
                    note(nc.vector.bn_aggr(mv[:, t, :], stats[:, t, :]))
                settle()
                tiles = slice(half * TPB, (half + 1) * TPB)
                nc.vector.tensor_scalar(rstd[:, 0, tiles], mv[:, tiles, 1], LN_EPS, None, ALU.add).then_inc(s_var, 1)

            def ln_apply(n, half):
                dve.wait_ge(s_rstd, B * n + half + 1)
                for t in tiles_of(half):
                    nc.vector.tensor_scalar(xn[:, t, 0:D], xs[:, t, :], mv[:, t, 0:1], rstd[:, 1, t:t + 1],
                                            ALU.subtract, ALU.mult).then_inc(s_xn, 1)

            for half in range(B):
                dve.wait_ge(s_x[half], 16)
                ln_stats(half)
            for half in range(B):
                ln_apply(0, half)
            dve.wait_ge(s_const, 16)
            lp = PS[6][:, :].rearrange("p (t e) -> p t e", t=NT)

            def router_shift():
                dve.wait_ge(s_lgp, 1)
                note(nc.vector.memset(sc[:, :, E:E + 2], -1.0))
                link(nc.vector.tensor_reduce(rsm[:, 0, :], lp, AX, ALU.max))
                nc.vector.tensor_tensor(lg, lp, rsm[:, 0, :].unsqueeze(2).broadcast_to([P, NT, E]), ALU.subtract)\
                  .then_inc(s_lgs, 1)

            def q_rest():
                dve.wait_ge(s_qp0, 1)
                for side in range(2):
                    nc.vector.tensor_tensor(qrest[:, side, :], q32[:, side, :], qparts[:, side, 0, :], ALU.subtract)\
                      .then_inc(s_qr, 1)

            for b in range(B):
                dve.wait_ge(s_keys, b + 1)
                for r in range(TOPK // 8):
                    c = slice(8 * r, 8 * r + 8)
                    for side in range(2):
                        note(nc.vector.max(topv[:, b, side, c], keys[:, b, side, :]))
                    settle()
                    for side in range(2):
                        note(nc.vector.max_index(topi[:, b, side, c], topv[:, b, side, c], keys[:, b, side, :]))
                    settle()
                    if r < TOPK // 8 - 1:
                        for side in range(2):
                            note(nc.vector.match_replace(keys[:, b, side, :], topv[:, b, side, c],
                                                         keys[:, b, side, :], -3.0e38))
                        settle()
                    if b == 1 and r == 1:
                        q_rest()
                for side in range(2):
                    n = 2 * b + side
                    note(nc.vector.tensor_scalar(vidx[:, b, side, :], topi[:, b, side, :], float(H0 if side else -H0),
                                                 const("vrow")[:, n:n + 1], ALU.mult, ALU.add))
                settle()
                nc.vector.transpose(vidxT[:, b * 2 * HG:(b + 1) * 2 * HG].bitcast(U32),
                                    vidx[:, b, :, :].rearrange("p s n -> p (s n)").bitcast(U32)).then_inc(s_vidx, 1)
                if b == 0:
                    router_shift()
            dve.wait_ge(s_qp0, 2)
            for side in range(2):
                nc.vector.tensor_tensor(qparts[:, side, 2, :], qrest[:, side, :], qparts[:, side, 1, :], ALU.subtract)\
                  .then_inc(s_qpart, 1)
            dve.wait_ge(s_lge, 1)
            link(nc.vector.tensor_reduce(rsm[:, 0, :], sc[:, :, 0:E], AX, ALU.add))
            link(nc.vector.reciprocal(rsm[:, 1, :], rsm[:, 0, :]))
            link(nc.vector.tensor_tensor(sc[:, :, 0:E], sc[:, :, 0:E],
                                         rsm[:, 1, :].unsqueeze(2).broadcast_to([P, NT, E]), ALU.mult))
            for t in range(NT):
                note(nc.vector.max(rt8[:, t, :], sc[:, t, 0:E]))
            settle()
            link(nc.vector.memset(rt8[:, :, KSEL:8], -1.0))
            for t in range(NT):
                note(nc.vector.match_replace(sr[:, t, :], rt8[:, t, :], sc[:, t, :], -2.0))
            settle()
            link(nc.vector.tensor_scalar(lg, sr[:, :, 0:E], -1.5, None, ALU.is_lt))
            for b in range(B):
                ins = nc.vector.tensor_tensor(skey[:, b::B, :], lg[:, b * TPB:(b + 1) * TPB, :],
                                              const("tokinv")[:, b * TPB:(b + 1) * TPB].unsqueeze(2)
                                              .broadcast_to([P, TPB, E]), ALU.mult)
            ins.then_inc(s_skey, 1)
            nc.vector.tensor_tensor(xn[:, :, D:TAB], lg, sc[:, :, 0:E], ALU.mult).then_inc(s_gate, 1)
            top = topv.rearrange("p b s n -> p (b s) n")
            link(nc.vector.tensor_tensor(dkf.rearrange("p (x n) -> p x n", n=TOPK), top,
                                         top[:, :, 0:1].broadcast_to([P, B * 2, TOPK]), ALU.subtract))

            def split(src, parts):
                link(nc.vector.tensor_copy(parts[0], src))
                link(nc.vector.tensor_tensor(src, src, parts[0], ALU.subtract))
                link(nc.vector.tensor_copy(parts[1], src))
                return nc.vector.tensor_tensor(parts[2], src, parts[1], ALU.subtract)

            split(dkf, [dkparts[:, a, :] for a in range(PARTS)]).then_inc(s_dk, 1)

            dve.wait_ge(s_skT, 1)
            for r in range(CAP // 8):
                c = slice(8 * r, 8 * r + 8)
                link(nc.vector.max(slots[:, c], slotk))
                if r < CAP // 8 - 1:
                    link(nc.vector.match_replace(slotk, slots[:, c], slotk, 0.0))
            nc.vector.tensor_scalar(slots[:, 0:1], slots[:, 0:1], 0.0, None, ALU.add).then_inc(s_slots, 1)
            dve.wait_ge(s_slotsTp, 1)
            key = nat_tmp[:, 0, :]
            link(nc.vector.tensor_scalar(nat_tmp[:, 1, :], PS[6][:, 0:E], 0.0, None, ALU.is_equal))
            link(nc.vector.tensor_tensor(nat_tmp[:, 1, :], PS[6][:, P + E:2 * P], nat_tmp[:, 1, :], ALU.mult))
            link(nc.vector.tensor_tensor(key, PS[6][:, 0:E], nat_tmp[:, 1, :], ALU.add))
            link(nc.vector.tensor_scalar(nat_tmp[:, 1, :], key, 0.0, const("slot"), ALU.is_equal, ALU.mult))
            link(nc.vector.tensor_scalar(key, key, -1.0, float(N), ALU.mult, ALU.add))
            nc.vector.tensor_tensor(sidx, key, nat_tmp[:, 1, :], ALU.add).then_inc(s_sidx, 1)

            def shared_hidden(i):
                rows, k = SROWS[i // B], 2 * (i % 3)
                h = hs[0:rows, i // B, (i % B) * S:(i % B + 1) * S]
                dve.wait_ge(s_sht, i + 1)
                if i < 3:
                    g = sga[0:rows, i, :]
                    link(nc.vector.scalar_tensor_tensor(g, g, 1.0, sh1[0:rows, i, :], ALU.add, ALU.mult))
                    nc.vector.scalar_tensor_tensor(h, g, 0.5, h, ALU.mult, ALU.mult).then_inc(s_hs, 1)
                else:
                    link(nc.vector.scalar_tensor_tensor(h, sgb[0:rows, i - 3, :], 1.0, PS[k][0:rows, :],
                                                        ALU.add, ALU.mult))
                    nc.vector.scalar_tensor_tensor(h, h, 0.5, PS[k + 1][0:rows, :], ALU.mult, ALU.mult)\
                      .then_inc(s_hs, 1)

            for i in range(3, NPAIR):
                shared_hidden(i)
            dve.wait_ge(s_absp, 1)
            link(nc.vector.tensor_scalar(tsum[:, 2:4], PS[7][:, 0:2], 1.0 / (FF * D), 1e-5, ALU.mult, ALU.max))
            link(nc.vector.tensor_scalar(tsum[:, 4:6], tsum[:, 2:4], 0.7, None, ALU.mult))
            link(nc.vector.tensor_scalar(tsum[:, 6:8], tsum[:, 4:6], -1.0, None, ALU.mult))
            nc.vector.tensor_scalar(tsum[:, 2:4], tsum[:, 2:4], -1.0, None, ALU.mult).then_inc(s_tsum, 1)
            dve.wait_ge(s_tsum, 1)
            for i in range(3):
                shared_hidden(i)

            def hidden(e, u):
                dve.wait_ge(s_th, e + 1)
                nc.vector.scalar_tensor_tensor(ge[:, u % 2, :], th[:, u % 2, :], 1.0, PS[1][:, 0:INTER],
                                               ALU.add, ALU.mult).then_inc(s_ge, 1)
                dve.wait_ge(s_ge, e + 1)
                nc.vector.scalar_tensor_tensor(hm[:, u % 2, :], ge[:, u % 2, :], 0.5,
                                               PS[1][:, INTER:2 * INTER], ALU.mult, ALU.mult).then_inc(s_hm, 1)

            def hidden_T(e, u):
                dve.wait_ge(s_hTp, e + 1)
                nc.vector.tensor_copy(heT[:, u % 2, :, :], PS[2][0:IC, 0:2 * P].rearrange("p (c n) -> p c n", c=2))\
                  .then_inc(s_hT, 1)

            def out_copy(g):
                dve.wait_ge(s_av, g + 1)
                nc.vector.tensor_copy(avT, PS[6][:, :]).then_inc(s_avT, 1)

            NORM = 9

            def normalise(b, g, k, chosen):
                if chosen.start == 0:
                    dve.wait_ge(s_natp, g + 1)
                tiles = slice(b * TPB, (b + 1) * TPB)
                nat = PS[7][:, :].rearrange("p (t c m) -> p t c m", t=TPB, c=4)

                def part(i):
                    return nat[:, :, :, i:i + 3 * COLS + 1:COLS]

                def of_group(ap):
                    return ap.rearrange("p t (a g c) -> p t g c a", a=Q4, c=4)[:, tiles, k, :, :]\
                             .rearrange("p t g c a -> p t (g c) a")

                sel = of_group(qmask)
                o = [of_group(onat[:, :, d::DV]) for d in range(DV)]
                w, w_top, w_bottom, w_more = [den[:, i] for i in range(4)]
                V = nc.vector
                for step, (make, settled) in enumerate((
                        (lambda: V.reciprocal(w, part(0)), 0),
                        (lambda: V.tensor_tensor(w_top, w, sel, ALU.mult), 1),
                        (lambda: V.tensor_tensor(w_bottom, w, w_top, ALU.subtract), 2),
                        (lambda: V.tensor_tensor(o[0], part(1), w_top, ALU.mult), 2),
                        (lambda: V.tensor_tensor(o[1], part(2), w_top, ALU.mult), 2),
                        (lambda: V.tensor_tensor(w, part(3), w_bottom, ALU.mult), 3),
                        (lambda: V.tensor_tensor(w_more, part(4), w_bottom, ALU.mult), 3),
                        (lambda: V.tensor_tensor(o[0], o[0], w, ALU.add), 6),
                        (lambda: V.tensor_tensor(o[1], o[1], w_more, ALU.add), 7))):
                    if not chosen.start <= step < chosen.stop:
                        continue
                    if settled:
                        dve.wait_ge(s_nrm, g * NORM + settled)
                    make().then_inc(s_nrm, 1)

            ff_w = [w.rearrange("p c n -> p (c n)").rearrange("p (k n) -> p k n", k=8) for w in (w_fc1, w_pj1)]

            def ternary(b, g, col):
                w = ff_w[b][:, col, :].rearrange("p k n -> p (k n)")
                for step, make in enumerate((
                        lambda: nc.vector.tensor_scalar(tern_t, w, tsum[:, 4 + b:5 + b], None, ALU.is_gt),
                        lambda: nc.vector.scalar_tensor_tensor(tern_t, w, tsum[:, 6 + b:7 + b], tern_t,
                                                               ALU.is_lt, ALU.subtract),
                        lambda: nc.vector.scalar_tensor_tensor(tern_t, tern_t, tsum[:, 2 + b:3 + b], w,
                                                               ALU.mult, ALU.subtract),
                        lambda: nc.vector.tensor_tensor(w, tern_t, w, ALU.add))):
                    make().then_inc(s_tern, 1)
                    dve.wait_ge(s_tern, g * 4 + (step + 1))

            def x1_add(t):
                dve.wait_ge(s_x1p, t + 1)
                nc.vector.tensor_tensor(xs[:, t, :], PS[4 + t % 2][:, 0:D], xs[:, t, :], ALU.add).then_inc(s_x1, 1)

            def group(g, b, k, after=None):
                for u in range(SLOTS):
                    if g is LAST and u == 3:
                        for t in range(3):
                            x1_add(t)
                    hidden_T(g * SLOTS + u, u)
                    if g is not LAST and u == 2:
                        out_copy(g + 1)
                    if g is not LAST or u + 1 < SLOTS:
                        hidden(g * SLOTS + (u + 1), u + 1)
                    if u == 0:
                        normalise(b, g, k, slice(3, NORM))
                    if g is not LAST and u == 3:
                        normalise(*after, slice(0, 3))
                    if u == 1:
                        ternary(b, g, k)

            hidden(0, 0)
            out_copy(0)
            normalise(0, 0, slice(0, 1), slice(0, 3))
            with dve.Fori(0, 7) as k:
                group(k, 0, bass.ds(k, 1), (0, k + 1, bass.ds(k + 1, 1)))
            group(7, 0, slice(7, 8), (1, 8, slice(0, 1)))
            with dve.Fori(0, 7) as k:
                group(k + 8, 1, bass.ds(k, 1), (1, k + 9, bass.ds(k + 1, 1)))
            group(LAST, 1, slice(7, 8))

            def routed_adds(half):
                tiles = slice(half * TPB, (half + 1) * TPB)
                for i in range(2):
                    link(nc.vector.tensor_tensor(xs[:, tiles, :], xs[:, tiles, :], racc[i][:, tiles, :], ALU.add))

            for t in range(3, TPB + 2):
                x1_add(t)
            dve.wait_ge(s_x1, TPB + 2)
            dve.wait_ge(s_racc, 32)
            routed_adds(0)
            ln_stats(0)
            for t in range(TPB + 2, NT):
                x1_add(t)
            dve.wait_ge(s_x1, NT)
            dve.wait_ge(s_ed, 2)
            note(nc.vector.tensor_scalar(edrow, edrow, 1e30, -1.0, ALU.min, ALU.mult))
            nc.vector.tensor_scalar(edcol, edcol, 1e30, -1.0, ALU.min, ALU.mult).then_inc(s_edn, 1)
            ln_apply(1, 0)
            routed_adds(1)
            for t in tiles_of(1):
                nc.vector.bn_stats(stats[:, t, :], xs[:, t, :]).then_inc(s_res, 1)
            dve.wait_ge(s_res, TPB)
            ln_aggregate(1)
            ln_apply(1, 1)
            def square(i):
                dve.wait_ge(s_relu, i + 1)
                h = hf[:, i % FC, (i // FC) * S:(i // FC + 1) * S]
                nc.vector.tensor_tensor(h, h, h, ALU.mult).then_inc(s_sq, 1)

            for i in range(FC):
                square(i)
            dve.wait_ge(s_xnT, 2 * NT)
            for c in range(DC):
                src = xnT[:, c, :].rearrange("p (b n) -> p b n", b=B)
                dst = dif[:, c, :].rearrange("p (b n) -> p b n", b=B)
                note(nc.vector.tensor_tensor(dst[:, :, 1:S], src[:, :, 0:S - 1], src[:, :, 1:S], ALU.subtract))
                note(nc.vector.tensor_scalar(dst[:, :, 0:1], src[:, :, 0:1], -1.0, None, ALU.mult))
            settle()

            def mixture(k):
                for c in range(DC):
                    ins = nc.vector.scalar_tensor_tensor(mix[:, k % 2, c * N:(c + 1) * N], dif[:, c, :],
                                                         maat[:, 2 * k + c:2 * k + c + 1], xnT[:, c, :],
                                                         ALU.mult, ALU.add)
                    if c < DC - 1:
                        note(ins)
                ins.then_inc(s_mix, 1)

            dve.wait_ge(s_l1c, 64)
            mixture(0)
            mixture(1)
            for i in range(FC, 2 * FC):
                square(i)
            for i in range(4):
                f, n = divmod(i, 2)
                dve.wait_ge(s_kT, i + 1)
                nc.vector.tensor_copy(rw[:, f, n * S:(n + 1) * S], PS[i][:, :]).then_inc(s_kf, 1)
            mixture(2)
            dve.wait_ge(s_gb, 32)
            nc.vector.tensor_scalar(gb[:, :, :], gb[:, :, :], 0.5, None, ALU.mult).then_inc(s_gbh, 1)
            for t in range(NT):
                dve.wait_ge(s_ffd, t + 1)
                nc.vector.tensor_tensor(xs[:, t, :], PS[4 + t % 4][:, 0:D], xs[:, t, :], ALU.add).then_inc(s_x2, 1)
            dve.wait_ge(s_edn, 1)
            for t in range(NT):
                dve.wait_ge(s_knp, t + 1)
                if t == 0:
                    dve.wait_ge(s_kdec, 1)
                nc.vector.tensor_tensor(kn[:, t, :].rearrange("p (h n) -> p h n", n=HN),
                                        PS[4 + t % 4][:, 0:D].rearrange("p (h n) -> p h n", n=HN),
                                        kdec.unsqueeze(2).broadcast_to([P, H1, HN]), ALU.mult).then_inc(s_kn, 1)
            dve.wait_ge(s_rTp, 4)
            mixture(3)
            for i in range(4):
                f, n = divmod(i, 2)
                dve.wait_ge(s_rq, i + 1)
                nc.vector.tensor_tensor(rw[:, f, n * S:(n + 1) * S].rearrange("p (t n) -> p t n", n=P),
                                        PS[i][:, :].rearrange("p (t n) -> p t n", n=P),
                                        wb[:, f, :].unsqueeze(1).broadcast_to([P, TPB, P]), ALU.mult).then_inc(s_rw, 1)
            dve.wait_ge(s_wmc, 1)
            for h in range(H1):
                note(nc.vector.scalar_tensor_tensor(wmask[:, h, :], ident, urow[:, h:h + 1], wmask[:, h, :],
                                                    ALU.mult, ALU.add))
            settle()
            for t in range(NT):
                dve.wait_ge(s_gt, t + 1)
                nc.vector.scalar_tensor_tensor(gn[:, t, :], gn[:, t, :], 1.0, PS[t % 4][:, 0:D], ALU.add, ALU.mult)\
                  .then_inc(s_g, 1)

            def state_update(u):
                f = u % 2
                dve.wait_ge(s_kvp, (u // 8) * 6 + u % 8 + 1)
                link(nc.vector.tensor_tensor(kvt, PS[6][:, 0:P], const("heads"), ALU.mult))
                nc.vector.scalar_tensor_tensor(state[:, f, :], state[:, f, :], wall[:, f:f + 1], kvt,
                                               ALU.mult, ALU.add).then_inc(s_st, 1)

            def norm_parts(t):
                y = xn[:, t, 0:D].rearrange("p (h n) -> p h n", n=HN)
                g = [gst[:, k, (t % 4) * H1:(t % 4 + 1) * H1] for k in range(3)]
                sq = gnt[:, (t % 4) * D:(t % 4 + 1) * D].rearrange("p (h n) -> p h n", n=HN)
                return y, g, sq

            def per_head(g):
                return g.unsqueeze(2).broadcast_to([P, H1, HN])

            def group_means(t):
                y, g, _ = norm_parts(t)
                dve.wait_ge(s_yn, t + 1)
                link(nc.vector.tensor_reduce(g[0], y, AX, ALU.add))
                link(nc.vector.tensor_scalar(g[1], g[0], 1.0 / HN, None, ALU.mult))
                link(nc.vector.tensor_tensor(y, y, per_head(g[1]), ALU.subtract))

            def group_variances(t):
                y, g, sq = norm_parts(t)
                link(nc.vector.tensor_tensor(sq, y, y, ALU.mult))
                link(nc.vector.tensor_reduce(g[0], sq, AX, ALU.add))
                nc.vector.tensor_scalar(g[0], g[0], 1.0 / HN, GN_EPS, ALU.mult, ALU.add).then_inc(s_gv, 1)

            def group_scale(t):
                y, g, _ = norm_parts(t)
                dve.wait_ge(s_gs, t + 1)
                link(nc.vector.reciprocal(g[1], g[1]))
                link(nc.vector.tensor_tensor(g[2], g[1], g[1], ALU.mult))
                link(nc.vector.tensor_tensor(g[2], g[2], g[0], ALU.mult))
                link(nc.vector.tensor_scalar(g[2], g[2], -0.5, 1.5, ALU.mult, ALU.add))
                link(nc.vector.tensor_tensor(g[1], g[1], g[2], ALU.mult))
                nc.vector.tensor_tensor(y, y, per_head(g[1]), ALU.mult).then_inc(s_gm, 1)

            norm_stages = (group_means, group_variances, group_scale)
            for u in range(UNITS):
                if u % 8 == 0:
                    if u:
                        dve.wait_ge(s_yTp, u)
                    nc.vector.memset(state, 0.0).then_inc(s_st, 1)
                    dve.wait_ge(s_st, 7 * (u // 8) + 1)
                f = u % 2
                for q in range(4):
                    a = 4 * u + q
                    dve.wait_ge(s_a1p, a + 1)
                    if a >= 8:
                        dve.wait_ge(s_yTp, u - 1)
                    heads = slice(HH * f + 4 * q, HH * f + 4 * q + 4)
                    nc.vector.tensor_tensor(aring[:, a % 8, :].rearrange("p (h n) -> p h n", h=4),
                                            PS[q][:, :].rearrange("p (h n) -> p h n", h=4), wmask[:, heads, :],
                                            ALU.mult).then_inc(s_a1, 1)
                if u >= 1 and (u - 1) % 8 < 6:
                    state_update(u - 1)
                for stage, norm in enumerate(norm_stages):
                    t, odd = divmod(u - 3 - stage, 2)
                    if t >= 0 and not odd:
                        norm(t)
            group_means(NT - 1)
            group_variances(NT - 2)
            group_variances(NT - 1)
            group_scale(NT - 2)
            group_scale(NT - 1)
            for t in range(NT):
                dve.wait_ge(s_op, t + 1)
                nc.vector.tensor_tensor(xs[:, t, :], PS[4 + t % 4][:, 0:D], xs[:, t, :], ALU.add).then_inc(s_o, 1)

        @block.tensor
        def _(pe):
            def product(o, pairs):
                for n, (w, m) in enumerate(pairs):
                    last = nc.tensor.matmul(o, w, m, start=(n == 0), stop=(n == len(pairs) - 1))
                return last

            def transposes(src, bank, done):
                for c in range(DC):
                    last = nc.tensor.transpose(bank[:, c * P:(c + 1) * P], src[:, c * P:(c + 1) * P], ident)
                last.then_inc(done, 1)

            def xn_transposes(base, tiles=range(NT)):
                for t in tiles:
                    pe.wait_ge(s_xn, base + t + 1)
                    if base + t >= 2:
                        pe.wait_ge(s_xnT, base + t - 1)
                    transposes(xn[:, t, 0:D], PS[t % 2], s_xnTp)

            def tok(t):
                return slice(t * P, (t + 1) * P)

            def half(b):
                return slice(b * S, (b + 1) * S)

            def qk_product(k, b, done):
                product(PS[(4, 2)[k] + b][:, :],
                        [(wqk[:, c, k * H0:(k + 1) * H0], xnT[:, c, half(b)]) for c in range(DC)]).then_inc(done, 1)

            pe.wait_ge(s_const, 16)
            for b in range(B):
                xn_transposes(0, range(b * TPB, (b + 1) * TPB))
                pe.wait_ge(s_wqkg, 32)
                pe.wait_ge(s_xnT, (b + 1) * TPB)
                qk_product(1, b, s_kp)
            for t in range(NT):
                last = product(PS[6][:, t * E:(t + 1) * E], [(xnT[:, c, tok(t)], wg[:, c, :]) for c in range(DC)])
            last.then_inc(s_lgp, 1)
            pe.wait_ge(s_wv, 16)
            for t in range(NT):
                if t >= 3:
                    pe.wait_ge(s_v, t - 2)
                product(PS[(0, 1, 7)[t % 3]][:, 0:D], [(xnT[:, c, tok(t)], wv[:, c, :]) for c in range(DC)])\
                    .then_inc(s_vp, 1)
            for b in range(B):
                qk_product(0, b, s_qp)
            pe.wait_ge(s_q32, B)
            pe.wait_ge(s_v, NT)
            for k in range(2):
                for t in range(4):
                    last = nc.tensor.transpose(PS[k][:, tok(t)], q32[:, 0, tok(4 * k + t)], ident)
                last.then_inc(s_qmp, 1)
            pe.wait_ge(s_skey, 1)
            for t in range(TPB):
                last = nc.tensor.transpose(PS[6][:, tok(t)], skey[:, B * t:B * (t + 1), :].rearrange("p b e -> p (b e)"),
                                           ident)
            last.then_inc(s_skTp, 1)

            def shared_up(i):
                rows, c0 = SROWS[i // B], P * (i // B)
                if i >= 3:
                    pe.wait_ge(s_sht, i - 2)
                for k in range(2):
                    last = product(PS[2 * (i % 3) + k][0:rows, :],
                                   [(wsh13[:, c, k * SHARED + c0:k * SHARED + c0 + rows], xnT[:, c, half(i % B)])
                                    for c in range(DC)])
                last.then_inc(s_shp, 1)

            pe.wait_ge(s_wsh, 48)
            pe.wait_ge(s_keys, B)
            pe.wait_ge(s_qm, 2)
            for i in range(NPAIR):
                shared_up(i)
            pe.wait_ge(s_slots, 1)
            pe.wait_ge(s_skT, 1)
            nc.tensor.transpose(PS[6][:, 0:P], slots, ident)
            pe.wait_ge(s_slotr, 1)
            nc.tensor.transpose(PS[6][:, P:2 * P], slotr, ident).then_inc(s_slotsTp, 1)
            pe.wait_ge(s_abs, 2)
            pe.wait_ge(s_fill, 4)
            nc.tensor.matmul(PS[7][:, 0:2], ones[:, :], tsum[:, 0:2], start=True, stop=True).then_inc(s_absp, 1)
            def tokens_T(u, gathered):
                pe.wait_ge(s_xe[u % SLOTS], gathered)
                transposes(xe[:, u % SLOTS, 0:D], PS[0], s_xeTp)

            def up(e, u, loaded):
                pe.wait_ge(s_wm[u % SLOTS], loaded)
                pe.wait_ge(s_xeT, e + 1)
                product(PS[1][:, 0:2 * INTER],
                        [(xeT[:, u % 2, c, :], w13r[u % SLOTS][:, c, :]) for c in range(DC)]).then_inc(s_hp, 1)

            def hidden_T(e, u):
                pe.wait_ge(s_hm, e + 1)
                for c in range(2):
                    last = nc.tensor.transpose(PS[2][0:IC, c * P:(c + 1) * P],
                                               hm[:, u % 2, c * IC:(c + 1) * IC], ident)
                last.then_inc(s_hTp, 1)

            def down(e, u):
                pe.wait_ge(s_hT, e + 1)
                product(PS[3][:, 0:D], [(heT[:, u % 2, c, :], w2r[u % SLOTS][:, c, :]) for c in range(2)])\
                    .then_inc(s_yp, 1)

            sk_v = sk.rearrange("p (g c) n -> p c g n", c=4)

            def logits(g, c, group):
                if c == 0:
                    pe.wait_ge(s_qxl, g * (16 * PARTS * PARTS) + 16 * PARTS * PARTS)
                if c >= 2:
                    pe.wait_ge(s_ex, g * 4 + (c - 1))
                nc.tensor.matmul(PS[4 + c % 2][:, :], sk_v[:, c, group, :].rearrange("p g n -> p (g n)"), qx[:, c, :],
                                 start=True, stop=True).then_inc(s_lp, 1)

            def weighted(g):
                pe.wait_ge(s_vpr, g + 1)
                pe.wait_ge(s_ex, g * 4 + 4)
                for c in range(4):
                    last = nc.tensor.matmul(PS[6][32 * c:32 * c + 32, :], vps[:, c, :], ex[:, c, :],
                                            start=True, stop=True, skip_group_check=True)
                last.then_inc(s_av, 1)

            def to_natural(g):
                pe.wait_ge(s_avT, g + 1)
                for t in range(TPB):
                    last = nc.tensor.transpose(PS[7][:, tok(t)], avT[:, tok(t)], ident)
                last.then_inc(s_natp, 1)

            def oT_transposes(t):
                if t == 0:
                    pe.wait_ge(s_nrm, 9 * NG)
                if t >= 2:
                    pe.wait_ge(s_oT, t - 1)
                transposes(onat[:, t, :], PS[6 + t % 2], s_oTp)

            def x1_product(t):
                pe.wait_ge(s_oT, t + 1)
                if t >= 2:
                    pe.wait_ge(s_x1, t - 1)
                product(PS[4 + t % 2][:, 0:D],
                        [(oT[:, c, tok(t)], wo0[:, c, :]) for c in range(DC)] +
                        [(hs[0:SROWS[c], c, tok(t)], wsh2[0:SROWS[c], c, :]) for c in range(3)]).then_inc(s_x1p, 1)

            def unit(g, u, group):
                e = g * SLOTS + u
                if g is not LAST or u + 1 < SLOTS:
                    tokens_T(u + 1, g * 16 + 16 * (1 + (u + 1) // SLOTS))
                if g is LAST:
                    for t in oT_at[u]:
                        oT_transposes(t)
                    if u == 2:
                        pe.wait_ge(s_wo0, 16)
                    for t in x1_at[u]:
                        x1_product(t)
                elif u < 2:
                    logits(g + 1, 2 * u, group)
                    logits(g + 1, 2 * u + 1, group)
                elif u == 2:
                    weighted(g + 1)
                else:
                    to_natural(g + 1)
                hidden_T(e, u)
                if g is not LAST or u + 1 < SLOTS:
                    up(g * SLOTS + (u + 1), u + 1, g * 32 + 32 * (1 + (u + 1) // SLOTS))
                pe.wait_ge(s_y, e + 1)
                down(e, u)

            pe.wait_ge(s_hs, 1)
            tokens_T(0, 16)
            up(0, 0, 32)
            pe.wait_ge(s_hs, 3)
            pe.wait_ge(s_skl, 16 * (2 * Q4 * B + PARTS - 1))
            for c in range(4):
                logits(0, c, slice(0, 1))
            weighted(0)
            pe.wait_ge(s_tsum, 1)
            to_natural(0)
            with pe.Fori(0, LAST) as g:
                for u in range(SLOTS):
                    unit(g, u, bass.ds(g + 1, 1))
            for u in range(SLOTS):
                unit(LAST, u, None)
            for t in range(4, NT):
                x1_product(t)

            for b in range(B):
                xn_transposes(NT, range(b * TPB, (b + 1) * TPB))
                pe.wait_ge(s_xnT, NT + (b + 1) * TPB)
                if b == 0:
                    pe.wait_ge(s_y, E + 1)
                    pe.wait_ge(s_x1, NT)
                    pe.wait_ge(s_tern, 4 * NG)
                for f in range(FC):
                    i = b * FC + f
                    if i >= 6:
                        pe.wait_ge(s_relu, i - 5)
                    product(PS[2 + i % 6][:, :],
                            [(w_fc1[:, c, f * P:(f + 1) * P], xnT[:, c, half(b)]) for c in range(DC)])\
                        .then_inc(s_ffp, 1)

            def mixed(k, c, cols):
                return mix[:, k % 2, c * N + cols.start:c * N + cols.stop]

            def project_T(k, w, bank_free, done):
                for i in range(4):
                    f, n = divmod(i, 2)
                    bank_free(i)
                    product(PS[i][:, :], [(w5[:, w, c, f * P:(f + 1) * P], mixed(k, c, half(n))) for c in range(DC)])\
                        .then_inc(done, 1)

            def project(k, w, bank, bank_free, done):
                for t in range(NT):
                    bank_free(t)
                    product(PS[bank + t % 4][:, 0:D], [(mixed(k, c, tok(t)), w5[:, w, c, :]) for c in range(DC)])\
                        .then_inc(done, 1)

            pe.wait_ge(s_w5, 16)
            pe.wait_ge(s_relu, 2 * FC)
            pe.wait_ge(s_mix, 1)
            project_T(0, 1, lambda i: None, s_kTp)
            pe.wait_ge(s_sq, 2 * FC)
            for t in range(NT):
                if t >= 4:
                    pe.wait_ge(s_x2, t - 3)
                product(PS[4 + t % 4][:, 0:D], [(hf[:, c, tok(t)], w_pj1[:, c, :]) for c in range(FC)]).then_inc(s_ffd, 1)
            pe.wait_ge(s_kf, 4)
            for t in range(NT):
                pe.wait_ge(s_x2, min(t + 5, NT))
                if t >= 4:
                    pe.wait_ge(s_kn, t - 3)
                for f in range(2):
                    last = nc.tensor.transpose(PS[4 + t % 4][:, f * P:(f + 1) * P], rw[:, f, tok(t)], ident)
                last.then_inc(s_knp, 1)
            pe.wait_ge(s_mix, 2)
            project_T(1, 0, lambda i: None, s_rTp)

            def v_bank(t):
                pe.wait_ge(s_kn, min(t + 5, NT))
                if t >= 4:
                    pe.wait_ge(s_v1, t - 3)

            pe.wait_ge(s_mix, 3)
            project(2, 2, 4, v_bank, s_v1p)

            def g_bank(t):
                if t < 4:
                    pe.wait_ge(s_rq, t + 1)
                    pe.wait_ge(s_rw, t + 1)
                else:
                    pe.wait_ge(s_g, t - 3)

            pe.wait_ge(s_mix, 4)
            project(3, 3, 0, g_bank, s_gp)

            def scores(u):
                t, f = divmod(u, 2)
                for q in range(4):
                    a = 4 * u + q
                    if a >= 4:
                        pe.wait_ge(s_a1, a - 3)
                    nc.tensor.matmul(PS[q][:, :], kq[:, f, q, tok(t)], rq[:, f, :, tok(t)], start=True, stop=True)\
                      .then_inc(s_a1p, 1)

            def outputs(u):
                t, f = divmod(u, 2)
                b, g = divmod(t, TPB)
                y = PS[4 + u % 2]
                if u >= 2:
                    pe.wait_ge(s_yT, u - 1)
                pe.wait_ge(s_st, 7 * b + max(1, 2 * g + f))
                nc.tensor.matmul(y[:, 0:P], state[:, f, :], rw[:, f, tok(t)], start=True, stop=False,
                                 skip_group_check=True)
                pe.wait_ge(s_a1, 4 * u + 4)
                pe.wait_ge(s_vd, t + 2)
                for h in range(4):
                    for q in range(4):
                        last = nc.tensor.matmul(y[32 * q:32 * q + 32, 0:P], vpr[:, t % 2, 4 * f + q, 32 * h:32 * h + 32],
                                                aring[:, (4 * u + q) % 8, h * P:(h + 1) * P], start=False,
                                                stop=(h == 3), skip_group_check=True)
                last.then_inc(s_yTp, 1)

            def state_product(u):
                t, f = divmod(u, 2)
                b, g = divmod(t, TPB)
                if g < TPB - 1:
                    n = 6 * b + 2 * g + f
                    if n:
                        pe.wait_ge(s_st, n + b + (1 if n % 6 else 0))
                    nc.tensor.matmul(PS[6][:, 0:P], kn[:, t, f * P:(f + 1) * P], vn[:, t, f * P:(f + 1) * P],
                                     start=True, stop=True).then_inc(s_kvp, 1)

            def y_natural(t):
                pe.wait_ge(s_yT, 2 * t + 2)
                if t >= 1:
                    pe.wait_ge(s_yn, t)
                for f in range(2):
                    last = nc.tensor.transpose(PS[7][:, f * P:(f + 1) * P], yTs[:, f, 0:P], ident)
                last.then_inc(s_ynp, 1)

            pe.wait_ge(s_g, NT)
            pe.wait_ge(s_v1, NT)
            scores(0)
            for u in range(UNITS):
                if u + 1 < UNITS:
                    scores(u + 1)
                outputs(u)
                state_product(u)
                if u >= 2 and u % 2 == 0:
                    y_natural(u // 2 - 1)
            y_natural(NT - 1)

            def z_transposes(t):
                pe.wait_ge(s_z, t + 1)
                if t == 0:
                    pe.wait_ge(s_a1, 4 * UNITS)
                if t >= 2:
                    pe.wait_ge(s_zT, t - 1)
                transposes(xn[:, t, 0:D], PS[t % 2], s_zTp)

            z_transposes(0)
            for t in range(NT):
                if t + 1 < NT:
                    z_transposes(t + 1)
                pe.wait_ge(s_zT, t + 1)
                if t == 0:
                    pe.wait_ge(s_yT, UNITS)
                    pe.wait_ge(s_st, 14)
                    pe.wait_ge(s_yn, NT)
                if t >= 4:
                    pe.wait_ge(s_o, t - 3)
                product(PS[4 + t % 4][:, 0:D], [(xnT[:, c, tok(t)], w5[:, 4, c, :]) for c in range(DC)]).then_inc(s_op, 1)


def kernel(**inputs):
    import concourse.bacc as bacc
    from concourse.bass_utils import run_bass_kernel_spmd

    a = {k: np.asarray(v) for k, v in inputs.items()}

    def chunks(w):
        c = w.shape[0] // P
        return np.ascontiguousarray(w.reshape(c, P, w.shape[1]).transpose(1, 0, 2))

    w1, w3 = a["L0_ffn_w1"], a["L0_ffn_w3"]
    w13 = np.concatenate([w1, w3], 1).transpose(0, 2, 1).reshape(E, DC, P, 2 * INTER).transpose(0, 2, 1, 3)
    w2 = a["L0_ffn_w2"].transpose(0, 2, 1).reshape(E, 2, IC, D).transpose(0, 2, 1, 3)
    maa = np.stack([a[f"L1_attn_time_maa_{k}"].reshape(DC, P) for k in "krvg"], 0)
    td = a["L1_attn_time_decay"].reshape(H1)
    arrays = {
        "x": a["L0_attn_x"],
        "consts": constants(),
        "w_qk": chunks(np.concatenate([a["L0_attn_Wq"], a["L0_attn_Wk"]], 0).T),
        "w_v": chunks(a["L0_attn_Wv"].T),
        "w_gate": chunks(a["L0_ffn_gate_w"].T),
        "w_sh13": chunks(np.concatenate([a["L0_ffn_sw1"], a["L0_ffn_sw3"]], 0).T),
        "w_sh2": a["L0_ffn_sw2"].T,
        "w_o0": chunks(a["L0_attn_Wo"].T),
        "w_13": w13,
        "w_2": w2,
        "maa": maa.transpose(2, 0, 1).reshape(P, 8),
        "td_row": td,
        "td_col": np.repeat(td, HN).reshape(2, P).T,
        "u_row": a["L1_attn_time_faaaa"].reshape(H1),
        "w_rkvgo": np.stack([chunks(a[f"L1_attn_W{k}"].T) for k in "rkvgo"], 1),
        "gamma": a["L1_attn_gamma"],
        "beta": a["L1_attn_beta"],
        "w_fc": chunks(a["L1_ffn_w_fc"].T),
        "w_pj": chunks(a["L1_ffn_w_proj"].T),
    }
    nc = bacc.Bacc("TRN2", target_bir_lowering=False, num_devices=1)
    arrays = {f"in_{k}": np.ascontiguousarray(v) for k, v in arrays.items()}
    args = [nc.dram_tensor(k, v.shape, mybir.dt.from_np(v.dtype), kind="ExternalInput").ap() for k, v in arrays.items()]
    out = nc.dram_tensor("out", (B, S, D), F32, kind="ExternalOutput").ap()
    block_kernel(nc, *args, out)
    r = run_bass_kernel_spmd(nc, [arrays], core_ids=[0])
    return r.results[0]["out"]
```
